# Optimizing a Trainium2 kernel written in Bass

```python
import numpy as np
import jax
import jax.numpy as jnp

def _softmax(x, axis=-1):
    return jax.nn.softmax(x, axis=axis)

def _gelu(x):
    return jax.nn.gelu(x, approximate=True)

def _silu(x):
    return jax.nn.silu(x)

def _sigmoid(x):
    return jax.nn.sigmoid(x)

def _layernorm(x, axis=-1, eps=1e-05):
    m = jnp.mean(x, axis=axis, keepdims=True)
    v = jnp.var(x, axis=axis, keepdims=True)
    return (x - m) / jnp.sqrt(v + eps)

def _scatter_add(tgt, idx, src, axis=0):
    return tgt.at[idx].add(src)

def _segment_sum(src, seg, n):
    return jax.ops.segment_sum(src, seg, n)
kernel_name = 'mk_early_fusion_d1_tok_img768_r4_55c2c6'

def setup_inputs(seed: int=0):
    np.random.seed(seed)
    _w = jnp.asarray

    def _rec_inputs():
        import jax
        import jax.numpy as jnp
        _rk = jax.random.key(seed)
        x = -0.000356955 + 1 * jax.random.normal(jax.random.fold_in(_rk, 1), (64, 3, 96, 96), jnp.float32)
        txt = -0.000573859 + 1.21648 * jax.random.normal(jax.random.fold_in(_rk, 2), (64, 32, 192), jnp.float32)
        return (x, txt)
    x, txt = _rec_inputs()

    def _L0_tok_setup():
        import jax, jax.numpy as jnp
        import numpy as np
        IMG = 224
        C = 3
        P = 16
        OV = 2
        WIN = P + 2 * OV
        STRIDE = (IMG - P - 2 * OV) // P + 1
        NG = (IMG - WIN) // STRIDE + 1
        NTOK = NG * NG
        TOK = C * WIN * WIN
        PROJ = 192
        B = 128

        def _get_tokens(imgs):
            starts = jnp.arange(NG) * STRIDE
            idx = starts[:, None] + jnp.arange(WIN)
            x = imgs[:, :, idx, :]
            x = x[:, :, :, :, idx]
            x = x.transpose(0, 1, 2, 4, 3, 5)
            return x.reshape(imgs.shape[0], NTOK, TOK)
        key = jax.random.key(seed)
        k1, k2, k3, k4 = jax.random.split(key, 4)
        return {'imgs': jax.random.normal(k1, (B, C, IMG, IMG), dtype=jnp.float32), 'proj_w': jax.random.normal(k2, (PROJ, TOK), dtype=jnp.float32) * 0.02, 'cls_token': jax.random.normal(k3, (1, 1, PROJ), dtype=jnp.float32), 'pos_embedding': jax.random.normal(k4, (NTOK + 1, PROJ), dtype=jnp.float32)}
    _L0_tok_all = _L0_tok_setup()
    _L0_tok_in = {k: v for k, v in _L0_tok_all.items() if k in ('proj_w', 'cls_token', 'pos_embedding')}
    del _L0_tok_all

    def _L0_attn_setup():
        import jax, jax.numpy as jnp
        import numpy as np
        B, T, C = (16, 512, 192)

        def _wkv(k, v, w, u):
            Bb, Tt, Cc = k.shape

            def step(carry, kv):
                num, den, mx = carry
                kt, vt = kv
                m_out = jnp.maximum(mx, kt + u)
                e1 = jnp.exp(mx - m_out)
                e2 = jnp.exp(kt + u - m_out)
                out = (e1 * num + e2 * vt) / (e1 * den + e2)
                m_new = jnp.maximum(mx + w, kt)
                e1s = jnp.exp(mx + w - m_new)
                e2s = jnp.exp(kt - m_new)
                return ((e1s * num + e2s * vt, e1s * den + e2s, m_new), out)
            init = (jnp.zeros((Bb, Cc), k.dtype), jnp.zeros((Bb, Cc), k.dtype), jnp.full((Bb, Cc), -1e+38, k.dtype))
            _, outs = jax.lax.scan(step, init, (jnp.swapaxes(k, 0, 1), jnp.swapaxes(v, 0, 1)))
            return jnp.swapaxes(outs, 0, 1)
        key = jax.random.key(seed)
        ks = jax.random.split(key, 10)
        s = 0.02
        return {'x': jax.random.normal(ks[0], (B, T, C), dtype=jnp.float32), 'time_decay': jax.random.normal(ks[1], (C,), dtype=jnp.float32) * 0.5, 'time_first': jax.random.normal(ks[2], (C,), dtype=jnp.float32) * 0.5, 'mix_k': jax.random.uniform(ks[3], (C,), dtype=jnp.float32), 'mix_v': jax.random.uniform(ks[4], (C,), dtype=jnp.float32), 'mix_r': jax.random.uniform(ks[5], (C,), dtype=jnp.float32), 'Wk': jax.random.normal(ks[6], (C, C), dtype=jnp.float32) * s, 'Wv': jax.random.normal(ks[7], (C, C), dtype=jnp.float32) * s, 'Wr': jax.random.normal(ks[8], (C, C), dtype=jnp.float32) * s, 'Wo': jax.random.normal(ks[9], (C, C), dtype=jnp.float32) * s}
    _L0_attn_all = _L0_attn_setup()
    _L0_attn_in = {k: v for k, v in _L0_attn_all.items() if k in ('time_decay', 'time_first', 'mix_k', 'mix_v', 'mix_r', 'Wk', 'Wv', 'Wr', 'Wo')}
    del _L0_attn_all

    def _L0_ffn_setup():
        import jax, jax.numpy as jnp
        import numpy as np
        DIM = 192
        HID = 128
        E = 16
        G = 8
        TOPK_G = 4
        TOPK_E = 4
        SCALE = 2.5
        B, S = (2, 512)
        key = jax.random.key(seed)
        ks = jax.random.split(key, 9)
        init = lambda k, shape: jax.random.normal(k, shape, dtype=jnp.float32) * 0.02
        z = lambda shape: jnp.zeros(shape, jnp.float32)
        return {'x': jax.random.normal(ks[0], (B, S, DIM), dtype=jnp.float32), 'gate_w': init(ks[1], (DIM, E)), 'gate_b': z((E,)), 'bias': z((E,)), 'Wu': init(ks[2], (E, DIM, HID)), 'bu': z((E, HID)), 'Wg': init(ks[3], (E, DIM, HID)), 'bg': z((E, HID)), 'Wd': init(ks[4], (E, HID, DIM)), 'bd': z((E, DIM)), 'sWu': init(ks[5], (DIM, HID)), 'sbu': z((HID,)), 'sWg': init(ks[6], (DIM, HID)), 'sbg': z((HID,)), 'sWd': init(ks[7], (HID, DIM)), 'sbd': z((DIM,))}
    _L0_ffn_all = _L0_ffn_setup()
    _L0_ffn_in = {k: v for k, v in _L0_ffn_all.items() if k in ('gate_w', 'gate_b', 'bias', 'Wu', 'bu', 'Wg', 'bg', 'Wd', 'bd', 'sWu', 'sbu', 'sWg', 'sbg', 'sWd', 'sbd')}
    del _L0_ffn_all
    return {'x': x, 'txt': txt, 'L0_tok_proj_w': _L0_tok_in['proj_w'], 'L0_tok_cls_token': _L0_tok_in['cls_token'], 'L0_tok_pos_embedding': _L0_tok_in['pos_embedding'], 'L0_attn_time_decay': _L0_attn_in['time_decay'], 'L0_attn_time_first': _L0_attn_in['time_first'], 'L0_attn_mix_k': _L0_attn_in['mix_k'], 'L0_attn_mix_v': _L0_attn_in['mix_v'], 'L0_attn_mix_r': _L0_attn_in['mix_r'], 'L0_attn_Wk': _L0_attn_in['Wk'], 'L0_attn_Wv': _L0_attn_in['Wv'], 'L0_attn_Wr': _L0_attn_in['Wr'], 'L0_attn_Wo': _L0_attn_in['Wo'], 'L0_ffn_gate_w': _L0_ffn_in['gate_w'], 'L0_ffn_gate_b': _L0_ffn_in['gate_b'], 'L0_ffn_bias': _L0_ffn_in['bias'], 'L0_ffn_Wu': _L0_ffn_in['Wu'], 'L0_ffn_bu': _L0_ffn_in['bu'], 'L0_ffn_Wg': _L0_ffn_in['Wg'], 'L0_ffn_bg': _L0_ffn_in['bg'], 'L0_ffn_Wd': _L0_ffn_in['Wd'], 'L0_ffn_bd': _L0_ffn_in['bd'], 'L0_ffn_sWu': _L0_ffn_in['sWu'], 'L0_ffn_sbu': _L0_ffn_in['sbu'], 'L0_ffn_sWg': _L0_ffn_in['sWg'], 'L0_ffn_sbg': _L0_ffn_in['sbg'], 'L0_ffn_sWd': _L0_ffn_in['sWd'], 'L0_ffn_sbd': _L0_ffn_in['sbd']}

def reference(x, txt, L0_tok_proj_w, L0_tok_cls_token, L0_tok_pos_embedding, L0_attn_time_decay, L0_attn_time_first, L0_attn_mix_k, L0_attn_mix_v, L0_attn_mix_r, L0_attn_Wk, L0_attn_Wv, L0_attn_Wr, L0_attn_Wo, L0_ffn_gate_w, L0_ffn_gate_b, L0_ffn_bias, L0_ffn_Wu, L0_ffn_bu, L0_ffn_Wg, L0_ffn_bg, L0_ffn_Wd, L0_ffn_bd, L0_ffn_sWu, L0_ffn_sbu, L0_ffn_sWg, L0_ffn_sbg, L0_ffn_sWd, L0_ffn_sbd):
    import jax
    import jax.numpy as jnp

    def _L0_tok_ref(imgs, proj_w, cls_token, pos_embedding):
        import jax, jax.numpy as jnp
        import numpy as np
        IMG = 224
        C = 3
        P = 16
        OV = 2
        WIN = P + 2 * OV
        STRIDE = (IMG - P - 2 * OV) // P + 1
        NG = (IMG - WIN) // STRIDE + 1
        NTOK = NG * NG
        TOK = C * WIN * WIN
        PROJ = 192
        B = 128

        def _get_tokens(imgs):
            starts = jnp.arange(NG) * STRIDE
            idx = starts[:, None] + jnp.arange(WIN)
            x = imgs[:, :, idx, :]
            x = x[:, :, :, :, idx]
            x = x.transpose(0, 1, 2, 4, 3, 5)
            return x.reshape(imgs.shape[0], NTOK, TOK)
        toks = _get_tokens(imgs)
        toks = jnp.einsum('btk,pk->btp', toks, proj_w)
        cls = jnp.broadcast_to(cls_token, (imgs.shape[0], 1, PROJ))
        tokens = jnp.concatenate([cls, toks], axis=1)
        return tokens + pos_embedding

    def _L0_attn_ref(x, time_decay, time_first, mix_k, mix_v, mix_r, Wk, Wv, Wr, Wo):
        import jax, jax.numpy as jnp
        import numpy as np
        B, T, C = (16, 512, 192)

        def _wkv(k, v, w, u):
            Bb, Tt, Cc = k.shape

            def step(carry, kv):
                num, den, mx = carry
                kt, vt = kv
                m_out = jnp.maximum(mx, kt + u)
                e1 = jnp.exp(mx - m_out)
                e2 = jnp.exp(kt + u - m_out)
                out = (e1 * num + e2 * vt) / (e1 * den + e2)
                m_new = jnp.maximum(mx + w, kt)
                e1s = jnp.exp(mx + w - m_new)
                e2s = jnp.exp(kt - m_new)
                return ((e1s * num + e2s * vt, e1s * den + e2s, m_new), out)
            init = (jnp.zeros((Bb, Cc), k.dtype), jnp.zeros((Bb, Cc), k.dtype), jnp.full((Bb, Cc), -1e+38, k.dtype))
            _, outs = jax.lax.scan(step, init, (jnp.swapaxes(k, 0, 1), jnp.swapaxes(v, 0, 1)))
            return jnp.swapaxes(outs, 0, 1)
        x_prev = jnp.pad(x, ((0, 0), (1, 0), (0, 0)))[:, :-1]
        k = jnp.einsum('btc,dc->btd', x * mix_k + x_prev * (1.0 - mix_k), Wk)
        v = jnp.einsum('btc,dc->btd', x * mix_v + x_prev * (1.0 - mix_v), Wv)
        r = jax.nn.sigmoid(jnp.einsum('btc,dc->btd', x * mix_r + x_prev * (1.0 - mix_r), Wr))
        w = -jnp.exp(time_decay)
        wkv = _wkv(k, v, w, time_first)
        return jnp.einsum('btc,dc->btd', r * wkv, Wo)

    def _L0_ffn_ref(x, gate_w, gate_b, bias, Wu, bu, Wg, bg, Wd, bd, sWu, sbu, sWg, sbg, sWd, sbd):
        import jax, jax.numpy as jnp
        import numpy as np
        DIM = 192
        HID = 128
        E = 16
        G = 8
        TOPK_G = 4
        TOPK_E = 4
        SCALE = 2.5
        B, S = (2, 512)
        orig_shape = x.shape
        xt = x.reshape(-1, DIM)
        T = xt.shape[0]
        scores = jax.nn.softmax(xt @ gate_w + gate_b, axis=-1)
        orig_scores = jax.lax.stop_gradient(scores)
        s = scores + bias[None, :]
        s3 = s.reshape(T, G, E // G)
        group_scores = jax.lax.top_k(s3, 2)[0].sum(-1)
        gidx = jax.lax.top_k(group_scores, TOPK_G)[1]
        gmask = jnp.any(jnp.arange(G)[None, None, :] == gidx[:, :, None], axis=1)
        s_masked = jnp.where(gmask[:, :, None], s3, -jnp.inf).reshape(T, E)
        _, idx = jax.lax.top_k(s_masked, TOPK_E)
        w = jnp.take_along_axis(orig_scores, idx, axis=1) * SCALE
        w_full = jnp.zeros((T, E), xt.dtype).at[jnp.arange(T)[:, None], idx].add(w)
        up = jax.nn.silu(jnp.einsum('td,edh->teh', xt, Wu) + bu)
        gt = jnp.einsum('td,edh->teh', xt, Wg) + bg
        act = up * gt * w_full[:, :, None]
        y = jnp.einsum('teh,ehd->td', act, Wd) + w_full @ bd
        sh = jax.nn.silu(xt @ sWu + sbu) * (xt @ sWg + sbg)
        y = y + sh @ sWd + sbd
        return y.reshape(orig_shape)
    h = _L0_tok_ref(x, L0_tok_proj_w, L0_tok_cls_token, L0_tok_pos_embedding)
    h = jnp.concatenate([h, txt], axis=1)
    h = h + _L0_attn_ref(_layernorm(h, axis=-1), L0_attn_time_decay, L0_attn_time_first, L0_attn_mix_k, L0_attn_mix_v, L0_attn_mix_r, L0_attn_Wk, L0_attn_Wv, L0_attn_Wr, L0_attn_Wo)
    h = h + _L0_ffn_ref(_layernorm(h, axis=-1), L0_ffn_gate_w, L0_ffn_gate_b, L0_ffn_bias, L0_ffn_Wu, L0_ffn_bu, L0_ffn_Wg, L0_ffn_bg, L0_ffn_Wd, L0_ffn_bd, L0_ffn_sWu, L0_ffn_sbu, L0_ffn_sWg, L0_ffn_sbg, L0_ffn_sWd, L0_ffn_sbd)
    return h

_drawn_inputs = setup_inputs


def setup_inputs(seed=0):
    import zlib

    import numpy as np

    out = dict(_drawn_inputs(seed))
    spreads = {'L0_ffn_gate_b': (0.0, 0.733),
     'L0_ffn_bias': (0.0, 0.1),
     'L0_ffn_bu': (0.0, 0.8),
     'L0_ffn_bg': (0.0, 0.8),
     'L0_ffn_bd': (0.0, 0.732),
     'L0_ffn_sbu': (0.0, 0.8),
     'L0_ffn_sbg': (0.0, 0.8),
     'L0_ffn_sbd': (0.0, 0.676)}
    factors = {'L0_attn_time_decay': 8.0,
     'L0_attn_time_first': 8.0,
     'L0_attn_mix_k': 8.0,
     'L0_attn_mix_v': 8.0,
     'L0_attn_mix_r': 8.0,
     'L0_attn_Wk': 8.0,
     'L0_attn_Wv': 3.072,
     'L0_attn_Wr': 8.0,
     'L0_attn_Wo': 3.122,
     'L0_ffn_gate_w': 3.636,
     'L0_ffn_Wu': 8.0,
     'L0_ffn_Wg': 8.0,
     'L0_ffn_Wd': 8.0,
     'L0_ffn_sWu': 7.465,
     'L0_ffn_sWg': 7.341,
     'L0_ffn_sWd': 6.946}
    for name, (base, spread) in spreads.items():
        noise = np.random.default_rng([zlib.crc32(name.encode()), seed]).standard_normal(out[name].shape)
        drawn = base * np.exp(spread * noise) if base else spread * noise
        out[name] = jnp.asarray(drawn.astype(out[name].dtype))
    for name, factor in factors.items():
        out[name] = (out[name] * factor).astype(out[name].dtype)
    return out
```

```python
from contextlib import ExitStack

import concourse.bass as bass
from concourse import mybir

F32 = mybir.dt.float32
F16 = mybir.dt.float16
ALU = mybir.AluOpType
ACT = mybir.ActivationFunctionType
AX_X = mybir.AxisListType.X

BATCH, CH, IMG = 64, 3, 96
D = 192
DA, DB = 128, 64
GRID, STRIDE, WIN = 16, 13, 20
TXT = 32
NPATCH = GRID * GRID
SEQ = 1 + NPATCH + TXT
PAIR = 2 * SEQ
PAIRS = BATCH // 2
EXP, HID = 16, 128
NX = EXP + 1
GROUPS, TOPK = 8, 4
SCALE = 2.5
EPS = 1e-5
TILES = [(t * 128, min(128, PAIR - t * 128)) for t in range(-(-PAIR // 128))]
NT = len(TILES)
PADT = NT * 128
TILE_GROUPS = [(0, 1), (2, 3), (4,)]
KC, KP = 10, 120
SLOTS = 2 * NX


def token_patches(t):
    last = -(-(IMG - 1) // STRIDE)
    return tuple((p // NPATCH, min(p % NPATCH // GRID, last), min(p % GRID, last)) for p in range(3 * t, 3 * t + 3))


DISTINCT = []
for _t in range(NPATCH):
    if token_patches(_t) not in DISTINCT:
        DISTINCT.append(token_patches(_t))
ND = len(DISTINCT)
WHICH = [DISTINCT.index(token_patches(t)) for t in range(NPATCH)]
PX = 2 * ND
YW = -(-PX // 3)
YT = [(k * YW, min(YW, PX - k * YW)) for k in range(3)]
XPIECES = 5
XPC = KC * PX // XPIECES


def selected():
    out = []
    for t0, rows in TILES:
        ks = set()
        for tok in range(t0, t0 + rows):
            b, t = divmod(tok, SEQ)
            if 1 <= t <= NPATCH:
                ks.add((b * ND + WHICH[t - 1]) // YW)
        out.append(sorted(ks))
    return out


SELECTED = selected()


def split_at_batch(t0, t1):
    out = []
    for b in range(2):
        lo, hi = max(t0, b * SEQ), min(t1, (b + 1) * SEQ)
        if lo < hi:
            out.append((lo, lo + b + 1, hi - lo))
    return out


TURNS = [[("A", 0, 512, 0)], [("A", 512, PAIR, 0), ("B", 0, 384, PAIR - 512)], [("B", 384, PAIR, 0)]]
SPLIT_ST = {0: (0, 1), 1: (2, 3), 2: (4,)}
PATCH_ST, EXPAND_ST, TURN1_ST, MIX_ST = (3, 4, 5), (6, 7, 8), (9, 10, 11), (12, 14, 16)
KVR_ST = {13: ("k0", "k1"), 14: ("k2",), 15: ("v0", "v1"), 16: ("v2",), 17: ("r0", "r1"), 18: ("r2",)}
Z_ST, EXP_ST, SCAN_ST, OSPLIT_ST = (15, 16, 17), 19, (20, 21, 22), 23
PROJ_ST, TURN2_ST, LOGIT_ST, WROW_ST = (24, 25, 26), (27, 28, 29), 30, 32


def norm_names(k, i):
    ts = TILE_GROUPS[i]
    return ([f"h{k}_{i}"] + [f"stats{k}_{t}" for t in ts] + [f"stats_set{k}_{i}"] + [f"aggr{k}_{t}" for t in ts] + [f"veps{k}_{i}"]
            + [f"{s}{k}_{t}" for t in ts for s in ("xn", "xd")])


def choose_names(c):
    return [c + s for s in ("thr", "gt", "eq", "cnt", "need", "cum", "le", "and", "sel")]


ROUTE = (["lg", "lmax", "lsh", "lsum", "lrec", "score", "biased", "gsum", "gsum_set"] + [f"gtop{t}" for t in range(NT)]
         + choose_names("g") + ["gbig", "masked", "masked2", "masked_set"] + [f"etop{t}" for t in range(NT)]
         + choose_names("e") + ["wfull", "w_hi", "w_lo"])
PE_ORDER, ACT_ORDER, DVE_ORDER, POOL_ORDER = [], [], [], []
for _s in range(SLOTS):
    if _s in SPLIT_ST:
        ACT_ORDER += [f"x_hi{i}" for i in SPLIT_ST[_s]]
        DVE_ORDER += [f"x_lo{i}" for i in SPLIT_ST[_s]]
    if _s in PATCH_ST:
        _i = PATCH_ST.index(_s)
        PE_ORDER.append(f"patch{_i}")
        ACT_ORDER.append(f"y_hi{_i}")
        DVE_ORDER.append(f"y_lo{_i}")
    for _k, _sts, _u in ((1, EXPAND_ST, "expand"), (2, PROJ_ST, "proj")):
        if _s in _sts:
            _i = _sts.index(_s)
            PE_ORDER.append(f"{_u}{_i}")
            DVE_ORDER += norm_names(_k, _i)
            POOL_ORDER.append(f"rstd{_k}_{_i}")
    if _s in TURN1_ST:
        _i = TURN1_ST.index(_s)
        PE_ORDER.append(f"turn1_{_i}")
        ACT_ORDER += [["xT_A0", "xT_A1"], ["xT_A2", "xT_B0", "xT_B1"], ["xT_B2"]][_i]
    if _s in MIX_ST:
        _q = "kvr"[MIX_ST.index(_s)]
        ACT_ORDER += [f"{_q}_hiA", f"{_q}_hiB"]
        DVE_ORDER += (["dA", "dB"] if _q == "k" else []) + [f"{_q}_{v}" for v in ("mA", "mB", "loA", "loB")]
    PE_ORDER += KVR_ST.get(_s, ())
    ACT_ORDER += KVR_ST.get(_s, ())
    if _s in Z_ST:
        DVE_ORDER += [f"{v}{Z_ST.index(_s)}" for v in ("m", "z", "zp", "zn", "qp", "qn")]
    if _s == EXP_ST:
        ACT_ORDER += [f"{e}{g}" for g in range(3) for e in ("e1s", "e2s", "e1", "e2", "er")]
    if _s in SCAN_ST:
        _g = SCAN_ST.index(_s)
        POOL_ORDER += [f"ev{_g}", f"t2{_g}"]
        DVE_ORDER += [f"{v}{_g}" for v in ("num", "den", "t1", "t3", "d1", "d2", "d3", "rec", "o")]
    if _s == OSPLIT_ST:
        ACT_ORDER += ["o_hiA", "o_hiB0", "o_hiB1"]
        DVE_ORDER += ["o_loA", "o_loB0", "o_loB1"]
    if _s in TURN2_ST:
        _i = TURN2_ST.index(_s)
        PE_ORDER.append(f"turn2_{_i}")
        ACT_ORDER += [["X_hA0"], ["X_hA1", "X_hB0"], ["X_hB1"]][_i]
        DVE_ORDER += [["X_lA0"], ["X_lA1", "X_lB0"], ["X_lB1"]][_i]
    if _s == LOGIT_ST:
        PE_ORDER.append("logits")
        ACT_ORDER.append("softmax")
        DVE_ORDER += ROUTE
    if _s == WROW_ST:
        PE_ORDER += ["wrow0", "wrow1", "wcol"]
        ACT_ORDER += ["wrow_c0", "wrow_c1", "wcol_c"]
READER = {f"patch{i}": ("dve", f"y_lo{i}") for i in range(3)}
READER.update({f"expand{i}": ("dve", f"h1_{i}") for i in range(3)})
READER.update({f"turn1_{i}": ("act", n) for i, n in enumerate(("xT_A1", "xT_B1", "xT_B2"))})
READER.update({f"{q}{g}": ("act", f"{q}{g}") for q in "kvr" for g in range(3)})
READER.update({f"proj{i}": ("dve", f"h2_{i}") for i in range(3)})
READER.update({f"turn2_{i}": ("dve", n) for i, n in enumerate(("X_lA0", "X_lB0", "X_lB1"))})
READER.update({"logits": ("dve", "lg"), "wrow0": ("act", "wrow_c0"), "wrow1": ("act", "wrow_c1"), "wcol": ("act", "wcol_c")})
SET_POOL = 24
WB = 2 * EXP
TXTS = [(b, lo, hi) for b in range(2) for t0, rows in TILES
        for lo, hi in [(max(t0, b * SEQ + 1 + NPATCH), min(t0 + rows, (b + 1) * SEQ))] if lo < hi]


def at(order, name, n):
    return n * len(order) + order.index(name) + 1


def build_fusion(nc, pixels, txt, pos, cls_token, patch_w, wkvr, wo, gate_w, wu, wg, wd, swu, swg, swd,
                 bd, sbd, gate_b, gate_bias, params, onehot, ident32, ident16, out):
    out_rows = out.rearrange("(n b) t c -> n (b t) c", b=2)
    with ExitStack() as ctx:
        def sb(name, shape, dt=F32):
            return ctx.enter_context(nc.sbuf_tensor(name, shape, dt))

        def sem(name):
            return ctx.enter_context(nc.semaphore(name))

        patch_hi, patch_lo = sb("patch_hi", [KP, KC, D], F16), sb("patch_lo", [KP, KC, D], F16)
        PW = 320
        kvr_w = {s: sb(f"kvr_{s}", [128, 3, PW], F16) for s in ("Ah", "Al", "Bh", "Bl")}
        wo_w = {s: sb(f"wo_{s}", [128, D], F16) for s in ("Ah", "Al", "Bh", "Bl")}
        gw_w = {s: sb(f"gw_{s}", [128, EXP], F16) for s in ("Ah", "Al", "Bh", "Bl")}
        up_w = {s: sb(f"up_{s}", [128, NX, HID], F16) for s in ("Ah", "Al", "Bh", "Bl")}
        gt_w = {s: sb(f"gt_{s}", [128, NX, HID], F16) for s in ("Ah", "Al", "Bh", "Bl")}
        dn_h, dn_l = sb("dn_h", [HID, NX, D], F16), sb("dn_l", [HID, NX, D], F16)
        bd_h, bd_l = sb("bd_h", [128, D], F16), sb("bd_l", [128, D], F16)
        par = sb("par", [128, 12 + 2 * NX])
        sel = sb("sel", [YW, 3, PAIR], F16)
        id32, id16 = sb("id32", [128, 128]), sb("id16", [128, 128], F16)
        gb_bc, bias_bc = sb("gb_bc", [128, EXP]), sb("bias_bc", [128, EXP])
        base = sb("base", [128, NT, D])
        decay = sb("decay", [128, 3])
        negw = sb("negw", [128, 3])
        wplusu = sb("wplusu", [128, 3])
        wfull = sb("wfull", [128, 3, SEQ])
        half = sb("half", [128, NT])
        reset_g, reset_e = sb("reset_g", [128, NT, GROUPS]), sb("reset_e", [128, NT, EXP])

        scan_buf, mix_buf = sb("scan_buf", [128, 4 * 3 * SEQ]), sb("mix_buf", [128, KC * PX])
        xraw = scan_buf[0:KP, 0:KC * PX]
        bd32 = sb("bd32", [128, D])
        x_hi, x_lo = (mix_buf[0:KP, i * KC * PX // 2:(i + 1) * KC * PX // 2].bitcast(F16).rearrange("p (c n) -> p c n", c=KC)
                      for i in range(2))
        y_hi, y_lo = sb("y_hi", [YW, 3, D], F16), sb("y_lo", [YW, 3, D], F16)
        h = [sb(f"h{p}", [128, NT, D]) for p in range(2)]
        stats, mv = sb("stats", [128, NT, 6]), sb("mv", [128, NT, 2])
        veps, rstd = sb("veps", [128, NT]), sb("rstd", [128, NT])
        xn = sb("xn", [128, NT, 256])
        xT = {s: sb(f"xT_{s}", [128, 2 * (SEQ + 1)]) for s in "AB"}
        dT, mix32 = ({s: mix_buf[:, j * KC * PX // 2 + i * PAIR:j * KC * PX // 2 + (i + 1) * PAIR] for i, s in enumerate("AB")}
                     for j in range(2))
        mixh = [sb(f"mixh{i}", [128, PAIR], F16) for i in range(2)]
        mixl = [sb(f"mixl{i}", [128, PAIR], F16) for i in range(2)]
        mixB = [sb(f"mixB{i}", [128, PAIR], F16) for i in range(2)]
        kvr = {q: sb(f"{q}32", [128, 3, SEQ]) for q in "kvr"}
        mrun, num, den = (sb(f"{s}run", [128, 3, SEQ + 1]) for s in ("m", "n", "d"))
        z = kvr["k"]
        zp, zn, qp, qn = (scan_buf[:, i * 3 * SEQ:(i + 1) * 3 * SEQ].rearrange("p (g t) -> p g t", g=3) for i in range(4))
        e1s, e2s, e1, e2 = zp, zn, qp, qn
        ev = sb("ev", [128, 3, SEQ])
        oh_A, ol_A = mixh[0], mixl[0]
        oh_B, ol_B = sb("oh_B", [128, PAIR], F16), sb("ol_B", [128, PAIR], F16)
        XAh, XAl, XB = ([sb(f"{s}{p}", [128, PADT], F16) for p in range(2)] for s in ("XAh", "XAl", "XB"))
        def r16(name, w=EXP):
            return sb(name, [128, NT, w])

        lg, ex, score, biased, masked = (r16(s) for s in ("lg", "ex", "score", "biased", "masked"))
        egt, eeq, ecum = (r16(s) for s in ("egt", "eeq", "ecum"))
        gsum, ggt, geq, gcum, gbig, gtop, etop = (r16(s, GROUPS) for s in ("gsum", "ggt", "geq", "gcum", "gbig", "gtop", "etop"))
        rs = {s: sb(s, [128, NT]) for s in ("lmax", "lsum", "lrec", "gthr", "gcnt", "gneed", "ethr", "ecnt", "eneed")}
        wfl = r16("wfl")
        settled = sb("settled", [1, 2])
        wcat = sb("wcat", [128, NT, 128], F16)
        wT = [sb(f"wT{p}", [128, PADT], F16) for p in range(2)]
        wrow16 = sb("wrow16", [EXP, PADT])
        wrow_buf = sb("wrow_buf", [128, EXP // 2 * PAIR])
        wrow = wrow_buf[0:1, :].rearrange("p (e t) -> p e t", e=EXP // 2)

        wb = [sb(f"wb{i}", [128, PAIR]) for i in range(2)]
        silu = [sb(f"silu{i}", [128, SEQ]) for i in range(2)]
        a32 = [sb(f"a32_{i}", [128, SEQ]) for i in range(4)]
        a_hi = [sb(f"a_hi{i}", [128, PAIR], F16) for i in range(2)]
        a_lo = [sb(f"a_lo{i}", [128, PAIR], F16) for i in range(2)]

        ups = ctx.enter_context(nc.psum_tensor("ups", [128, 2, 512], F32))
        gts = ctx.enter_context(nc.psum_tensor("gts", [128, 2, 512], F32))
        ysum = ctx.enter_context(nc.psum_tensor("ysum", [128, 3, 512], F32))
        ahead = ctx.enter_context(nc.psum_tensor("ahead", [128, 512], F32))
        ahead16 = ahead[:, :].bitcast(F16)

        consts_in = sem("consts_in")
        stage_in = [sem("stage_in0"), sem("stage_in1")]
        set_dve, set_act, set_pool = sem("set_dve"), sem("set_act"), sem("set_pool")
        base_in = sem("base_in")
        pixels_in, txt_in, wrow_in = sem("pixels_in"), sem("txt_in"), sem("wrow_in")
        pe_ahead, act_ahead, dve_ahead, pool_ahead = (sem(s) for s in ("pe_ahead", "act_ahead", "dve_ahead", "pool_ahead"))
        up_ready, gate_ready = sem("up_ready"), sem("gate_ready")
        silu_done, gated, weighted, hi_done, lo_done = (sem(s) for s in ("silu_done", "gated", "weighted", "hi_done", "lo_done"))
        wb_done, down_done, fin_done, out_done = (sem(s) for s in ("wb_done", "down_done", "fin_done", "out_done"))

        def rows3(ap):
            return ap.rearrange("e k h -> k e h")

        SW = NX * D
        stage = [wrow_buf[:, 0:SW], scan_buf[:, 0:SW]]
        jobs = []

        def job(hi, lo, parts, p, shape):
            jobs.append((hi, lo, parts, p, shape))

        for s in range(2):
            ks = slice(0, DA) if s == 0 else slice(DA, D)
            for name, dst, routed, shared in (("up", up_w, wu, swu), ("gt", gt_w, wg, swg)):
                hi, lo = (dst["Ah"], dst["Al"]) if s == 0 else (dst["Bh"], dst["Bl"])
                parts = []
                for r in range(1 + s):
                    ps = slice(0, DA) if s == 0 else slice(r * DB, (r + 1) * DB)
                    parts.append((ps, slice(1, NX), rows3(routed)[ks]))
                    parts.append((ps, slice(0, 1), shared[ks].unsqueeze(1)))
                job(hi[:, :, :], lo[:, :, :], parts, 128, (NX, HID))
        job(dn_h[:, :, :], dn_l[:, :, :], [(slice(0, HID), slice(1, NX), rows3(wd)),
                                           (slice(0, HID), slice(0, 1), swd.unsqueeze(1))], 128, (NX, D))
        job(patch_hi[:, :, :], patch_lo[:, :, :], [(slice(0, KP), slice(0, KC), patch_w)], KP, (KC, D))
        for s in range(2):
            ks = slice(0, DA) if s == 0 else slice(DA, D)
            c = "AB"[s]
            places = [slice(0, DA)] if s == 0 else [slice(0, DB), slice(DB, 2 * DB)]
            for o0, o1, w0 in ((0, DA, 0), (DA, D, DA + DB)):
                job(kvr_w[c + "h"][:, :, w0:w0 + o1 - o0], kvr_w[c + "l"][:, :, w0:w0 + o1 - o0],
                    [(ps, slice(0, 3), wkvr[ks, :, o0:o1]) for ps in places], 128, (3, o1 - o0))
            job(wo_w[c + "h"][:, :].unsqueeze(1), wo_w[c + "l"][:, :].unsqueeze(1),
                [(ps, slice(0, 1), wo[ks].unsqueeze(1)) for ps in places], 128, (1, D))
            job(gw_w[c + "h"][:, :].unsqueeze(1), gw_w[c + "l"][:, :].unsqueeze(1),
                [(ps, slice(0, 1), gate_w[ks].unsqueeze(1)) for ps in places], 128, (1, EXP))
        JOBS = len(jobs)
        staged = [0, 0]
        need = []
        for j, (_, _, parts, _, _) in enumerate(jobs):
            staged[j % 2] += 16 * len(parts)
            need.append(staged[j % 2])

        def view(j):
            rows, cols = jobs[j][4]
            return stage[j % 2][0:jobs[j][3], 0:rows * cols].rearrange("p (a b) -> p a b", a=rows)

        SET_DVE = (["z_settled", "z_base", "z_bd", "z_cls", "z_kh", "z_kl", "z_BH", "z_BL"] + [f"hi{j}" if s == 0 else f"lo{j}" for j in range(JOBS) for s in range(2)]
                   + ["bdhi", "bdlo", "cls0", "cls2", "negw", "wplusu", "onesq", "wfull0", "wfull1", "wfull2"])
        BASE_DMAS = 5 + sum(max(t0, b * SEQ) < min(t0 + rows, b * SEQ + 1 + NPATCH) for b in range(2) for t0, rows in TILES)
        PD, PU, PM, PBU, PBG = 0, 3, 6, 12, 12 + NX
        clsT = xn[:, :, 0:D]

        def q_at(name):
            return SET_DVE.index(name) + 1

        block = ctx.enter_context(nc.Block())

        @block.sync
        def _(sp):
            nconst = 0
            for dst, src in ((par[:, :], params), (sel[:, :, :], onehot), (id32[:, :], ident32), (id16[:, :], ident16),
                             (gb_bc[:, :], gate_b.partition_broadcast(128)), (bias_bc[:, :], gate_bias.partition_broadcast(128))):
                sp.dma_start(dst, src).then_inc(consts_in, 16)
                nconst += 1
            sp.wait_ge(set_dve, q_at("z_cls"))
            nb = 0
            for b in range(2):
                for t, (t0, rows) in enumerate(TILES):
                    lo, hi = max(t0, b * SEQ), min(t0 + rows, b * SEQ + 1 + NPATCH)
                    if lo < hi:
                        sp.dma_start(base[lo - t0:hi - t0, t, :], pos[lo - b * SEQ:hi - b * SEQ]).then_inc(base_in, 16)
                        nb += 1
            for b in range(2):
                sp.dma_start(clsT[b * SEQ % 128:b * SEQ % 128 + 1, b * SEQ // 128, :], cls_token).then_inc(base_in, 16)
            for p0 in (0, 32):
                sp.dma_start(bd32[p0:p0 + EXP, :], bd).then_inc(base_in, 16)
            sp.dma_start(bd32[96:97, :], sbd).then_inc(base_in, 16)
            assert nb + 5 == BASE_DMAS
            for j, (_, _, parts, _, _) in enumerate(jobs):
                if j >= 2:
                    sp.wait_ge(set_dve, q_at(f"lo{j - 2}"))
                for ps, rs_, src in parts:
                    sp.dma_start(view(j)[ps, rs_, :], src).then_inc(stage_in[j % 2], 16)

            def ahead_loads(n):
                m = n if type(n) is int else sp.snap(n)
                if type(n) is not int or n > 0:
                    sp.wait_ge(dve_ahead, at(DVE_ORDER, "o2", n - 1))
                sp.dma_start(xraw[:, :], pixels[m]).then_inc(pixels_in, 16)
                if type(n) is not int or n > 0:
                    sp.wait_ge(dve_ahead, at(DVE_ORDER, "h1_2", n - 1))
                for b, lo, hi in TXTS:
                    t, r = divmod(lo, 128)
                    t_lo = lo - b * SEQ - 1 - NPATCH
                    sp.dma_start(base[r:r + hi - lo, t, :], txt[m, b, t_lo:t_lo + hi - lo, :]).then_inc(txt_in, 16)

            def wrow_load(n, second):
                if second:
                    sp.wait_ge(wb_done, EXP * n + EXP // 2)
                else:
                    sp.wait_ge(act_ahead, at(ACT_ORDER, "wrow_c1", n))
                e0 = EXP // 2 * second
                sp.dma_start(wrow[:, :, :], wrow16[e0:e0 + EXP // 2, 0:PAIR]).then_inc(wrow_in, 16)

            def store(n, pp):
                m = n if type(n) is int else sp.snap(n)
                sp.wait_ge(fin_done, 3 * n + 3)
                for t, (t0, rows) in enumerate(TILES):
                    sp.dma_start(out_rows[m, t0:t0 + rows, :], h[pp][0:rows, t, :]).then_inc(out_done, 16)

            def body(n, pp):
                if type(n) is not int or n > 0:
                    store(n - 1, (pp + 1) % 2)
                wrow_load(n, 1)
                if type(n) is not int or n + 2 < PAIRS:
                    ahead_loads(n + 2)
                if type(n) is not int or n + 1 < PAIRS:
                    wrow_load(n + 1, 0)

            sp.wait_ge(set_dve, q_at("cls2"))
            ahead_loads(0)
            ahead_loads(1)
            wrow_load(0, 0)
            body(0, 0)
            with sp.Fori(0, PAIRS // 2 - 2) as i:
                for p in range(2):
                    body(2 * i + 1 + p, (1 + p) % 2)
            for n in range(PAIRS - 3, PAIRS):
                body(n, n % 2)
            store(PAIRS - 1, 1)
            sp.wait_ge(out_done, 16 * NT * PAIRS)

        @block.gpsimd
        def _(pool):
            fills = [(half[:, :], -0.5), (wcat[:, :, :], 0.0), (wcat[:, :, 96:97], 1.0), (mrun[:, :, 0:1], -1e38),
                     (num[:, :, 0:1], 0.0), (den[:, :, 0:1], 0.0)]
            fills += [(m[:, :, 1:w], 1.0) for m, w in ((reset_g, GROUPS), (reset_e, EXP))]
            fills += [(m[:, :, 0:1], 0.0) for m in (reset_g, reset_e)]
            fills += [(xT[s][:, b * (SEQ + 1):b * (SEQ + 1) + 1], 0.0) for s in "AB" for b in range(2)]
            fills += [(m[p][:, PAIR:PADT], 0.0) for m in (XAh, XAl, XB) for p in range(2)]
            fills += [(m[ps, cs], 0.0) for m in (oh_B, ol_B) for ps, cs in ((slice(0, DB), slice(SEQ, PAIR)),
                                                                        (slice(DB, 128), slice(0, SEQ)))]
            assert len(fills) == SET_POOL
            for k, (ap, value) in enumerate(fills):
                if k:
                    pool.wait_ge(set_pool, k)
                pool.memset(ap, value).then_inc(set_pool, 1)
            pool.wait_ge(set_pool, SET_POOL)

            def rstd_(k, i, n):
                ts = TILE_GROUPS[i]
                rows = TILES[ts[-1]][1]
                c = slice(ts[0], ts[-1] + 1)
                pool.wait_ge(dve_ahead, at(DVE_ORDER, f"veps{k}_{i}", n))
                pool.tensor_tensor(rstd[0:rows, c], veps[0:rows, c], half[0:rows, c], ALU.pow).then_inc(pool_ahead, 1)

            def ahead_step(st, n, p):
                if st in EXPAND_ST:
                    rstd_(1, EXPAND_ST.index(st), n)
                if st in SCAN_ST:
                    g = SCAN_ST.index(st)
                    pool.wait_ge(act_ahead, at(ACT_ORDER, f"er{g}", n))
                    pool.tensor_tensor(ev[:, g, :], e2s[:, g, :], kvr["v"][:, g, :], ALU.mult).then_inc(pool_ahead, 1)
                    pool.tensor_tensor(z[:, g, :], e2[:, g, :], kvr["v"][:, g, :], ALU.mult).then_inc(pool_ahead, 1)
                if st in PROJ_ST:
                    rstd_(2, PROJ_ST.index(st), n)

            def low_part(n, s, pp):
                S = 34 * n + s
                e, b = divmod(s, 2)
                pool.wait_ge(hi_done, S + 1)
                pool.tensor_tensor(a_lo[(pp + e) % 2][:, b * SEQ:(b + 1) * SEQ], a32[(34 * pp + s) % 4][:, :],
                                   a_hi[(pp + e) % 2][:, b * SEQ:(b + 1) * SEQ], ALU.subtract).then_inc(lo_done, 1)

            def body(n, pp, first=False, last=False):
                for s in range(SLOTS):
                    e, b = divmod(s, 2)
                    if e > 0:
                        pool.wait_ge(wb_done, EXP * n + e)
                        pool.wait_ge(gated, 34 * n + s + 1)
                        pool.tensor_tensor(a32[(34 * pp + s) % 4][:, :], a32[(34 * pp + s) % 4][:, :],
                                           wb[e % 2][:, b * SEQ:(b + 1) * SEQ], ALU.mult).then_inc(weighted, 1)
                    broadcast = b == 1 and e < EXP
                    if broadcast:
                        if e in (0, EXP // 2):
                            pool.wait_ge(wrow_in, 32 * n + (16 if e == 0 else 32))
                        if e >= 2 or not first:
                            pool.wait_ge(weighted, WB * n + 2 * (e - 1))
                    if s > 0:
                        low_part(n, s - 1, pp)
                    if broadcast:
                        pool.partition_broadcast(wb[(e + 1) % 2][:, :], wrow[0:1, e % (EXP // 2), :], 128).then_inc(wb_done, 1)
                    if not last:
                        ahead_step(s, n + 1, (pp + 1) % 2)
                low_part(n, SLOTS - 1, pp)

            for st in range(SLOTS):
                ahead_step(st, 0, 0)
            body(0, 0, first=True)
            with pool.Fori(0, PAIRS // 2 - 1) as i:
                for p in range(2):
                    body(2 * i + 1 + p, (1 + p) % 2)
            body(PAIRS - 1, 1, last=True)

        @block.scalar
        def _(act):
            act.wait_ge(consts_in, 16 * 6)
            act.activation(decay[:, :], par[:, PD:PD + 3], ACT.Exp).then_inc(set_act, 1)
            act.wait_ge(set_pool, SET_POOL)

            def ahead_step(st, n, p):
                later = type(n) is not int or n > 0
                if st in SPLIT_ST:
                    for i in SPLIT_ST[st]:
                        if i == 0:
                            act.wait_ge(pixels_in, 16 * n + 16)
                            if later:
                                act.wait_ge(pe_ahead, at(PE_ORDER, "patch2", n - 1))
                        c = slice(i * XPC, (i + 1) * XPC)
                        act.activation(x_hi[:, :, :].rearrange("p a b -> p (a b)")[:, c], xraw[:, c], ACT.Copy)\
                           .then_inc(act_ahead, 1)
                if st in PATCH_ST:
                    i = PATCH_ST.index(st)
                    act.wait_ge(pe_ahead, at(PE_ORDER, f"patch{i}", n))
                    act.activation(y_hi[0:YT[i][1], i, :], ahead[0:YT[i][1], 0:D], ACT.Copy).then_inc(act_ahead, 1)
                if st in TURN1_ST:
                    i = TURN1_ST.index(st)
                    act.wait_ge(pe_ahead, at(PE_ORDER, f"turn1_{i}", n))
                    if later:
                        act.wait_ge(dve_ahead, at(DVE_ORDER, "r_mB", n - 1))
                    for s, lo, hi, col in TURNS[i]:
                        for tok, c, ln in split_at_batch(lo, hi):
                            act.activation(xT[s][:, c:c + ln], ahead[:, col + tok - lo:col + tok - lo + ln], ACT.Copy)\
                               .then_inc(act_ahead, 1)
                if st in MIX_ST:
                    qi = MIX_ST.index(st)
                    q = "kvr"[qi]
                    for s, dst in (("A", mixh[qi % 2]), ("B", mixB[qi % 2])):
                        act.wait_ge(dve_ahead, at(DVE_ORDER, f"{q}_m{s}", n))
                        if s == "A" and (qi == 2 or later):
                            act.wait_ge(pe_ahead, at(PE_ORDER, {0: "r2", 1: "v2", 2: "k2"}[qi], n if qi == 2 else n - 1))
                        act.activation(dst[:, :], mix32[s][:, :], ACT.Copy).then_inc(act_ahead, 1)
                for name in KVR_ST.get(st, ()):
                    q, g = name[0], int(name[1])
                    act.wait_ge(pe_ahead, at(PE_ORDER, name, n))
                    if later and g == 0:
                        act.wait_ge(dve_ahead, at(DVE_ORDER, "o2", n - 1))
                    act.activation(kvr[q][:, g, :], ahead[:, 0:SEQ], ACT.Copy).then_inc(act_ahead, 1)
                if st == EXP_ST:
                    for g in range(3):
                        act.wait_ge(dve_ahead, at(DVE_ORDER, f"qn{g}", n))
                        act.activation(e1s[:, g, :], zp[:, g, :], ACT.Exp, scale=-1.0).then_inc(act_ahead, 1)
                        act.activation(e2s[:, g, :], zn[:, g, :], ACT.Exp).then_inc(act_ahead, 1)
                        act.activation(e1[:, g, :], qp[:, g, :], ACT.Exp, scale=-1.0).then_inc(act_ahead, 1)
                        act.activation(e2[:, g, :], qn[:, g, :], ACT.Exp).then_inc(act_ahead, 1)
                        act.wait_ge(act_ahead, at(ACT_ORDER, "r2", n))
                        act.activation(kvr["r"][:, g, :], kvr["r"][:, g, :], ACT.Exp, scale=-1.0).then_inc(act_ahead, 1)
                if st == OSPLIT_ST:
                    act.wait_ge(dve_ahead, at(DVE_ORDER, "o2", n))
                    if later:
                        act.wait_ge(pe_ahead, at(PE_ORDER, "proj2", n - 1))
                    act.activation(oh_A[:, :].rearrange("p (b t) -> p b t", b=2), ev[:, 0:2, :], ACT.Copy).then_inc(act_ahead, 1)
                    for b in range(2):
                        ps, cs = slice(b * DB, (b + 1) * DB), slice(b * SEQ, (b + 1) * SEQ)
                        act.activation(oh_B[ps, cs], ev[ps, 2, :], ACT.Copy).then_inc(act_ahead, 1)
                if st in TURN2_ST:
                    i = TURN2_ST.index(st)
                    act.wait_ge(pe_ahead, at(PE_ORDER, f"turn2_{i}", n))
                    for s, lo, hi, col in TURNS[i]:
                        dst = XAh[p] if s == "A" else XB[p]
                        act.activation(dst[:, lo:hi], ahead[:, col:col + hi - lo], ACT.Copy).then_inc(act_ahead, 1)
                if st == LOGIT_ST:
                    act.wait_ge(dve_ahead, at(DVE_ORDER, "lsh", n))
                    act.activation(ex[:, :, :], lg[:, :, :], ACT.Exp).then_inc(act_ahead, 1)
                if st == WROW_ST:
                    for i, (c0, c1) in enumerate(((0, 512), (512, PADT))):
                        act.wait_ge(pe_ahead, at(PE_ORDER, f"wrow{i}", n))
                        if later:
                            act.wait_ge(wb_done, EXP * n)
                        act.activation(wrow16[:, c0:c1], ahead[0:EXP, 0:c1 - c0], ACT.Copy).then_inc(act_ahead, 1)
                    act.wait_ge(pe_ahead, at(PE_ORDER, "wcol", n))
                    act.activation(wT[p][:, :], ahead16[:, 0:PADT], ACT.Copy).then_inc(act_ahead, 1)

            def high_part(n, s, pp):
                S = 34 * n + s
                e, b = divmod(s, 2)
                if e > 0:
                    act.wait_ge(weighted, WB * n + s - 1)
                else:
                    act.wait_ge(gated, S + 1)
                if b == 0:
                    if e >= 2:
                        act.wait_ge(down_done, NX * n + e - 1)
                    elif type(n) is not int or n > 0:
                        act.wait_ge(down_done, NX * n + e - 1)
                act.activation(a_hi[(pp + e) % 2][:, b * SEQ:(b + 1) * SEQ], a32[(34 * pp + s) % 4][:, :], ACT.Copy)\
                   .then_inc(hi_done, 1)

            def body(n, pp, last=False):
                for s in range(SLOTS):
                    S = 34 * n + s
                    e = s // 2
                    act.wait_ge(up_ready, S + 1)
                    if s >= 2 or type(n) is not int or n > 0:
                        act.wait_ge(gated, S - 1)
                    act.activation(silu[s % 2][:, :], ups[:, s % 2, 0:SEQ], ACT.Silu, bias=par[:, PBU + e:PBU + e + 1])\
                       .then_inc(silu_done, 1)
                    if s > 0:
                        high_part(n, s - 1, pp)
                    if not last:
                        ahead_step(s, n + 1, (pp + 1) % 2)
                high_part(n, SLOTS - 1, pp)

            for st in range(SLOTS):
                ahead_step(st, 0, 0)
            body(0, 0)
            with act.Fori(0, PAIRS // 2 - 1) as i:
                for p in range(2):
                    body(2 * i + 1 + p, (1 + p) % 2)
            body(PAIRS - 1, 1, last=True)

        @block.vector
        def _(dve):
            dve.memset(settled[:, :], 0.0).then_inc(set_dve, 1)
            dve.memset(base[:, :, :], 0.0).then_inc(set_dve, 1)
            dve.memset(bd32[:, :], 0.0).then_inc(set_dve, 1)
            dve.memset(clsT[:, :, :], 0.0).then_inc(set_dve, 1)
            for c in ("Ah", "Al", "Bh", "Bl"):
                dve.memset(kvr_w[c][:, :, :], 0.0).then_inc(set_dve, 1)
            for j, (hi, lo, parts, rows, shape) in enumerate(jobs):
                dve.wait_ge(stage_in[j % 2], need[j])
                if j == 0:
                    dve.wait_ge(set_dve, q_at("z_BL"))
                dve.tensor_copy(hi, view(j)).then_inc(set_dve, 1)
                dve.wait_ge(set_dve, q_at(f"hi{j}"))
                dve.tensor_tensor(lo, view(j), hi, ALU.subtract).then_inc(set_dve, 1)
            dve.wait_ge(base_in, 16 * BASE_DMAS)
            dve.tensor_copy(bd_h[:, :], bd32[:, :]).then_inc(set_dve, 1)
            dve.wait_ge(set_dve, q_at("bdhi"))
            dve.tensor_tensor(bd_l[:, :], bd32[:, :], bd_h[:, :], ALU.subtract).then_inc(set_dve, 1)
            for t in (0, SEQ // 128):
                dve.tensor_tensor(base[:, t, :], base[:, t, :], clsT[:, t, :], ALU.add).then_inc(set_dve, 1)
            dve.wait_ge(set_act, 1)
            dve.tensor_scalar(negw[:, :], decay[:, :], -1.0, None, ALU.mult).then_inc(set_dve, 1)
            dve.wait_ge(set_dve, q_at("negw"))
            dve.tensor_tensor(wplusu[:, :], negw[:, :], par[:, PU:PU + 3], ALU.add).then_inc(set_dve, 1)
            dve.memset(wfull[:, :, :], 1.0).then_inc(set_dve, 1)
            dve.wait_ge(set_dve, q_at("onesq"))
            for g in range(3):
                dve.tensor_scalar(wfull[:, g, :], wfull[:, g, :], negw[:, g:g + 1], None, ALU.mult).then_inc(set_dve, 1)
            dve.wait_ge(set_dve, len(SET_DVE))
            dve.wait_ge(set_pool, SET_POOL)

            def after(name, n):
                dve.wait_ge(dve_ahead, at(DVE_ORDER, name, n))

            def settle(before, name, n):
                after(before, n)
                dve.tensor_copy(settled[0:1, 0:1], settled[0:1, 1:2]).then_inc(dve_ahead, 1)

            def layernorm(k, i, n, p):
                ts = TILE_GROUPS[i]
                rows = TILES[ts[-1]][1]
                c = slice(ts[0], ts[-1] + 1)
                hp = h[p]
                after(f"h{k}_{i}", n)
                for t in ts:
                    dve.bn_stats(stats[0:rows, t, :], hp[0:rows, t, :]).then_inc(dve_ahead, 1)
                settle(f"stats{k}_{ts[-1]}", f"stats_set{k}_{i}", n)
                for t in ts:
                    dve.bn_aggr(mv[0:rows, t, :], stats[0:rows, t, :]).then_inc(dve_ahead, 1)
                after(f"aggr{k}_{ts[-1]}", n)
                dve.tensor_scalar(veps[0:rows, c], mv[0:rows, c, 1], EPS, None, ALU.add).then_inc(dve_ahead, 1)
                dve.wait_ge(pool_ahead, at(POOL_ORDER, f"rstd{k}_{i}", n))
                for t in ts:
                    for dst, src in ((slice(0, D), slice(0, D)), (slice(D, 256), slice(DA, D))):
                        dve.tensor_scalar(xn[0:rows, t, dst], hp[0:rows, t, src], mv[0:rows, t, 0:1], rstd[0:rows, t:t + 1],
                                          ALU.subtract, ALU.mult).then_inc(dve_ahead, 1)

            def select4(x, thr, top, gt, eq, cnt, need_, cum, reset, w, names, n):
                bc = [128, NT, w]
                dve.tensor_copy(rs[thr][:, :], top[:, :, TOPK - 1]).then_inc(dve_ahead, 1)
                after(names + "thr", n)
                tb = rs[thr][:, :].unsqueeze(2).to_broadcast(bc)
                dve.tensor_tensor(gt[:, :, :], x[:, :, :], tb, ALU.is_gt).then_inc(dve_ahead, 1)
                dve.tensor_tensor(eq[:, :, :], x[:, :, :], tb, ALU.is_equal).then_inc(dve_ahead, 1)
                after(names + "gt", n)
                dve.tensor_reduce(rs[cnt][:, :], gt[:, :, :], AX_X, ALU.add).then_inc(dve_ahead, 1)
                after(names + "cnt", n)
                dve.tensor_scalar(rs[need_][:, :], rs[cnt][:, :], -1.0, float(TOPK), ALU.mult, ALU.add).then_inc(dve_ahead, 1)
                dve.tensor_tensor_scan(cum[:, :, :].rearrange("p a b -> p (a b)"), reset[:, :, :].rearrange("p a b -> p (a b)"),
                                       eq[:, :, :].rearrange("p a b -> p (a b)"), 0.0, ALU.mult, ALU.add).then_inc(dve_ahead, 1)
                after(names + "cum", n)
                dve.tensor_tensor(cum[:, :, :], cum[:, :, :], rs[need_][:, :].unsqueeze(2).to_broadcast(bc), ALU.is_le)\
                   .then_inc(dve_ahead, 1)
                after(names + "le", n)
                dve.tensor_tensor(eq[:, :, :], cum[:, :, :], eq[:, :, :], ALU.mult).then_inc(dve_ahead, 1)
                after(names + "and", n)
                dve.tensor_tensor(gt[:, :, :], gt[:, :, :], eq[:, :, :], ALU.add).then_inc(dve_ahead, 1)
                after(names + "sel", n)

            def ahead_step(st, n, p):
                later = type(n) is not int or n > 0
                if st in SPLIT_ST:
                    for i in SPLIT_ST[st]:
                        c = slice(i * XPC, (i + 1) * XPC)
                        dve.wait_ge(act_ahead, at(ACT_ORDER, f"x_hi{i}", n))
                        dve.tensor_tensor(x_lo[:, :, :].rearrange("p a b -> p (a b)")[:, c], xraw[:, c],
                                          x_hi[:, :, :].rearrange("p a b -> p (a b)")[:, c], ALU.subtract).then_inc(dve_ahead, 1)
                if st in PATCH_ST:
                    i = PATCH_ST.index(st)
                    dve.wait_ge(act_ahead, at(ACT_ORDER, f"y_hi{i}", n))
                    dve.tensor_tensor(y_lo[0:YT[i][1], i, :], ahead[0:YT[i][1], 0:D], y_hi[0:YT[i][1], i, :], ALU.subtract)\
                       .then_inc(dve_ahead, 1)
                for k, STS, use in ((1, EXPAND_ST, "expand"), (2, PROJ_ST, "proj")):
                    if st in STS:
                        i = STS.index(st)
                        ts = TILE_GROUPS[i]
                        rows, c = TILES[ts[-1]][1], slice(ts[0], ts[-1] + 1)
                        src = ahead[0:rows, 0:len(ts) * D].rearrange("p (t d) -> p t d", t=len(ts))
                        dve.wait_ge(pe_ahead, at(PE_ORDER, f"{use}{i}", n))
                        if k == 1:
                            dve.wait_ge(txt_in, 16 * len(TXTS) * n + 16 * len(TXTS))
                            if later:
                                if i == 0 and not (type(n) is int and n < 2):
                                    dve.wait_ge(out_done, 16 * NT * (n - 1))
                        addend = base if k == 1 else h[p]
                        dve.tensor_tensor(h[p][0:rows, c, :], src, addend[0:rows, c, :], ALU.add).then_inc(dve_ahead, 1)
                        layernorm(k, i, n, p)
                if st in MIX_ST:
                    qi = MIX_ST.index(st)
                    q = "kvr"[qi]
                    view2 = {s: xT[s][:, :].rearrange("p (b t) -> p b t", b=2) for s in "AB"}
                    two = lambda m: m[:, :].rearrange("p (b t) -> p b t", b=2)
                    if qi == 0:
                        for s in "AB":
                            dve.wait_ge(act_ahead, at(ACT_ORDER, f"xT_{s}2", n))
                            dve.tensor_tensor(two(dT[s]), view2[s][:, :, 1:SEQ + 1], view2[s][:, :, 0:SEQ], ALU.subtract)\
                               .then_inc(dve_ahead, 1)
                        after("dB", n)
                    for si, s in enumerate("AB"):
                        dve.scalar_tensor_tensor(out=two(mix32[s]), in0=two(dT[s]), scalar=par[:, PM + 2 * qi + si:PM + 2 * qi + si + 1],
                                                 in1=view2[s][:, :, 0:SEQ], op0=ALU.mult, op1=ALU.add).then_inc(dve_ahead, 1)
                    dve.wait_ge(act_ahead, at(ACT_ORDER, f"{q}_hiA", n))
                    dve.tensor_tensor(mixl[qi % 2][:, :], mix32["A"][:, :], mixh[qi % 2][:, :], ALU.subtract).then_inc(dve_ahead, 1)
                    dve.wait_ge(act_ahead, at(ACT_ORDER, f"{q}_hiB", n))
                    dve.tensor_tensor(mixB[qi % 2][DB:128, :], mix32["B"][DB:128, :], mixB[qi % 2][DB:128, :], ALU.subtract)\
                       .then_inc(dve_ahead, 1)
                    after(f"{q}_loB", n)
                if st in Z_ST:
                    g = Z_ST.index(st)
                    dve.wait_ge(act_ahead, at(ACT_ORDER, f"k{g}", n))
                    dve.tensor_tensor_scan(mrun[:, g, 1:SEQ + 1], wfull[:, g, :], kvr["k"][:, g, :], -1e38, ALU.add, ALU.max)\
                       .then_inc(dve_ahead, 1)
                    after(f"m{g}", n)
                    dve.scalar_tensor_tensor(out=z[:, g, :], in0=kvr["k"][:, g, :], scalar=negw[:, g:g + 1],
                                             in1=mrun[:, g, 0:SEQ], op0=ALU.subtract, op1=ALU.subtract).then_inc(dve_ahead, 1)
                    after(f"z{g}", n)
                    dve.tensor_scalar(zp[:, g, :], z[:, g, :], 0.0, None, ALU.max).then_inc(dve_ahead, 1)
                    dve.tensor_scalar(zn[:, g, :], z[:, g, :], 0.0, None, ALU.min).then_inc(dve_ahead, 1)
                    dve.tensor_scalar(qp[:, g, :], z[:, g, :], wplusu[:, g:g + 1], 0.0, ALU.add, ALU.max).then_inc(dve_ahead, 1)
                    dve.tensor_scalar(qn[:, g, :], z[:, g, :], wplusu[:, g:g + 1], 0.0, ALU.add, ALU.min).then_inc(dve_ahead, 1)
                if st in SCAN_ST:
                    g = SCAN_ST.index(st)
                    dve.wait_ge(pool_ahead, at(POOL_ORDER, f"t2{g}", n))
                    dve.tensor_tensor_scan(num[:, g, 1:SEQ + 1], e1s[:, g, :], ev[:, g, :], 0.0, ALU.mult, ALU.add)\
                       .then_inc(dve_ahead, 1)
                    dve.tensor_tensor_scan(den[:, g, 1:SEQ + 1], e1s[:, g, :], e2s[:, g, :], 0.0, ALU.mult, ALU.add)\
                       .then_inc(dve_ahead, 1)
                    after(f"num{g}", n)
                    dve.tensor_tensor(ev[:, g, :], e1[:, g, :], num[:, g, 0:SEQ], ALU.mult).then_inc(dve_ahead, 1)
                    after(f"t1{g}", n)
                    dve.tensor_tensor(ev[:, g, :], ev[:, g, :], z[:, g, :], ALU.add).then_inc(dve_ahead, 1)
                    after(f"den{g}", n)
                    dve.tensor_tensor(e1s[:, g, :], e1[:, g, :], den[:, g, 0:SEQ], ALU.mult).then_inc(dve_ahead, 1)
                    after(f"d1{g}", n)
                    dve.tensor_tensor(e1s[:, g, :], e1s[:, g, :], e2[:, g, :], ALU.add).then_inc(dve_ahead, 1)
                    after(f"d2{g}", n)
                    dve.scalar_tensor_tensor(out=e1s[:, g, :], in0=kvr["r"][:, g, :], scalar=1.0, in1=e1s[:, g, :],
                                             op0=ALU.add, op1=ALU.mult).then_inc(dve_ahead, 1)
                    after(f"d3{g}", n)
                    dve.reciprocal(e1s[:, g, :], e1s[:, g, :]).then_inc(dve_ahead, 1)
                    after(f"rec{g}", n)
                    dve.tensor_tensor(ev[:, g, :], ev[:, g, :], e1s[:, g, :], ALU.mult).then_inc(dve_ahead, 1)
                if st == OSPLIT_ST:
                    dve.wait_ge(act_ahead, at(ACT_ORDER, "o_hiA", n))
                    two = lambda m: m[:, :].rearrange("p (b t) -> p b t", b=2)
                    dve.tensor_tensor(two(ol_A), ev[:, 0:2, :], two(oh_A), ALU.subtract).then_inc(dve_ahead, 1)
                    for b in range(2):
                        ps, cs = slice(b * DB, (b + 1) * DB), slice(b * SEQ, (b + 1) * SEQ)
                        dve.wait_ge(act_ahead, at(ACT_ORDER, f"o_hiB{b}", n))
                        dve.tensor_tensor(ol_B[ps, cs], ev[ps, 2, :], oh_B[ps, cs], ALU.subtract).then_inc(dve_ahead, 1)
                if st in TURN2_ST:
                    i = TURN2_ST.index(st)
                    last = {0: "X_hA0", 1: "X_hB0", 2: "X_hB1"}[i]
                    dve.wait_ge(act_ahead, at(ACT_ORDER, last, n))
                    for s, lo, hi, col in TURNS[i]:
                        if s == "A":
                            dve.tensor_tensor(XAl[p][:, lo:hi], ahead[:, col:col + hi - lo], XAh[p][:, lo:hi], ALU.subtract)\
                               .then_inc(dve_ahead, 1)
                        else:
                            dve.tensor_tensor(XB[p][DB:128, lo:hi], ahead[DB:128, col:col + hi - lo], XB[p][DB:128, lo:hi],
                                              ALU.subtract).then_inc(dve_ahead, 1)
                if st == LOGIT_ST:
                    bc = [128, NT, EXP]
                    all_t = lambda m: m[:, :].unsqueeze(1).to_broadcast(bc)
                    per_t = lambda m: rs[m][:, :].unsqueeze(2).to_broadcast(bc)
                    dve.wait_ge(pe_ahead, at(PE_ORDER, "logits", n))
                    dve.tensor_tensor(lg[:, :, :], ahead[:, 0:NT * EXP].rearrange("p (t e) -> p t e", t=NT), all_t(gb_bc), ALU.add)\
                       .then_inc(dve_ahead, 1)
                    after("lg", n)
                    dve.tensor_reduce(rs["lmax"][:, :], lg[:, :, :], AX_X, ALU.max).then_inc(dve_ahead, 1)
                    after("lmax", n)
                    dve.tensor_tensor(lg[:, :, :], lg[:, :, :], per_t("lmax"), ALU.subtract).then_inc(dve_ahead, 1)
                    dve.wait_ge(act_ahead, at(ACT_ORDER, "softmax", n))
                    dve.tensor_reduce(rs["lsum"][:, :], ex[:, :, :], AX_X, ALU.add).then_inc(dve_ahead, 1)
                    after("lsum", n)
                    dve.reciprocal(rs["lrec"][:, :], rs["lsum"][:, :]).then_inc(dve_ahead, 1)
                    after("lrec", n)
                    dve.tensor_tensor(score[:, :, :], ex[:, :, :], per_t("lrec"), ALU.mult).then_inc(dve_ahead, 1)
                    after("score", n)
                    dve.tensor_tensor(biased[:, :, :], score[:, :, :], all_t(bias_bc), ALU.add).then_inc(dve_ahead, 1)
                    after("biased", n)
                    pairs = biased[:, :, :].rearrange("p t (g k) -> p t g k", k=2)
                    dve.tensor_tensor(gsum[:, :, :], pairs[:, :, :, 0], pairs[:, :, :, 1], ALU.add).then_inc(dve_ahead, 1)
                    settle("gsum", "gsum_set", n)
                    for t in range(NT):
                        dve.max(gtop[:, t, :], gsum[:, t, :]).then_inc(dve_ahead, 1)
                    after(f"gtop{NT - 1}", n)
                    select4(gsum, "gthr", gtop, ggt, geq, "gcnt", "gneed", gcum, reset_g, GROUPS, "g", n)
                    dve.tensor_scalar(gbig[:, :, :], ggt[:, :, :], 1e30, -1e30, ALU.mult, ALU.add).then_inc(dve_ahead, 1)
                    flat = lambda m: m[:, :, :].rearrange("p t g -> p (t g)").unsqueeze(2).to_broadcast([128, NT * GROUPS, 2])
                    f2 = lambda m: m[:, :, :].rearrange("p t (g k) -> p (t g) k", k=2)
                    dve.tensor_tensor(f2(masked), f2(biased), flat(ggt), ALU.mult).then_inc(dve_ahead, 1)
                    after("masked", n)
                    dve.tensor_tensor(f2(masked), f2(masked), flat(gbig), ALU.add).then_inc(dve_ahead, 1)
                    settle("masked2", "masked_set", n)
                    for t in range(NT):
                        dve.max(etop[:, t, :], masked[:, t, :]).then_inc(dve_ahead, 1)
                    after(f"etop{NT - 1}", n)
                    select4(masked, "ethr", etop, egt, eeq, "ecnt", "eneed", ecum, reset_e, EXP, "e", n)
                    dve.scalar_tensor_tensor(out=wfl[:, :, :], in0=score[:, :, :], scalar=SCALE, in1=egt[:, :, :],
                                             op0=ALU.mult, op1=ALU.mult).then_inc(dve_ahead, 1)
                    after("wfull", n)
                    dve.tensor_copy(wcat[:, :, 0:EXP], wfl[:, :, :]).then_inc(dve_ahead, 1)
                    after("w_hi", n)
                    dve.tensor_tensor(wcat[:, :, 32:32 + EXP], wfl[:, :, :], wcat[:, :, 0:EXP], ALU.subtract).then_inc(dve_ahead, 1)

            def finish(n, pp):
                dve.wait_ge(down_done, NX * n + NX)
                for i, ts in enumerate(TILE_GROUPS):
                    rows, c = TILES[ts[-1]][1], slice(ts[0], ts[-1] + 1)
                    src = ysum[0:rows, i, 0:len(ts) * D].rearrange("p (t d) -> p t d", t=len(ts))
                    dve.tensor_tensor(h[pp][0:rows, c, :], src, h[pp][0:rows, c, :], ALU.add).then_inc(fin_done, 1)

            def body(n, pp, first=False, last=False):
                for s in range(SLOTS):
                    S = 34 * n + s
                    e = s // 2
                    dve.wait_ge(silu_done, S + 1)
                    dve.wait_ge(gate_ready, S + 1)
                    if s >= 4 or not first:
                        dve.wait_ge(lo_done, S - 3)
                    dve.scalar_tensor_tensor(out=a32[(34 * pp + s) % 4][:, :], in0=gts[:, s % 2, 0:SEQ],
                                             scalar=par[:, PBG + e:PBG + e + 1], in1=silu[s % 2][:, :],
                                             op0=ALU.add, op1=ALU.mult).then_inc(gated, 1)
                    if s == 1 and not first:
                        finish(n - 1, (pp + 1) % 2)
                    if not last:
                        ahead_step(s, n + 1, (pp + 1) % 2)

            for st in range(SLOTS):
                ahead_step(st, 0, 0)
            body(0, 0, first=True)
            with dve.Fori(0, PAIRS // 2 - 1) as i:
                for p in range(2):
                    body(2 * i + 1 + p, (1 + p) % 2)
            body(PAIRS - 1, 1, last=True)
            finish(PAIRS - 1, 1)

        @block.tensor
        def _(pe):
            pe.wait_ge(set_dve, len(SET_DVE))
            pe.wait_ge(set_pool, SET_POOL)

            def free(name, n):
                k = PE_ORDER.index(name)
                if k == 0:
                    if type(n) is int and n == 0:
                        return
                    who, step, m = "act", "wcol_c", n - 1
                else:
                    (who, step), m = READER[PE_ORDER[k - 1]], n
                if who == "act":
                    pe.wait_ge(act_ahead, at(ACT_ORDER, step, m))
                else:
                    pe.wait_ge(dve_ahead, at(DVE_ORDER, step, m))

            def chain(dst, terms, skip=False):
                for i, (lhsT, rhs) in enumerate(terms):
                    mm = pe.matmul(dst, lhsT, rhs, start=(i == 0), stop=(i == len(terms) - 1))
                return mm

            def ahead_step(st, n, p):
                if st in PATCH_ST:
                    i = PATCH_ST.index(st)
                    cs = slice(YT[i][0], YT[i][0] + YT[i][1])
                    pe.wait_ge(dve_ahead, at(DVE_ORDER, f"x_lo{XPIECES - 1}", n))
                    free(f"patch{i}", n)
                    chain(ahead[0:YT[i][1], 0:D], [(x[:, c, cs], w[:, c, :]) for c in range(KC) for x, w in
                                                   ((x_hi, patch_hi), (x_lo, patch_hi), (x_hi, patch_lo))]).then_inc(pe_ahead, 1)
                if st in EXPAND_ST:
                    i = EXPAND_ST.index(st)
                    free(f"expand{i}", n)
                    ts = TILE_GROUPS[i]
                    for j, t in enumerate(ts):
                        t0, rows = TILES[t]
                        terms = [(sel[0:YT[k][1], k, t0:t0 + rows], y[0:YT[k][1], k, :]) for k in SELECTED[t] for y in (y_hi, y_lo)]
                        for m, (a, b_) in enumerate(terms):
                            mm = pe.matmul(ahead[0:rows, j * D:(j + 1) * D], a, b_, start=(j == 0 and m == 0),
                                           stop=(m == len(terms) - 1), skip_group_check=True)
                    mm.then_inc(pe_ahead, 1)
                for k, STS in ((1, TURN1_ST), (2, TURN2_ST)):
                    if st in STS:
                        i = STS.index(st)
                        free(f"turn{k}_{i}", n)
                        pe.wait_ge(dve_ahead, at(DVE_ORDER, f"xd{k}_{(3, 4, 4)[i]}", n))
                        for s, lo, hi, col in TURNS[i]:
                            for t, (t0, rows) in enumerate(TILES):
                                if lo <= t0 < hi:
                                    cs = slice(0, DA) if s == "A" else slice(DA, 256)
                                    mm = pe.transpose(ahead[:, col + t0 - lo:col + t0 - lo + rows], xn[0:rows, t, cs],
                                                      id32[0:rows, 0:rows])
                        mm.then_inc(pe_ahead, 1)
                for name in KVR_ST.get(st, ()):
                    q, g = name[0], int(name[1])
                    qi = "kvr".index(q)
                    free(name, n)
                    pe.wait_ge(dve_ahead, at(DVE_ORDER, f"{q}_loB", n))
                    W = {s: kvr_w[s][:, qi, :] for s in kvr_w}

                    def terms(b, c0):
                        ws, cs = slice(c0, c0 + 128), slice(b * SEQ, (b + 1) * SEQ)
                        mh, ml, mb = mixh[qi % 2][:, cs], mixl[qi % 2][:, cs], mixB[qi % 2][:, cs]
                        return [(W["Ah"][:, ws], mh), (W["Ah"][:, ws], ml), (W["Al"][:, ws], mh),
                                (W["Bh"][:, ws], mb), (W["Bl"][:, ws], mb)]
                    both = terms(g, 0) if g < 2 else terms(0, DA + DB) + terms(1, DA)
                    chain(ahead[:, 0:SEQ], both).then_inc(pe_ahead, 1)
                if st in PROJ_ST:
                    i = PROJ_ST.index(st)
                    free(f"proj{i}", n)
                    pe.wait_ge(dve_ahead, at(DVE_ORDER, "o_loB1", n))
                    for j, t in enumerate(TILE_GROUPS[i]):
                        t0, rows = TILES[t]
                        cs = slice(t0, t0 + rows)
                        terms_ = [(oh_A[:, cs], wo_w["Ah"]), (ol_A[:, cs], wo_w["Ah"]), (oh_A[:, cs], wo_w["Al"]),
                                  (oh_B[:, cs], wo_w["Bh"]), (ol_B[:, cs], wo_w["Bh"]), (oh_B[:, cs], wo_w["Bl"])]
                        for m, (a, b_) in enumerate(terms_):
                            mm = pe.matmul(ahead[0:rows, j * D:(j + 1) * D], a, b_[:, :], start=(j == 0 and m == 0),
                                           stop=(m == 5), skip_group_check=True)
                    mm.then_inc(pe_ahead, 1)
                if st == LOGIT_ST:
                    free("logits", n)
                    for t in range(NT):
                        cs = slice(t * 128, (t + 1) * 128)
                        terms_ = [(XAh[p][:, cs], gw_w["Ah"]), (XAl[p][:, cs], gw_w["Ah"]), (XAh[p][:, cs], gw_w["Al"]),
                                  (XB[p][:, cs], gw_w["Bh"]), (XB[p][:, cs], gw_w["Bl"])]
                        for m, (a, b_) in enumerate(terms_):
                            mm = pe.matmul(ahead[:, t * EXP:(t + 1) * EXP], a, b_[:, :], start=(t == 0 and m == 0),
                                           stop=(m == 4), skip_group_check=True)
                    mm.then_inc(pe_ahead, 1)
                if st == WROW_ST:
                    for i, ts in enumerate((range(4), range(4, NT))):
                        pe.wait_ge(dve_ahead, at(DVE_ORDER, "w_lo", n))
                        free(f"wrow{i}", n)
                        for t in ts:
                            mm = pe.transpose(ahead[0:EXP, (t - ts[0]) * 128:(t - ts[0] + 1) * 128], wfl[:, t, :], id32[:, :])
                        mm.then_inc(pe_ahead, 1)
                    free("wcol", n)
                    for t in range(NT):
                        mm = pe.transpose(ahead16[:, t * 128:(t + 1) * 128], wcat[:, t, :], id16[:, :])
                    mm.then_inc(pe_ahead, 1)

            def down(n, e, pp):
                pe.wait_ge(lo_done, 34 * n + 2 * e + 2)
                if e == 0 and (type(n) is not int or n > 0):
                    pe.wait_ge(fin_done, 3 * n)
                for t, (t0, rows) in enumerate(TILES):
                    i, j = divmod(t, 2)
                    ah, al = a_hi[(pp + e) % 2][:, t0:t0 + rows], a_lo[(pp + e) % 2][:, t0:t0 + rows]
                    dst = ysum[0:rows, i, j * D:(j + 1) * D]
                    pe.matmul(dst, ah, dn_h[:, e, :], start=(e == 0 and j == 0), stop=False, skip_group_check=True)
                    pe.matmul(dst, ah, dn_l[:, e, :], start=False, stop=False, skip_group_check=True)
                    mm = pe.matmul(dst, al, dn_h[:, e, :], start=False, stop=False, skip_group_check=True)
                    if e == NX - 1:
                        w = wT[pp][:, t0:t0 + rows]
                        pe.matmul(dst, w, bd_h[:, :], start=False, stop=False, skip_group_check=True)
                        mm = pe.matmul(dst, w, bd_l[:, :], start=False, stop=True, skip_group_check=True)
                mm.then_inc(down_done, 1)

            def body(n, pp, first=False, last=False):
                for s in range(SLOTS):
                    e, b = divmod(s, 2)
                    S = 34 * n + s
                    cs = slice(b * SEQ, (b + 1) * SEQ)
                    if s == 0:
                        pe.wait_ge(dve_ahead, at(DVE_ORDER, "X_lB1", n))
                    x5 = (XAh[pp][:, cs], XAl[pp][:, cs], XAh[pp][:, cs], XB[pp][:, cs], XB[pp][:, cs])
                    if s >= 2 or not first:
                        pe.wait_ge(silu_done, S - 1)
                    chain(ups[:, s % 2, 0:SEQ], [(up_w[k][:, e, :], x) for k, x in zip(("Ah", "Ah", "Al", "Bh", "Bl"), x5)])\
                        .then_inc(up_ready, 1)
                    if s >= 2 or not first:
                        pe.wait_ge(gated, S - 1)
                    chain(gts[:, s % 2, 0:SEQ], [(gt_w[k][:, e, :], x) for k, x in zip(("Ah", "Ah", "Al", "Bh", "Bl"), x5)])\
                        .then_inc(gate_ready, 1)
                    if b == 1 and e > 0:
                        down(n, e - 1, pp)
                    if s == 0 and not first:
                        down(n - 1, NX - 1, (pp + 1) % 2)
                    if not last:
                        ahead_step(s, n + 1, (pp + 1) % 2)

            for st in range(SLOTS):
                ahead_step(st, 0, 0)
            body(0, 0, first=True)
            with pe.Fori(0, PAIRS // 2 - 1) as i:
                for p in range(2):
                    body(2 * i + 1 + p, (1 + p) % 2)
            body(PAIRS - 1, 1, last=True)
            down(PAIRS - 1, NX - 1, 1)


_OUTS = [((BATCH, SEQ, D), 'float32')]


def kernel(**inputs):
    import numpy as _np
    import concourse.bacc as _bacc
    from concourse import mybir as _mybir
    from concourse.bass_utils import run_bass_kernel_spmd as _run

    v = {k: _np.asarray(a) for k, a in inputs.items()}
    n = {k.replace("L0_tok_", "").replace("L0_attn_", "").replace("L0_ffn_", ""): a for k, a in v.items()}

    c = _np.array([[p[0] for p in tok] for tok in DISTINCT])
    step = _np.arange(WIN)
    r = _np.minimum(_np.array([[p[1] for p in tok] for tok in DISTINCT])[:, :, None] * STRIDE + step, IMG - 1)
    q = _np.minimum(_np.array([[p[2] for p in tok] for tok in DISTINCT])[:, :, None] * STRIDE + step, IMG - 1)
    win = n["x"][:, c[:, :, None, None], r[:, :, :, None], q[:, :, None, :]]
    pixels = win.reshape(PAIRS, 2, ND, KC, KP).transpose(0, 4, 3, 1, 2).reshape(PAIRS, KP, KC * PX)

    onehot = _np.zeros((YW, 3, PAIR), _np.float16)
    for b in range(2):
        for t in range(NPATCH):
            k, row = divmod(b * ND + WHICH[t], YW)
            onehot[row, k, b * SEQ + 1 + t] = 1

    def chan(a, parts):
        cols = [a[:DA]] * (parts - 1) + [_np.concatenate([a[DA:], a[DA:]])]
        return _np.stack(cols, 1)

    params = _np.concatenate(
        [chan(n["time_decay"], 3), chan(n["time_first"], 3), chan(n["mix_k"], 2), chan(n["mix_v"], 2), chan(n["mix_r"], 2),
         n["sbu"][:, None], n["bu"].T, n["sbg"][:, None], n["bg"].T], 1)
    arrays = {
        "pixels": pixels, "txt": n["txt"].reshape(PAIRS, 2, TXT, D), "pos": n["pos_embedding"], "cls_token": n["cls_token"][0],
        "patch_w": n["proj_w"].T.reshape(KC, KP, D).transpose(1, 0, 2),
        "wkvr": _np.stack([n["Wk"].T, n["Wv"].T, n["Wr"].T], 1), "wo": n["Wo"].T, "gate_w": n["gate_w"],
        "wu": n["Wu"], "wg": n["Wg"], "wd": n["Wd"], "swu": n["sWu"], "swg": n["sWg"], "swd": n["sWd"],
        "bd": n["bd"], "sbd": n["sbd"][None, :], "gate_b": n["gate_b"], "gate_bias": n["bias"], "params": params,
        "onehot": onehot, "ident32": _np.eye(128, dtype=_np.float32), "ident16": _np.eye(128, dtype=_np.float16),
    }
    nc = _bacc.Bacc("TRN2", target_bir_lowering=False, num_devices=1)
    feed, args = {}, {}
    for name, a in arrays.items():
        a = _np.ascontiguousarray(a)
        feed[f"in_{name}"] = a
        args[name] = nc.dram_tensor(f"in_{name}", a.shape, _mybir.dt.from_np(a.dtype), kind="ExternalInput").ap()
    args["out"] = nc.dram_tensor("out_0", _OUTS[0][0], _mybir.dt.from_np(_np.dtype(_OUTS[0][1])), kind="ExternalOutput").ap()
    build_fusion(nc, **args)
    res = _run(nc, [feed], core_ids=[0])
    return res.results[0]["out_0"]
```

```python
from contextlib import ExitStack

import concourse.bass as bass
from concourse import mybir

F32 = mybir.dt.float32
F16 = mybir.dt.float16
ALU = mybir.AluOpType
ACT = mybir.ActivationFunctionType
AX_X = mybir.AxisListType.X

BATCH, CH, IMG = 64, 3, 96
D = 192
DA, DB = 128, 64
GRID, STRIDE, WIN = 16, 13, 20
TXT = 32
NPATCH = GRID * GRID
SEQ = 1 + NPATCH + TXT
PAIR = 2 * SEQ
PAIRS = BATCH // 2
EXP, HID = 16, 128
NX = EXP + 1
GROUPS, TOPK = 8, 4
SCALE = 2.5
EPS = 1e-5
TILES = [(t * 128, min(128, PAIR - t * 128)) for t in range(-(-PAIR // 128))]
NT = len(TILES)
PADT = NT * 128
TILE_GROUPS = [(0, 1), (2, 3), (4,)]
KC, KP = 10, 120
SLOTS = 2 * NX


def token_patches(t):
    last = -(-(IMG - 1) // STRIDE)
    return tuple((p // NPATCH, min(p % NPATCH // GRID, last), min(p % GRID, last)) for p in range(3 * t, 3 * t + 3))


DISTINCT = []
for _t in range(NPATCH):
    if token_patches(_t) not in DISTINCT:
        DISTINCT.append(token_patches(_t))
ND = len(DISTINCT)
WHICH = [DISTINCT.index(token_patches(t)) for t in range(NPATCH)]
PX = 2 * ND
YW = -(-PX // 3)
YT = [(k * YW, min(YW, PX - k * YW)) for k in range(3)]
XPIECES = 5
XPC = KC * PX // XPIECES


def selected():
    out = []
    for t0, rows in TILES:
        ks = set()
        for tok in range(t0, t0 + rows):
            b, t = divmod(tok, SEQ)
            if 1 <= t <= NPATCH:
                ks.add((b * ND + WHICH[t - 1]) // YW)
        out.append(sorted(ks))
    return out


SELECTED = selected()


def split_at_batch(t0, t1):
    out = []
    for b in range(2):
        lo, hi = max(t0, b * SEQ), min(t1, (b + 1) * SEQ)
        if lo < hi:
            out.append((lo, lo + b + 1, hi - lo))
    return out


LANES = {"T": 0, "F": 1, "P": 2}
TURNS = [[("A", 0, 512, 0)], [("A", 512, PAIR, 0), ("B", 0, 384, PAIR - 512)], [("B", 384, PAIR, 0)]]
PE_PLAN = {1: "T.wrow0 T.wrow1 F.expand0", 2: "F.expand1", 3: "T.wcol F.expand2", 4: "F.turn1_0",
           5: "F.turn1_1 F.turn1_2", 9: "F.k0 F.k1", 10: "F.k2", 11: "F.r0 F.r1", 12: "F.r2", 13: "F.v0 F.v1",
           14: "F.v2", 15: "P.patch0", 16: "P.patch1", 17: "P.patch2", 27: "F.proj0", 28: "F.proj1",
           29: "F.proj2", 30: "F.turn2_0", 31: "F.turn2_1 F.turn2_2", 32: "F.logits"}
ACT_PLAN = {1: "T.wrow_c0 T.wrow_c1", 2: "P.x_hi0", 3: "T.wcol_c P.x_hi1 P.x_hi2", 4: "F.turned1_0 P.x_hi3 P.x_hi4",
            5: "F.turned1_1 F.turned1_2", 8: "F.highk", 9: "F.k0 F.k1", 10: "F.k2 F.highr", 11: "F.r0 F.r1",
            12: "F.r2 F.highv", 13: "F.v0 F.v1 F.relu0", 14: "F.v2 F.relu1 F.relu2", 15: "F.exps0 F.exps1 F.exps2",
            26: "F.ohigh", 30: "F.turned2_0", 31: "F.turned2_1 F.turned2_2", 32: "F.softmax"}
DVE_PLAN = {0: "T.route3", 2: "F.sum1_0 F.sum1_1", 3: "F.norm1_0 F.norm1_1 F.sum1_2",
            4: "F.norm1_2 P.x_lo0 P.x_lo1", 5: "P.x_lo2 P.x_lo3 P.x_lo4", 6: "F.diff", 7: "F.mixk", 8: "F.lowk",
            9: "F.mixr", 10: "F.lowr", 11: "F.mixv", 12: "F.lowv F.run0", 13: "F.run1 F.run2", 15: "P.y0", 16: "P.y1",
            17: "P.y2 F.scanA0", 18: "F.scanB0", 19: "F.scanC0", 20: "F.scanA1", 21: "F.scanB1", 22: "F.scanC1",
            23: "F.scanA2", 24: "F.scanB2", 25: "F.scanC2", 26: "F.olow", 27: "F.sum2_0", 28: "F.norm2_0 F.sum2_1",
            29: "F.norm2_1 F.sum2_2", 30: "F.norm2_2 F.xlow0", 31: "F.xlow1 F.xlow2", 32: "F.route1", 33: "F.route2"}
POOL_PLAN = {2: "F.rstd1_0 F.rstd1_1", 3: "F.rstd1_2", 17: "F.shares0", 18: "F.shares1", 19: "F.shares2",
             27: "F.rstd2_0", 28: "F.rstd2_1", 29: "F.rstd2_2"}


def choose_names(c):
    return [c + s for s in ("thr", "gt", "eq", "cnt", "need", "cum", "le", "and", "sel")]


PARTS = {"diff": ["dA", "dB"], "olow": ["o_loA", "o_loB0", "o_loB1"], "ohigh": ["o_hiA", "o_hiB0", "o_hiB1"],
         "route1": ["lg", "lmax", "lsh", "lsum", "lrec", "score", "biased", "gsum"],
         "route2": ["gsum_set"] + [f"gtop{t}" for t in range(NT)] + choose_names("g") + ["gbig", "masked", "masked2"],
         "route3": ["masked_set"] + [f"etop{t}" for t in range(NT)] + choose_names("e") + ["wfull", "w_hi", "w_lo"],
         "xlow0": ["X_lA0"], "xlow1": ["X_lA1", "X_lB0"], "xlow2": ["X_lB1"],
         "turned1_0": ["xT_A0", "xT_A1"], "turned1_1": ["xT_A2", "xT_B0", "xT_B1"], "turned1_2": ["xT_B2"],
         "turned2_0": ["X_hA0"], "turned2_1": ["X_hA1", "X_hB0"], "turned2_2": ["X_hB1"]}
for _g in range(3):
    PARTS[f"y{_g}"] = [f"y_hi{_g}", f"y_lo{_g}"]
    PARTS[f"run{_g}"] = [f"m{_g}", f"z{_g}"]
    PARTS[f"relu{_g}"] = [f"{v}{_g}" for v in ("zp", "zn", "qp", "qn")]
    PARTS[f"exps{_g}"] = [f"{v}{_g}" for v in ("e1s", "e2s", "e1", "e2", "er")]
    PARTS[f"shares{_g}"] = [f"ev{_g}", f"t2{_g}"]
    PARTS[f"scanA{_g}"] = [f"{v}{_g}" for v in ("num", "den", "t1", "t3")]
    PARTS[f"scanB{_g}"] = [f"{v}{_g}" for v in ("d1", "d2", "d3", "recA")]
    PARTS[f"scanC{_g}"] = [f"{v}{_g}" for v in ("recB", "o")]
    _ts = TILE_GROUPS[_g]
    for _k in (1, 2):
        PARTS[f"sum{_k}_{_g}"] = ([f"h{_k}_{_g}"] + [f"stats{_k}_{t}" for t in _ts] + [f"stats_set{_k}_{_g}"]
                                  + [f"aggr{_k}_{t}" for t in _ts] + [f"veps{_k}_{_g}"])
        PARTS[f"norm{_k}_{_g}"] = [f"{v}{_k}_{t}" for t in _ts for v in ("xn", "xd")]
for _q in "kvr":
    PARTS[f"mix{_q}"] = [f"{_q}_mA", f"{_q}_mB"]
    PARTS[f"high{_q}"] = [f"{_q}_hiA", f"{_q}_hiB"]
    PARTS[f"low{_q}"] = [f"{_q}_loA", f"{_q}_loB"]


def order_of(plan):
    out = {lane: [] for lane in LANES}
    for st in sorted(plan):
        for item in plan[st].split():
            lane, name = item.split(".")
            out[lane] += PARTS.get(name, [name])
    return out


PE, ACTE, DVE, POOL = (order_of(p) for p in (PE_PLAN, ACT_PLAN, DVE_PLAN, POOL_PLAN))
USES = [tuple(item.split(".")) for st in sorted(PE_PLAN) for item in PE_PLAN[st].split()]
READER = {f"patch{i}": ("dve", f"y_lo{i}") for i in range(3)}
READER.update({f"expand{i}": ("dve", f"h1_{i}") for i in range(3)})
READER.update({f"turn1_{i}": ("act", n) for i, n in enumerate(("xT_A1", "xT_B1", "xT_B2"))})
READER.update({f"{q}{g}": ("act", f"{q}{g}") for q in "kvr" for g in range(3)})
READER.update({f"proj{i}": ("dve", f"h2_{i}") for i in range(3)})
READER.update({f"turn2_{i}": ("dve", n) for i, n in enumerate(("X_lA0", "X_lB0", "X_lB1"))})
READER.update({"logits": ("dve", "lg"), "wrow0": ("act", "wrow_c0"), "wrow1": ("act", "wrow_c1"), "wcol": ("act", "wcol_c")})
SET_POOL = 25
WB = 2 * EXP
ROWS_EVEN, ROWS_ODD = 4, 3
TXTS = [(b, lo, hi) for b in range(2) for t0, rows in TILES
        for lo, hi in [(max(t0, b * SEQ + 1 + NPATCH), min(t0 + rows, (b + 1) * SEQ))] if lo < hi]


def cut_at_bank(c0, c1):
    edge = (c0 // 512 + 1) * 512
    return [(c0, c1)] if c1 <= edge else [(c0, edge), (edge, c1)]


def at(order, name, n):
    return n * len(order) + order.index(name) + 1


def known(n):
    return n if type(n) is int else None


def build_fusion(nc, pixels, txt, pos, cls_token, patch_w, wkvr, wo, gate_w, wu, wg, wd, swu, swg, swd,
                 bd, sbd, gate_b, gate_bias, params, onehot, ident32, ident16, out):
    out_rows = out.rearrange("(n b) t c -> n (b t) c", b=2)
    with ExitStack() as ctx:
        def sb(name, shape, dt=F32):
            return ctx.enter_context(nc.sbuf_tensor(name, shape, dt))

        def sem(name):
            return ctx.enter_context(nc.semaphore(name))

        patch_hi, patch_lo = sb("patch_hi", [KP, KC, D], F16), sb("patch_lo", [KP, KC, D], F16)
        PW = 320
        kvr_w = {s: sb(f"kvr_{s}", [128, 3, PW], F16) for s in ("Ah", "Al", "Bh", "Bl")}
        wo_w = {s: sb(f"wo_{s}", [128, D], F16) for s in ("Ah", "Al", "Bh", "Bl")}
        gw_w = {s: sb(f"gw_{s}", [128, EXP], F16) for s in ("Ah", "Al", "Bh", "Bl")}
        up_w = {s: sb(f"up_{s}", [128, NX, HID], F16) for s in ("Ah", "Al", "Bh", "Bl")}
        gt_w = {s: sb(f"gt_{s}", [128, NX, HID], F16) for s in ("Ah", "Al", "Bh", "Bl")}
        dn_h, dn_l = sb("dn_h", [HID, NX, D], F16), sb("dn_l", [HID, NX, D], F16)
        bd_h, bd_l = sb("bd_h", [128, D], F16), sb("bd_l", [128, D], F16)
        par = sb("par", [128, 12 + 2 * NX])
        sel = sb("sel", [YW, 3, PAIR], F16)
        id32, id16 = sb("id32", [128, 128]), sb("id16", [128, 128], F16)
        gb_bc, bias_bc = sb("gb_bc", [128, EXP]), sb("bias_bc", [128, EXP])
        base = sb("base", [128, NT, D])
        decay = sb("decay", [128, 3])
        negw = sb("negw", [128, 3])
        wplusu, minusc = sb("wplusu", [128, 3]), sb("minusc", [128, 3])
        wfull = sb("wfull", [128, 3, SEQ])
        half = sb("half", [128, NT])
        reset_g, reset_e = sb("reset_g", [128, NT, GROUPS]), sb("reset_e", [128, NT, EXP])

        scan_buf, early_buf = sb("scan_buf", [128, 4 * 3 * SEQ]), sb("early_buf", [128, KC * PX + 4 * PAIR])
        xraw = scan_buf[0:KP, 0:KC * PX]
        bd32 = sb("bd32", [128, D])
        x_hi, x_lo = (early_buf[0:KP, i * KC * PX // 2:(i + 1) * KC * PX // 2].bitcast(F16).rearrange("p (c n) -> p c n", c=KC)
                      for i in range(2))
        y_hi, y_lo = sb("y_hi", [YW, 3, D], F16), sb("y_lo", [YW, 3, D], F16)
        h = [sb(f"h{p}", [128, NT, D]) for p in range(2)]
        stats, mv = sb("stats", [128, NT, 6]), sb("mv", [128, NT, 2])
        veps, rstd = sb("veps", [128, NT]), sb("rstd", [128, NT])
        xn = sb("xn", [128, NT, 256])
        xT = {s: sb(f"xT_{s}", [128, 2 * (SEQ + 1)]) for s in "AB"}
        dT, mix32 = ({s: early_buf[:, KC * PX + (2 * j + i) * PAIR:KC * PX + (2 * j + i + 1) * PAIR] for i, s in enumerate("AB")}
                     for j in range(2))
        mixh = [sb(f"mixh{i}", [128, PAIR], F16) for i in range(2)]
        mixl = [sb(f"mixl{i}", [128, PAIR], F16) for i in range(2)]
        mixB = [sb(f"mixB{i}", [128, PAIR], F16) for i in range(2)]
        kvr = {q: sb(f"{q}32", [128, 3, SEQ]) for q in "kvr"}
        mrun, num, den = (sb(f"{s}run", [128, 3, SEQ + 1]) for s in ("m", "n", "d"))
        z = kvr["k"]
        zp, zn, qp, qn = (scan_buf[:, i * 3 * SEQ:(i + 1) * 3 * SEQ].rearrange("p (g t) -> p g t", g=3) for i in range(4))
        e1s, e2s, e1, e2 = zp, zn, qp, qn
        ev_buf = sb("ev_buf", [128, NT * D])
        ev = ev_buf[:, 0:3 * SEQ].rearrange("p (g t) -> p g t", g=3)
        yout = ev_buf[:, :].rearrange("p (t d) -> p t d", t=NT)
        oh_A, ol_A = mixh[0], mixl[0]
        oh_B, ol_B = sb("oh_B", [128, PAIR], F16), sb("ol_B", [128, PAIR], F16)
        XAh, XAl, XB = ([sb(f"{s}{p}", [128, PADT], F16) for p in range(2)] for s in ("XAh", "XAl", "XB"))
        def r16(name, w=EXP):
            return sb(name, [128, NT, w])

        lg, ex, score, biased, masked = (r16(s) for s in ("lg", "ex", "score", "biased", "masked"))
        egt, eeq, ecum = (r16(s) for s in ("egt", "eeq", "ecum"))
        gsum, ggt, geq, gcum, gbig, gtop, etop = (r16(s, GROUPS) for s in ("gsum", "ggt", "geq", "gcum", "gbig", "gtop", "etop"))
        rs = {s: sb(s, [128, NT]) for s in ("lmax", "lsum", "lrec", "gthr", "gcnt", "gneed", "ethr", "ecnt", "eneed")}
        wfl = r16("wfl")
        settled, carried = sb("settled", [1, 2]), sb("carried", [1, 1])
        carry_done = sem("carry_done")
        wcat = sb("wcat", [128, NT, 128], F16)
        wT = [sb(f"wT{p}", [128, PADT], F16) for p in range(2)]
        wrow16 = sb("wrow16", [EXP, PADT])
        wrow_buf = sb("wrow_buf", [1, 4 * PAIR])
        wrow = wrow_buf[0:1, :].rearrange("p (e t) -> p e t", e=4)

        wb = [sb(f"wb{i}", [128, PAIR]) for i in range(2)]
        silu = [sb(f"silu{i}", [128, SEQ]) for i in range(2)]
        a32 = [sb(f"a32_{i}", [128, SEQ]) for i in range(4)]
        a_hi = [sb(f"a_hi{i}", [128, PAIR], F16) for i in range(2)]
        a_lo = [sb(f"a_lo{i}", [128, PAIR], F16) for i in range(2)]

        ups = ctx.enter_context(nc.psum_tensor("ups", [128, 2, 512], F32))
        gts = ctx.enter_context(nc.psum_tensor("gts", [128, 2, 512], F32))
        ysum = ctx.enter_context(nc.psum_tensor("ysum", [128, 2 * 512], F32))
        lanes_ps = ctx.enter_context(nc.psum_tensor("lanes_ps", [128, 2, 512], F32))

        def bank(name):
            return lanes_ps[:, [u[1] for u in USES].index(name) % 2, :]


        consts_in = sem("consts_in")
        stage_in = [sem("stage_in0"), sem("stage_in1")]
        set_dve, set_act, set_pool = sem("set_dve"), sem("set_act"), sem("set_pool")
        base_in = sem("base_in")
        pixels_in, txt_in = sem("pixels_in"), sem("txt_in")
        rows_in = [sem("rows_even_in"), sem("rows_odd_in")]
        pe_f, act_f, dve_f, pool_f = (sem(s) for s in ("pe_front", "act_front", "dve_front", "pool_front"))
        pe_t, act_t, dve_t = (sem(s) for s in ("pe_tail", "act_tail", "dve_tail"))
        pe_p, act_p, dve_p = (sem(s) for s in ("pe_patch", "act_patch", "dve_patch"))
        up_ready, gate_ready = sem("up_ready"), sem("gate_ready")
        silu_done, gated, weighted, hi_done, lo_done = (sem(s) for s in ("silu_done", "gated", "weighted", "hi_done", "lo_done"))
        wb_done, down_done, fin_done, out_done = (sem(s) for s in ("wb_done", "down_done", "fin_done", "out_done"))

        def rows3(ap):
            return ap.rearrange("e k h -> k e h")

        SW = NX * D
        stage = [early_buf[:, 0:SW], scan_buf[:, 0:SW]]
        jobs = []

        def job(hi, lo, parts, p, shape):
            jobs.append((hi, lo, parts, p, shape))

        for s in range(2):
            ks = slice(0, DA) if s == 0 else slice(DA, D)
            for name, dst, routed, shared in (("up", up_w, wu, swu), ("gt", gt_w, wg, swg)):
                hi, lo = (dst["Ah"], dst["Al"]) if s == 0 else (dst["Bh"], dst["Bl"])
                parts = []
                for r in range(1 + s):
                    ps = slice(0, DA) if s == 0 else slice(r * DB, (r + 1) * DB)
                    parts.append((ps, slice(1, NX), rows3(routed)[ks]))
                    parts.append((ps, slice(0, 1), shared[ks].unsqueeze(1)))
                job(hi[:, :, :], lo[:, :, :], parts, 128, (NX, HID))
        job(dn_h[:, :, :], dn_l[:, :, :], [(slice(0, HID), slice(1, NX), rows3(wd)),
                                           (slice(0, HID), slice(0, 1), swd.unsqueeze(1))], 128, (NX, D))
        job(patch_hi[:, :, :], patch_lo[:, :, :], [(slice(0, KP), slice(0, KC), patch_w)], KP, (KC, D))
        for s in range(2):
            ks = slice(0, DA) if s == 0 else slice(DA, D)
            c = "AB"[s]
            places = [slice(0, DA)] if s == 0 else [slice(0, DB), slice(DB, 2 * DB)]
            for o0, o1, w0 in ((0, DA, 0), (DA, D, DA + DB)):
                job(kvr_w[c + "h"][:, :, w0:w0 + o1 - o0], kvr_w[c + "l"][:, :, w0:w0 + o1 - o0],
                    [(ps, slice(0, 3), wkvr[ks, :, o0:o1]) for ps in places], 128, (3, o1 - o0))
            job(wo_w[c + "h"][:, :].unsqueeze(1), wo_w[c + "l"][:, :].unsqueeze(1),
                [(ps, slice(0, 1), wo[ks].unsqueeze(1)) for ps in places], 128, (1, D))
            job(gw_w[c + "h"][:, :].unsqueeze(1), gw_w[c + "l"][:, :].unsqueeze(1),
                [(ps, slice(0, 1), gate_w[ks].unsqueeze(1)) for ps in places], 128, (1, EXP))
        JOBS = len(jobs)
        staged = [0, 0]
        need = []
        for j, (_, _, parts, _, _) in enumerate(jobs):
            staged[j % 2] += 16 * len(parts)
            need.append(staged[j % 2])

        def view(j):
            rows, cols = jobs[j][4]
            return stage[j % 2][0:jobs[j][3], 0:rows * cols].rearrange("p (a b) -> p a b", a=rows)

        T, F, P = "TFP"
        SET_DVE = (["z_settled", "z_base", "z_bd", "z_cls", "z_kh", "z_kl", "z_BH", "z_BL"] + [f"hi{j}" if s == 0 else f"lo{j}" for j in range(JOBS) for s in range(2)]
                   + ["bdhi", "bdlo", "cls0", "cls2", "negw", "wplusu", "minusc", "onesq", "wfull0", "wfull1", "wfull2"])
        BASE_DMAS = 5 + sum(max(t0, b * SEQ) < min(t0 + rows, b * SEQ + 1 + NPATCH) for b in range(2) for t0, rows in TILES)
        PD, PU, PM, PBU, PBG = 0, 3, 6, 12, 12 + NX
        clsT = xn[:, :, 0:D]

        def q_at(name):
            return SET_DVE.index(name) + 1

        def steps_of(plan, st, n, pp):
            out_ = []
            for item in plan.get(st, "").split():
                lane, name = item.split(".")
                m = n + LANES[lane]
                if known(n) is None or 0 <= m < PAIRS:
                    out_.append((name, m, (pp + LANES[lane]) % 2))
            return out_

        block = ctx.enter_context(nc.Block())

        @block.sync
        def _(sp):
            nconst = 0
            for dst, src in ((par[:, :], params), (sel[:, :, :], onehot), (id32[:, :], ident32), (id16[:, :], ident16),
                             (gb_bc[:, :], gate_b.partition_broadcast(128)), (bias_bc[:, :], gate_bias.partition_broadcast(128))):
                sp.dma_start(dst, src).then_inc(consts_in, 16)
                nconst += 1
            sp.wait_ge(set_dve, q_at("z_cls"))
            nb = 0
            for b in range(2):
                for t, (t0, rows) in enumerate(TILES):
                    lo, hi = max(t0, b * SEQ), min(t0 + rows, b * SEQ + 1 + NPATCH)
                    if lo < hi:
                        sp.dma_start(base[lo - t0:hi - t0, t, :], pos[lo - b * SEQ:hi - b * SEQ]).then_inc(base_in, 16)
                        nb += 1
            for b in range(2):
                sp.dma_start(clsT[b * SEQ % 128:b * SEQ % 128 + 1, b * SEQ // 128, :], cls_token).then_inc(base_in, 16)
            for p0 in (0, 32):
                sp.dma_start(bd32[p0:p0 + EXP, :], bd).then_inc(base_in, 16)
            sp.dma_start(bd32[96:97, :], sbd).then_inc(base_in, 16)
            assert nb + 5 == BASE_DMAS
            for j, (_, _, parts, _, _) in enumerate(jobs):
                if j >= 2:
                    sp.wait_ge(set_dve, q_at(f"lo{j - 2}"))
                for ps, rs_, src in parts:
                    sp.dma_start(view(j)[ps, rs_, :], src).then_inc(stage_in[j % 2], 16)

            def load_pixels(n):
                m = n if known(n) is not None else sp.snap(n)
                if known(n) is None or n > 1:
                    sp.wait_ge(dve_f, at(DVE[F], "o2", n - 2))
                elif n == 1:
                    sp.wait_ge(dve_p, at(DVE[P], f"x_lo{XPIECES - 1}", 0))
                sp.dma_start(xraw[:, :], pixels[m]).then_inc(pixels_in, 16)

            def load_txt(n):
                m = n if known(n) is not None else sp.snap(n)
                if known(n) is None or n > 0:
                    sp.wait_ge(dve_f, at(DVE[F], "h1_2", n - 1))
                for b, lo, hi in TXTS:
                    t, r = divmod(lo, 128)
                    t_lo = lo - b * SEQ - 1 - NPATCH
                    sp.dma_start(base[r:r + hi - lo, t, :], txt[m, b, t_lo:t_lo + hi - lo, :]).then_inc(txt_in, 16)

            def load_rows(n, j):
                if j == 0:
                    sp.wait_ge(act_t, at(ACTE[T], "wrow_c1", n))
                    sp.dma_start(wrow[:, :, :], wrow16[0:4, 0:PAIR]).then_inc(rows_in[0], 16)
                else:
                    e0 = 2 * j + 2
                    sp.wait_ge(wb_done, EXP * n + 2 * j)
                    sp.dma_start(wrow[:, e0 % 4:e0 % 4 + 2, :], wrow16[e0:e0 + 2, 0:PAIR]).then_inc(rows_in[j % 2], 16)

            def store(n, pp):
                m = n if known(n) is not None else sp.snap(n)
                sp.wait_ge(fin_done, 3 * n + 3)
                for t, (t0, rows) in enumerate(TILES):
                    sp.dma_start(out_rows[m, t0:t0 + rows, :], yout[0:rows, t, :]).then_inc(out_done, 16)

            def body(n, pp):
                load_rows(n, 0)
                if known(n) is None or n > 0:
                    store(n - 1, (pp + 1) % 2)
                if known(n) is None or n + 2 < PAIRS:
                    load_txt(n + 2)
                for j in range(1, 7):
                    load_rows(n, j)
                    if j == 5 and (known(n) is None or n + 3 < PAIRS):
                        load_pixels(n + 3)

            sp.wait_ge(set_dve, q_at("cls2"))
            load_pixels(0)
            load_txt(0)
            load_pixels(1)
            load_txt(1)
            load_pixels(2)
            body(0, 0)
            with sp.Fori(0, (PAIRS - 4) // 2) as i:
                for p in range(2):
                    body(2 * i + 1 + p, (1 + p) % 2)
            for n in range(PAIRS - 3, PAIRS):
                body(n, n % 2)
            store(PAIRS - 1, 1)
            sp.wait_ge(out_done, 16 * NT * PAIRS)

        @block.gpsimd
        def _(pool):
            fills = [(carried[:, :], 0.0), (half[:, :], -0.5), (wcat[:, :, :], 0.0), (wcat[:, :, 96:97], 1.0), (mrun[:, :, 0:1], -1e38),
                     (num[:, :, 0:1], 0.0), (den[:, :, 0:1], 0.0)]
            fills += [(m[:, :, 1:w], 1.0) for m, w in ((reset_g, GROUPS), (reset_e, EXP))]
            fills += [(m[:, :, 0:1], 0.0) for m in (reset_g, reset_e)]
            fills += [(xT[s][:, b * (SEQ + 1):b * (SEQ + 1) + 1], 0.0) for s in "AB" for b in range(2)]
            fills += [(m[p][:, PAIR:PADT], 0.0) for m in (XAh, XAl, XB) for p in range(2)]
            fills += [(m[ps, cs], 0.0) for m in (oh_B, ol_B) for ps, cs in ((slice(0, DB), slice(SEQ, PAIR)),
                                                                        (slice(DB, 128), slice(0, SEQ)))]
            assert len(fills) == SET_POOL
            for k, (ap, value) in enumerate(fills):
                if k:
                    pool.wait_ge(set_pool, k)
                pool.memset(ap, value).then_inc(set_pool, 1)
            pool.wait_ge(set_pool, SET_POOL)

            def step(name, n, p):
                if name[:4] == "rstd":
                    k, i = name[4:].split("_")
                    ts = TILE_GROUPS[int(i)]
                    rows, c = TILES[ts[-1]][1], slice(ts[0], ts[-1] + 1)
                    pool.wait_ge(dve_f, at(DVE[F], f"veps{k}_{i}", n))
                    pool.tensor_tensor(rstd[0:rows, c], veps[0:rows, c], half[0:rows, c], ALU.pow).then_inc(pool_f, 1)
                if name[:6] == "shares":
                    g = int(name[6])
                    if g == 0 and (known(n) is None or n >= 2):
                        pool.wait_ge(out_done, 16 * NT * (n - 1))
                    pool.wait_ge(act_f, at(ACTE[F], f"er{g}", n))
                    pool.tensor_tensor(ev[:, g, :], e2s[:, g, :], kvr["v"][:, g, :], ALU.mult).then_inc(pool_f, 1)
                    pool.tensor_tensor(z[:, g, :], e2[:, g, :], kvr["v"][:, g, :], ALU.mult).then_inc(pool_f, 1)

            def low_part(n, s, pp):
                S = 34 * n + s
                e, b = divmod(s, 2)
                pool.wait_ge(hi_done, S + 1)
                pool.tensor_tensor(a_lo[(pp + e) % 2][:, b * SEQ:(b + 1) * SEQ], a32[(34 * pp + s) % 4][:, :],
                                   a_hi[(pp + e) % 2][:, b * SEQ:(b + 1) * SEQ], ALU.subtract).then_inc(lo_done, 1)

            def broadcast(n, x, first):
                j = 0 if x < 4 else (x - 2) // 2
                count = (ROWS_EVEN if j % 2 == 0 else ROWS_ODD) * n + j // 2 + 1
                pool.wait_ge(rows_in[j % 2], 16 * count)
                if x >= 2 or not first:
                    pool.wait_ge(weighted, WB * n + 2 * (x - 1))
                if x or not first:
                    pool.wait_ge(carry_done, EXP * n + x)
                pool.tensor_tensor(carried[:, :], half[0:1, 0:1], half[0:1, 0:1], ALU.mult).then_inc(carry_done, 1)
                pool.partition_broadcast(wb[(x + 1) % 2][:, :], wrow[0:1, x % 4, :], 128).then_inc(wb_done, 1)

            def body(n, pp, first=False):
                for s in range(SLOTS):
                    e, b = divmod(s, 2)
                    for name, m, p in steps_of(POOL_PLAN, s, n, pp):
                        step(name, m, p)
                    if s > 0:
                        low_part(n, s - 1, pp)
                    if s == 2:
                        broadcast(n, 0, first)
                    if e > 0:
                        pool.wait_ge(wb_done, EXP * n + e)
                        pool.wait_ge(gated, 34 * n + s + 1)
                        pool.tensor_tensor(a32[(34 * pp + s) % 4][:, :], a32[(34 * pp + s) % 4][:, :],
                                           wb[e % 2][:, b * SEQ:(b + 1) * SEQ], ALU.mult).then_inc(weighted, 1)
                    if b == 1 and 0 < e < EXP:
                        broadcast(n, e, first)
                low_part(n, SLOTS - 1, pp)

            for st in range(SLOTS):
                for name, m, p in steps_of({k: " ".join(i for i in v.split() if i[0] == "P") for k, v in POOL_PLAN.items()}, st, -2, 0):
                    step(name, m, p)
            for st in range(SLOTS):
                for name, m, p in steps_of(POOL_PLAN, st, -1, 1):
                    step(name, m, p)
            body(0, 0, first=True)
            with pool.Fori(0, (PAIRS - 4) // 2) as i:
                for p in range(2):
                    body(2 * i + 1 + p, (1 + p) % 2)
            for n in range(PAIRS - 3, PAIRS):
                body(n, n % 2)

        @block.scalar
        def _(act):
            act.wait_ge(consts_in, 16 * 6)
            act.activation(decay[:, :], par[:, PD:PD + 3], ACT.Exp).then_inc(set_act, 1)
            act.wait_ge(set_pool, SET_POOL)

            def step(name, n, p):
                later = known(n) is None or n > 0
                if name[:4] == "x_hi":
                    i = int(name[4])
                    if i == 0:
                        act.wait_ge(pixels_in, 16 * n + 16)
                        if later:
                            act.wait_ge(pe_p, at(PE[P], "patch2", n - 1))
                    c = slice(i * XPC, (i + 1) * XPC)
                    act.activation(x_hi[:, :, :].rearrange("p a b -> p (a b)")[:, c], xraw[:, c], ACT.Copy).then_inc(act_p, 1)
                if name[:7] == "turned1":
                    i = int(name[8])
                    act.wait_ge(pe_f, at(PE[F], f"turn1_{i}", n))
                    if later:
                        act.wait_ge(dve_f, at(DVE[F], "v_mB", n - 1))
                    for s, lo, hi, col in TURNS[i]:
                        for tok, c, ln in split_at_batch(lo, hi):
                            act.activation(xT[s][:, c:c + ln], bank(f"turn1_{i}")[:, col + tok - lo:col + tok - lo + ln],
                                           ACT.Copy).then_inc(act_f, 1)
                if name[:4] == "high":
                    q = name[4]
                    qi = "krv".index(q)
                    for s, dst in (("A", mixh[qi % 2]), ("B", mixB[qi % 2])):
                        act.wait_ge(dve_f, at(DVE[F], f"{q}_m{s}", n))
                        if s == "A" and (qi == 2 or later):
                            act.wait_ge(pe_f, at(PE[F], {0: "v2", 1: "r2", 2: "k2"}[qi], n if qi == 2 else n - 1))
                        act.activation(dst[:, :], mix32[s][:, :], ACT.Copy).then_inc(act_f, 1)
                if name[0] in "kvr" and len(name) == 2:
                    q, g = name[0], int(name[1])
                    act.wait_ge(pe_f, at(PE[F], name, n))
                    if later and g == 0:
                        act.wait_ge(dve_f, at(DVE[F], "o2", n - 1))
                    act.activation(kvr[q][:, g, :], bank(name)[:, 0:SEQ], ACT.Copy).then_inc(act_f, 1)
                if name[:4] == "relu":
                    g = int(name[4])
                    act.wait_ge(dve_f, at(DVE[F], f"z{g}", n))
                    if later and g == 0:
                        act.wait_ge(dve_p, at(DVE[P], f"x_lo{XPIECES - 1}", n + 1 if known(n) is None else min(n + 1, PAIRS - 1)))
                    elif g == 0:
                        act.wait_ge(dve_p, at(DVE[P], f"x_lo{XPIECES - 1}", 1))
                    act.activation(zp[:, g, :], z[:, g, :], ACT.Relu).then_inc(act_f, 1)
                    act.activation(zn[:, g, :], z[:, g, :], ACT.Relu, scale=-1.0).then_inc(act_f, 1)
                    act.activation(qp[:, g, :], z[:, g, :], ACT.Relu, bias=wplusu[:, g:g + 1]).then_inc(act_f, 1)
                    act.activation(qn[:, g, :], z[:, g, :], ACT.Relu, bias=minusc[:, g:g + 1], scale=-1.0).then_inc(act_f, 1)
                if name[:4] == "exps":
                    g = int(name[4])
                    act.wait_ge(act_f, at(ACTE[F], f"qn{g}", n))
                    for e_ in (e1s, e2s, e1, e2):
                        act.activation(e_[:, g, :], e_[:, g, :], ACT.Exp, scale=-1.0).then_inc(act_f, 1)
                    act.activation(kvr["r"][:, g, :], kvr["r"][:, g, :], ACT.Exp, scale=-1.0).then_inc(act_f, 1)
                if name == "ohigh":
                    act.wait_ge(dve_f, at(DVE[F], "o2", n))
                    if later:
                        act.wait_ge(pe_f, at(PE[F], "proj2", n - 1))
                    act.activation(oh_A[:, :].rearrange("p (b t) -> p b t", b=2), ev[:, 0:2, :], ACT.Copy).then_inc(act_f, 1)
                    for b in range(2):
                        ps, cs = slice(b * DB, (b + 1) * DB), slice(b * SEQ, (b + 1) * SEQ)
                        act.activation(oh_B[ps, cs], ev[ps, 2, :], ACT.Copy).then_inc(act_f, 1)
                if name[:7] == "turned2":
                    i = int(name[8])
                    act.wait_ge(pe_f, at(PE[F], f"turn2_{i}", n))
                    for s, lo, hi, col in TURNS[i]:
                        dst = XAh[p] if s == "A" else XB[p]
                        act.activation(dst[:, lo:hi], bank(f"turn2_{i}")[:, col:col + hi - lo], ACT.Copy).then_inc(act_f, 1)
                if name == "softmax":
                    act.wait_ge(dve_f, at(DVE[F], "lsh", n))
                    act.activation(ex[:, :, :], lg[:, :, :], ACT.Exp).then_inc(act_f, 1)
                if name[:6] == "wrow_c":
                    i = int(name[6])
                    c0, c1 = ((0, 512), (512, PADT))[i]
                    act.wait_ge(pe_t, at(PE[T], f"wrow{i}", n))
                    if later and i == 0:
                        act.wait_ge(rows_in[0], 16 * ROWS_EVEN * n)
                        act.wait_ge(rows_in[1], 16 * ROWS_ODD * n)
                        act.wait_ge(wb_done, EXP * n)
                    act.activation(wrow16[:, c0:c1], bank(f"wrow{i}")[0:EXP, 0:c1 - c0], ACT.Copy).then_inc(act_t, 1)
                if name == "wcol_c":
                    act.wait_ge(pe_t, at(PE[T], "wcol", n))
                    act.activation(wT[p][:, :], bank("wcol").bitcast(F16)[:, 0:PADT], ACT.Copy).then_inc(act_t, 1)

            def high_part(n, s, pp):
                S = 34 * n + s
                e, b = divmod(s, 2)
                if e > 0:
                    act.wait_ge(weighted, WB * n + s - 1)
                else:
                    act.wait_ge(gated, S + 1)
                if b == 0:
                    if e >= 2:
                        act.wait_ge(down_done, NX * n + e - 1)
                    elif type(n) is not int or n > 0:
                        act.wait_ge(down_done, NX * n + e - 1)
                act.activation(a_hi[(pp + e) % 2][:, b * SEQ:(b + 1) * SEQ], a32[(34 * pp + s) % 4][:, :], ACT.Copy)\
                   .then_inc(hi_done, 1)

            def body(n, pp):
                for s in range(SLOTS):
                    S = 34 * n + s
                    e = s // 2
                    for name, m, p in steps_of(ACT_PLAN, s, n, pp):
                        step(name, m, p)
                    act.wait_ge(up_ready, S + 1)
                    if s >= 2 or known(n) is None or n > 0:
                        act.wait_ge(gated, S - 1)
                    act.activation(silu[s % 2][:, :], ups[:, s % 2, 0:SEQ], ACT.Silu, bias=par[:, PBU + e:PBU + e + 1])\
                       .then_inc(silu_done, 1)
                    if s > 0:
                        high_part(n, s - 1, pp)
                high_part(n, SLOTS - 1, pp)

            for st in range(SLOTS):
                for name, m, p in steps_of({k: " ".join(i for i in v.split() if i[0] == "P") for k, v in ACT_PLAN.items()}, st, -2, 0):
                    step(name, m, p)
            for st in range(SLOTS):
                for name, m, p in steps_of(ACT_PLAN, st, -1, 1):
                    step(name, m, p)
            body(0, 0)
            with act.Fori(0, (PAIRS - 4) // 2) as i:
                for p in range(2):
                    body(2 * i + 1 + p, (1 + p) % 2)
            for n in range(PAIRS - 3, PAIRS):
                body(n, n % 2)

        @block.vector
        def _(dve):
            dve.memset(settled[:, :], 0.0).then_inc(set_dve, 1)
            dve.memset(base[:, :, :], 0.0).then_inc(set_dve, 1)
            dve.memset(bd32[:, :], 0.0).then_inc(set_dve, 1)
            dve.memset(clsT[:, :, :], 0.0).then_inc(set_dve, 1)
            for c in ("Ah", "Al", "Bh", "Bl"):
                dve.memset(kvr_w[c][:, :, :], 0.0).then_inc(set_dve, 1)
            for j, (hi, lo, parts, rows, shape) in enumerate(jobs):
                dve.wait_ge(stage_in[j % 2], need[j])
                if j == 0:
                    dve.wait_ge(set_dve, q_at("z_BL"))
                dve.tensor_copy(hi, view(j)).then_inc(set_dve, 1)
                dve.wait_ge(set_dve, q_at(f"hi{j}"))
                dve.tensor_tensor(lo, view(j), hi, ALU.subtract).then_inc(set_dve, 1)
            dve.wait_ge(base_in, 16 * BASE_DMAS)
            dve.tensor_copy(bd_h[:, :], bd32[:, :]).then_inc(set_dve, 1)
            dve.wait_ge(set_dve, q_at("bdhi"))
            dve.tensor_tensor(bd_l[:, :], bd32[:, :], bd_h[:, :], ALU.subtract).then_inc(set_dve, 1)
            for t in (0, SEQ // 128):
                dve.tensor_tensor(base[:, t, :], base[:, t, :], clsT[:, t, :], ALU.add).then_inc(set_dve, 1)
            dve.wait_ge(set_act, 1)
            dve.tensor_scalar(negw[:, :], decay[:, :], -1.0, None, ALU.mult).then_inc(set_dve, 1)
            dve.wait_ge(set_dve, q_at("negw"))
            dve.tensor_tensor(wplusu[:, :], negw[:, :], par[:, PU:PU + 3], ALU.add).then_inc(set_dve, 1)
            dve.wait_ge(set_dve, q_at("wplusu"))
            dve.tensor_scalar(minusc[:, :], wplusu[:, :], -1.0, None, ALU.mult).then_inc(set_dve, 1)
            dve.memset(wfull[:, :, :], 1.0).then_inc(set_dve, 1)
            dve.wait_ge(set_dve, q_at("onesq"))
            for g in range(3):
                dve.tensor_scalar(wfull[:, g, :], wfull[:, g, :], negw[:, g:g + 1], None, ALU.mult).then_inc(set_dve, 1)
            dve.wait_ge(set_dve, len(SET_DVE))
            dve.wait_ge(set_pool, SET_POOL)

            def after(name, n):
                dve.wait_ge(dve_f, at(DVE[F], name, n))

            def after_t(name, n):
                dve.wait_ge(dve_t, at(DVE[T], name, n))

            def select4(x, thr, top, gt, eq, cnt, need_, cum, reset, w, names, n, done, after):
                bc = [128, NT, w]
                dve.tensor_copy(rs[thr][:, :], top[:, :, TOPK - 1]).then_inc(done, 1)
                after(names + "thr", n)
                tb = rs[thr][:, :].unsqueeze(2).to_broadcast(bc)
                dve.tensor_tensor(gt[:, :, :], x[:, :, :], tb, ALU.is_gt).then_inc(done, 1)
                dve.tensor_tensor(eq[:, :, :], x[:, :, :], tb, ALU.is_equal).then_inc(done, 1)
                after(names + "gt", n)
                dve.tensor_reduce(rs[cnt][:, :], gt[:, :, :], AX_X, ALU.add).then_inc(done, 1)
                after(names + "cnt", n)
                dve.tensor_scalar(rs[need_][:, :], rs[cnt][:, :], -1.0, float(TOPK), ALU.mult, ALU.add).then_inc(done, 1)
                dve.tensor_tensor_scan(cum[:, :, :].rearrange("p a b -> p (a b)"), reset[:, :, :].rearrange("p a b -> p (a b)"),
                                       eq[:, :, :].rearrange("p a b -> p (a b)"), 0.0, ALU.mult, ALU.add).then_inc(done, 1)
                after(names + "cum", n)
                dve.tensor_tensor(cum[:, :, :], cum[:, :, :], rs[need_][:, :].unsqueeze(2).to_broadcast(bc), ALU.is_le)\
                   .then_inc(done, 1)
                after(names + "le", n)
                dve.tensor_tensor(eq[:, :, :], cum[:, :, :], eq[:, :, :], ALU.mult).then_inc(done, 1)
                after(names + "and", n)
                dve.tensor_tensor(gt[:, :, :], gt[:, :, :], eq[:, :, :], ALU.add).then_inc(done, 1)
                after(names + "sel", n)

            def step(name, n, p):
                later = known(n) is None or n > 0
                two = lambda m: m[:, :].rearrange("p (b t) -> p b t", b=2)
                flat_x = lambda m: m[:, :, :].rearrange("p a b -> p (a b)")
                if name[:4] == "x_lo":
                    i = int(name[4])
                    c = slice(i * XPC, (i + 1) * XPC)
                    dve.wait_ge(act_p, at(ACTE[P], f"x_hi{i}", n))
                    dve.tensor_tensor(flat_x(x_lo)[:, c], xraw[:, c], flat_x(x_hi)[:, c], ALU.subtract).then_inc(dve_p, 1)
                if name[0] == "y":
                    i = int(name[1])
                    rows = YT[i][1]
                    dve.wait_ge(pe_p, at(PE[P], f"patch{i}", n))
                    dve.tensor_copy(y_hi[0:rows, i, :], bank(f"patch{i}")[0:rows, 0:D]).then_inc(dve_p, 1)
                    dve.wait_ge(dve_p, at(DVE[P], f"y_hi{i}", n))
                    dve.tensor_tensor(y_lo[0:rows, i, :], bank(f"patch{i}")[0:rows, 0:D], y_hi[0:rows, i, :], ALU.subtract)\
                       .then_inc(dve_p, 1)
                if name[:3] == "sum":
                    k, i = int(name[3]), int(name[5])
                    ts = TILE_GROUPS[i]
                    rows, c = TILES[ts[-1]][1], slice(ts[0], ts[-1] + 1)
                    use = ("expand", "proj")[k - 1] + str(i)
                    src = bank(use)[0:rows, 0:len(ts) * D].rearrange("p (t d) -> p t d", t=len(ts))
                    dve.wait_ge(pe_f, at(PE[F], use, n))
                    if k == 1:
                        dve.wait_ge(txt_in, 16 * len(TXTS) * n + 16 * len(TXTS))
                        if i == 0 and (known(n) is None or n >= 2):
                            dve.wait_ge(fin_done, 3 * (n - 1))
                    addend = base if k == 1 else h[p]
                    dve.tensor_tensor(h[p][0:rows, c, :], src, addend[0:rows, c, :], ALU.add).then_inc(dve_f, 1)
                    after(f"h{k}_{i}", n)
                    for t in ts:
                        dve.bn_stats(stats[0:rows, t, :], h[p][0:rows, t, :]).then_inc(dve_f, 1)
                    after(f"stats{k}_{ts[-1]}", n)
                    dve.tensor_copy(settled[0:1, 0:1], settled[0:1, 1:2]).then_inc(dve_f, 1)
                    for t in ts:
                        dve.bn_aggr(mv[0:rows, t, :], stats[0:rows, t, :]).then_inc(dve_f, 1)
                    after(f"aggr{k}_{ts[-1]}", n)
                    dve.tensor_scalar(veps[0:rows, c], mv[0:rows, c, 1], EPS, None, ALU.add).then_inc(dve_f, 1)
                if name[:4] == "norm":
                    k, i = int(name[4]), int(name[6])
                    dve.wait_ge(pool_f, at(POOL[F], f"rstd{k}_{i}", n))
                    for t in TILE_GROUPS[i]:
                        rows = TILES[t][1]
                        for dst, src in ((slice(0, D), slice(0, D)), (slice(D, 256), slice(DA, D))):
                            dve.tensor_scalar(xn[0:rows, t, dst], h[p][0:rows, t, src], mv[0:rows, t, 0:1], rstd[0:rows, t:t + 1],
                                              ALU.subtract, ALU.mult).then_inc(dve_f, 1)
                shifted = {s: xT[s][:, :].rearrange("p (b t) -> p b t", b=2) for s in "AB"}
                if name == "diff":
                    for s in "AB":
                        dve.wait_ge(act_f, at(ACTE[F], f"xT_{s}2", n))
                        dve.tensor_tensor(two(dT[s]), shifted[s][:, :, 1:SEQ + 1], shifted[s][:, :, 0:SEQ], ALU.subtract)\
                           .then_inc(dve_f, 1)
                if name[:3] == "mix":
                    q = name[3]
                    after("dB" if q == "k" else {"r": "k_loB", "v": "r_loB"}[q], n)
                    for si, s in enumerate("AB"):
                        col = PM + 2 * "kvr".index(q) + si
                        dve.scalar_tensor_tensor(out=two(mix32[s]), in0=two(dT[s]), scalar=par[:, col:col + 1],
                                                 in1=shifted[s][:, :, 0:SEQ], op0=ALU.mult, op1=ALU.add).then_inc(dve_f, 1)
                if name[:3] == "low":
                    q = name[3]
                    qi = "krv".index(q)
                    dve.wait_ge(act_f, at(ACTE[F], f"{q}_hiA", n))
                    dve.tensor_tensor(mixl[qi % 2][:, :], mix32["A"][:, :], mixh[qi % 2][:, :], ALU.subtract).then_inc(dve_f, 1)
                    dve.wait_ge(act_f, at(ACTE[F], f"{q}_hiB", n))
                    dve.tensor_tensor(mixB[qi % 2][DB:128, :], mix32["B"][DB:128, :], mixB[qi % 2][DB:128, :], ALU.subtract)\
                       .then_inc(dve_f, 1)
                if name[:3] == "run":
                    g = int(name[3])
                    dve.wait_ge(act_f, at(ACTE[F], f"k{g}", n))
                    dve.tensor_tensor_scan(mrun[:, g, 1:SEQ + 1], wfull[:, g, :], kvr["k"][:, g, :], -1e38, ALU.add, ALU.max)\
                       .then_inc(dve_f, 1)
                    after(f"m{g}", n)
                    dve.scalar_tensor_tensor(out=z[:, g, :], in0=kvr["k"][:, g, :], scalar=negw[:, g:g + 1],
                                             in1=mrun[:, g, 0:SEQ], op0=ALU.subtract, op1=ALU.subtract).then_inc(dve_f, 1)
                if name[:5] == "scanA":
                    g = int(name[5])
                    dve.wait_ge(pool_f, at(POOL[F], f"t2{g}", n))
                    dve.tensor_tensor_scan(num[:, g, 1:SEQ + 1], e1s[:, g, :], ev[:, g, :], 0.0, ALU.mult, ALU.add)\
                       .then_inc(dve_f, 1)
                    dve.tensor_tensor_scan(den[:, g, 1:SEQ + 1], e1s[:, g, :], e2s[:, g, :], 0.0, ALU.mult, ALU.add)\
                       .then_inc(dve_f, 1)
                    after(f"num{g}", n)
                    dve.tensor_tensor(ev[:, g, :], e1[:, g, :], num[:, g, 0:SEQ], ALU.mult).then_inc(dve_f, 1)
                    after(f"t1{g}", n)
                    dve.tensor_tensor(ev[:, g, :], ev[:, g, :], z[:, g, :], ALU.add).then_inc(dve_f, 1)
                if name[:5] == "scanB":
                    g = int(name[5])
                    after(f"den{g}", n)
                    dve.tensor_tensor(e1s[:, g, :], e1[:, g, :], den[:, g, 0:SEQ], ALU.mult).then_inc(dve_f, 1)
                    after(f"d1{g}", n)
                    dve.tensor_tensor(e1s[:, g, :], e1s[:, g, :], e2[:, g, :], ALU.add).then_inc(dve_f, 1)
                    after(f"d2{g}", n)
                    dve.scalar_tensor_tensor(out=e1s[:, g, :], in0=kvr["r"][:, g, :], scalar=1.0, in1=e1s[:, g, :],
                                             op0=ALU.add, op1=ALU.mult).then_inc(dve_f, 1)
                    after(f"d3{g}", n)
                    dve.reciprocal(e1s[:, g, 0:SEQ // 2], e1s[:, g, 0:SEQ // 2]).then_inc(dve_f, 1)
                if name[:5] == "scanC":
                    g = int(name[5])
                    dve.reciprocal(e1s[:, g, SEQ // 2:SEQ], e1s[:, g, SEQ // 2:SEQ]).then_inc(dve_f, 1)
                    after(f"recB{g}", n)
                    dve.tensor_tensor(ev[:, g, :], ev[:, g, :], e1s[:, g, :], ALU.mult).then_inc(dve_f, 1)
                if name == "olow":
                    dve.wait_ge(act_f, at(ACTE[F], "o_hiA", n))
                    dve.tensor_tensor(two(ol_A), ev[:, 0:2, :], two(oh_A), ALU.subtract).then_inc(dve_f, 1)
                    for b in range(2):
                        ps, cs = slice(b * DB, (b + 1) * DB), slice(b * SEQ, (b + 1) * SEQ)
                        dve.wait_ge(act_f, at(ACTE[F], f"o_hiB{b}", n))
                        dve.tensor_tensor(ol_B[ps, cs], ev[ps, 2, :], oh_B[ps, cs], ALU.subtract).then_inc(dve_f, 1)
                if name[:4] == "xlow":
                    i = int(name[4])
                    dve.wait_ge(act_f, at(ACTE[F], ("X_hA0", "X_hB0", "X_hB1")[i], n))
                    ps_ = bank(f"turn2_{i}")
                    for s, lo, hi, col in TURNS[i]:
                        if s == "A":
                            dve.tensor_tensor(XAl[p][:, lo:hi], ps_[:, col:col + hi - lo], XAh[p][:, lo:hi], ALU.subtract)\
                               .then_inc(dve_f, 1)
                        else:
                            dve.tensor_tensor(XB[p][DB:128, lo:hi], ps_[DB:128, col:col + hi - lo], XB[p][DB:128, lo:hi],
                                              ALU.subtract).then_inc(dve_f, 1)
                bc = [128, NT, EXP]
                all_t = lambda m: m[:, :].unsqueeze(1).to_broadcast(bc)
                per_t = lambda m: rs[m][:, :].unsqueeze(2).to_broadcast(bc)
                flat = lambda m: m[:, :, :].rearrange("p t g -> p (t g)").unsqueeze(2).to_broadcast([128, NT * GROUPS, 2])
                f2 = lambda m: m[:, :, :].rearrange("p t (g k) -> p (t g) k", k=2)
                if name == "route1":
                    dve.wait_ge(pe_f, at(PE[F], "logits", n))
                    dve.tensor_tensor(lg[:, :, :], bank("logits")[:, 0:NT * EXP].rearrange("p (t e) -> p t e", t=NT), all_t(gb_bc), ALU.add)\
                       .then_inc(dve_f, 1)
                    after("lg", n)
                    dve.tensor_reduce(rs["lmax"][:, :], lg[:, :, :], AX_X, ALU.max).then_inc(dve_f, 1)
                    after("lmax", n)
                    dve.tensor_tensor(lg[:, :, :], lg[:, :, :], per_t("lmax"), ALU.subtract).then_inc(dve_f, 1)
                    dve.wait_ge(act_f, at(ACTE[F], "softmax", n))
                    dve.tensor_reduce(rs["lsum"][:, :], ex[:, :, :], AX_X, ALU.add).then_inc(dve_f, 1)
                    after("lsum", n)
                    dve.reciprocal(rs["lrec"][:, :], rs["lsum"][:, :]).then_inc(dve_f, 1)
                    after("lrec", n)
                    dve.tensor_tensor(score[:, :, :], ex[:, :, :], per_t("lrec"), ALU.mult).then_inc(dve_f, 1)
                    after("score", n)
                    dve.tensor_tensor(biased[:, :, :], score[:, :, :], all_t(bias_bc), ALU.add).then_inc(dve_f, 1)
                    after("biased", n)
                    pairs = biased[:, :, :].rearrange("p t (g k) -> p t g k", k=2)
                    dve.tensor_tensor(gsum[:, :, :], pairs[:, :, :, 0], pairs[:, :, :, 1], ALU.add).then_inc(dve_f, 1)
                if name == "route2":
                    after("gsum", n)
                    dve.tensor_copy(settled[0:1, 0:1], settled[0:1, 1:2]).then_inc(dve_f, 1)
                    for t in range(NT):
                        dve.max(gtop[:, t, :], gsum[:, t, :]).then_inc(dve_f, 1)
                    after(f"gtop{NT - 1}", n)
                    select4(gsum, "gthr", gtop, ggt, geq, "gcnt", "gneed", gcum, reset_g, GROUPS, "g", n, dve_f, after)
                    dve.tensor_scalar(gbig[:, :, :], ggt[:, :, :], 1e30, -1e30, ALU.mult, ALU.add).then_inc(dve_f, 1)
                    dve.tensor_tensor(f2(masked), f2(biased), flat(ggt), ALU.mult).then_inc(dve_f, 1)
                    after("masked", n)
                    dve.tensor_tensor(f2(masked), f2(masked), flat(gbig), ALU.add).then_inc(dve_f, 1)
                if name == "route3":
                    after("masked2", n)
                    dve.tensor_copy(settled[0:1, 0:1], settled[0:1, 1:2]).then_inc(dve_t, 1)
                    for t in range(NT):
                        dve.max(etop[:, t, :], masked[:, t, :]).then_inc(dve_t, 1)
                    after_t(f"etop{NT - 1}", n)
                    select4(masked, "ethr", etop, egt, eeq, "ecnt", "eneed", ecum, reset_e, EXP, "e", n, dve_t, after_t)
                    dve.scalar_tensor_tensor(out=wfl[:, :, :], in0=score[:, :, :], scalar=SCALE, in1=egt[:, :, :],
                                             op0=ALU.mult, op1=ALU.mult).then_inc(dve_t, 1)
                    after_t("wfull", n)
                    dve.tensor_copy(wcat[:, :, 0:EXP], wfl[:, :, :]).then_inc(dve_t, 1)
                    after_t("w_hi", n)
                    dve.tensor_tensor(wcat[:, :, 32:32 + EXP], wfl[:, :, :], wcat[:, :, 0:EXP], ALU.subtract).then_inc(dve_t, 1)


            def finish(n, pp):
                if known(n) is None or n > 0:
                    dve.wait_ge(out_done, 16 * NT * n)
                dve.wait_ge(dve_f, at(DVE[F], "o_loB1", n + 1 if known(n) is None else min(n + 1, PAIRS - 1)))
                dve.wait_ge(down_done, NX * n + NX)
                for i, ts in enumerate(TILE_GROUPS):
                    rows, c = TILES[ts[-1]][1], slice(ts[0], ts[-1] + 1)
                    src = ysum[0:rows, ts[0] * D:(ts[-1] + 1) * D].rearrange("p (t d) -> p t d", t=len(ts))
                    dve.tensor_tensor(yout[0:rows, c, :], src, h[pp][0:rows, c, :], ALU.add).then_inc(fin_done, 1)

            def body(n, pp, first=False):
                for s in range(SLOTS):
                    S = 34 * n + s
                    e = s // 2
                    for name, m, p in steps_of(DVE_PLAN, s, n, pp):
                        step(name, m, p)
                    dve.wait_ge(silu_done, S + 1)
                    dve.wait_ge(gate_ready, S + 1)
                    if s >= 4 or not first:
                        dve.wait_ge(lo_done, S - 3)
                    dve.scalar_tensor_tensor(out=a32[(34 * pp + s) % 4][:, :], in0=gts[:, s % 2, 0:SEQ],
                                             scalar=par[:, PBG + e:PBG + e + 1], in1=silu[s % 2][:, :],
                                             op0=ALU.add, op1=ALU.mult).then_inc(gated, 1)
                    if s == 1 and not first:
                        finish(n - 1, (pp + 1) % 2)

            for st in range(SLOTS):
                for name, m, p in steps_of({k: " ".join(i for i in v.split() if i[0] == "P") for k, v in DVE_PLAN.items()}, st, -2, 0):
                    step(name, m, p)
            for st in range(SLOTS):
                for name, m, p in steps_of(DVE_PLAN, st, -1, 1):
                    step(name, m, p)
            body(0, 0, first=True)
            with dve.Fori(0, (PAIRS - 4) // 2) as i:
                for p in range(2):
                    body(2 * i + 1 + p, (1 + p) % 2)
            for n in range(PAIRS - 3, PAIRS):
                body(n, n % 2)
            finish(PAIRS - 1, 1)

        @block.tensor
        def _(pe):
            pe.wait_ge(set_dve, len(SET_DVE))
            pe.wait_ge(set_pool, SET_POOL)

            def free(name, n):
                k = [u[1] for u in USES].index(name)
                body_n = n - LANES[USES[k][0]]
                k -= 2
                while True:
                    lane, use = USES[k]
                    m = (body_n if k >= 0 else body_n - 1) + LANES[lane]
                    if known(n) is None or 0 <= m < PAIRS:
                        break
                    if k < -len(USES) + 2:
                        return
                    k -= 2
                who, last = READER[use]
                if who == "act":
                    pe.wait_ge({T: act_t, F: act_f}[lane], at(ACTE[lane], last, m))
                else:
                    pe.wait_ge({F: dve_f, P: dve_p}[lane], at(DVE[lane], last, m))

            def chain(dst, terms, skip=False):
                for i, (lhsT, rhs) in enumerate(terms):
                    mm = pe.matmul(dst, lhsT, rhs, start=(i == 0), stop=(i == len(terms) - 1))
                return mm

            def step(name, n, p):
                out_ps = bank(name)
                free(name, n)
                if name[:5] == "patch":
                    i = int(name[5])
                    cs = slice(YT[i][0], YT[i][0] + YT[i][1])
                    pe.wait_ge(dve_p, at(DVE[P], f"x_lo{XPIECES - 1}", n))
                    chain(out_ps[0:YT[i][1], 0:D], [(x[:, c, cs], w[:, c, :]) for c in range(KC) for x, w in
                                                    ((x_hi, patch_hi), (x_lo, patch_hi), (x_hi, patch_lo))]).then_inc(pe_p, 1)
                if name[:6] == "expand":
                    i = int(name[6])
                    pe.wait_ge(dve_p, at(DVE[P], "y_lo2", n))
                    for j, t in enumerate(TILE_GROUPS[i]):
                        t0, rows = TILES[t]
                        terms = [(sel[0:YT[k][1], k, t0:t0 + rows], y[0:YT[k][1], k, :]) for k in SELECTED[t] for y in (y_hi, y_lo)]
                        for m, (a, b_) in enumerate(terms):
                            mm = pe.matmul(out_ps[0:rows, j * D:(j + 1) * D], a, b_, start=(j == 0 and m == 0),
                                           stop=(m == len(terms) - 1), skip_group_check=True)
                    mm.then_inc(pe_f, 1)
                if name[:4] == "turn":
                    k, i = int(name[4]), int(name[6])
                    pe.wait_ge(dve_f, at(DVE[F], f"xd{k}_{(3, 4, 4)[i]}", n))
                    for s, lo, hi, col in TURNS[i]:
                        for t, (t0, rows) in enumerate(TILES):
                            if lo <= t0 < hi:
                                cs = slice(0, DA) if s == "A" else slice(DA, 256)
                                mm = pe.transpose(out_ps[:, col + t0 - lo:col + t0 - lo + rows], xn[0:rows, t, cs],
                                                  id32[0:rows, 0:rows])
                    mm.then_inc(pe_f, 1)
                if name[0] in "kvr" and len(name) == 2:
                    q, g = name[0], int(name[1])
                    qb = "krv".index(q) % 2
                    pe.wait_ge(dve_f, at(DVE[F], f"{q}_loB", n))
                    W = {s: kvr_w[s][:, "kvr".index(q), :] for s in kvr_w}

                    def terms(b, c0):
                        ws, cs = slice(c0, c0 + 128), slice(b * SEQ, (b + 1) * SEQ)
                        mh, ml, mb = mixh[qb][:, cs], mixl[qb][:, cs], mixB[qb][:, cs]
                        return [(W["Ah"][:, ws], mh), (W["Ah"][:, ws], ml), (W["Al"][:, ws], mh),
                                (W["Bh"][:, ws], mb), (W["Bl"][:, ws], mb)]
                    both = terms(g, 0) if g < 2 else terms(0, DA + DB) + terms(1, DA)
                    chain(out_ps[:, 0:SEQ], both).then_inc(pe_f, 1)
                if name[:4] == "proj":
                    i = int(name[4])
                    pe.wait_ge(dve_f, at(DVE[F], "o_loB1", n))
                    for j, t in enumerate(TILE_GROUPS[i]):
                        t0, rows = TILES[t]
                        cs = slice(t0, t0 + rows)
                        terms_ = [(oh_A[:, cs], wo_w["Ah"]), (ol_A[:, cs], wo_w["Ah"]), (oh_A[:, cs], wo_w["Al"]),
                                  (oh_B[:, cs], wo_w["Bh"]), (ol_B[:, cs], wo_w["Bh"]), (oh_B[:, cs], wo_w["Bl"])]
                        for m, (a, b_) in enumerate(terms_):
                            mm = pe.matmul(out_ps[0:rows, j * D:(j + 1) * D], a, b_[:, :], start=(j == 0 and m == 0),
                                           stop=(m == 5), skip_group_check=True)
                    mm.then_inc(pe_f, 1)
                if name == "logits":
                    pe.wait_ge(dve_f, at(DVE[F], "X_lB1", n))
                    for t in range(NT):
                        cs = slice(t * 128, (t + 1) * 128)
                        terms_ = [(XAh[p][:, cs], gw_w["Ah"]), (XAl[p][:, cs], gw_w["Ah"]), (XAh[p][:, cs], gw_w["Al"]),
                                  (XB[p][:, cs], gw_w["Bh"]), (XB[p][:, cs], gw_w["Bl"])]
                        for m, (a, b_) in enumerate(terms_):
                            mm = pe.matmul(out_ps[:, t * EXP:(t + 1) * EXP], a, b_[:, :], start=(t == 0 and m == 0),
                                           stop=(m == 4), skip_group_check=True)
                    mm.then_inc(pe_f, 1)
                if name[:4] == "wrow":
                    i = int(name[4])
                    ts = (range(4), range(4, NT))[i]
                    pe.wait_ge(dve_t, at(DVE[T], "w_lo", n))
                    for t in ts:
                        mm = pe.transpose(out_ps[0:EXP, (t - ts[0]) * 128:(t - ts[0] + 1) * 128], wfl[:, t, :], id32[:, :])
                    mm.then_inc(pe_t, 1)
                if name == "wcol":
                    for t in range(NT):
                        mm = pe.transpose(out_ps.bitcast(F16)[:, t * 128:(t + 1) * 128], wcat[:, t, :], id16[:, :])
                    mm.then_inc(pe_t, 1)

            def down(n, e, pp):
                pe.wait_ge(lo_done, 34 * n + 2 * e + 2)
                if e == 0 and (known(n) is None or n > 0):
                    pe.wait_ge(fin_done, 3 * n)
                if e == NX - 1:
                    pe.wait_ge(act_t, at(ACTE[T], "wcol_c", n))
                opened = set()
                for t, (t0, rows) in enumerate(TILES):
                    ah, al = a_hi[(pp + e) % 2][:, t0:t0 + rows], a_lo[(pp + e) % 2][:, t0:t0 + rows]
                    terms = [(ah, dn_h[:, e, :]), (ah, dn_l[:, e, :]), (al, dn_h[:, e, :])]
                    if e == NX - 1:
                        terms += [(wT[pp][:, t0:t0 + rows], bd_h[:, :]), (wT[pp][:, t0:t0 + rows], bd_l[:, :])]
                    for lhsT, w in terms:
                        for c0, c1 in cut_at_bank(t * D, (t + 1) * D):
                            mm = pe.matmul(ysum[0:rows, c0:c1], lhsT, w[:, c0 - t * D:c1 - t * D],
                                           start=(e == 0 and c0 // 512 not in opened), stop=(e == NX - 1), skip_group_check=True)
                            opened.add(c0 // 512)
                mm.then_inc(down_done, 1)

            def body(n, pp, first=False):
                for s in range(SLOTS):
                    e, b = divmod(s, 2)
                    S = 34 * n + s
                    cs = slice(b * SEQ, (b + 1) * SEQ)
                    for name, m, p in steps_of(PE_PLAN, s, n, pp):
                        step(name, m, p)
                    if s == 0:
                        pe.wait_ge(dve_f, at(DVE[F], "X_lB1", n))
                    x5 = (XAh[pp][:, cs], XAl[pp][:, cs], XAh[pp][:, cs], XB[pp][:, cs], XB[pp][:, cs])
                    if s >= 2 or not first:
                        pe.wait_ge(silu_done, S - 1)
                    chain(ups[:, s % 2, 0:SEQ], [(up_w[k][:, e, :], x) for k, x in zip(("Ah", "Ah", "Al", "Bh", "Bl"), x5)])\
                        .then_inc(up_ready, 1)
                    if s >= 2 or not first:
                        pe.wait_ge(gated, S - 1)
                    chain(gts[:, s % 2, 0:SEQ], [(gt_w[k][:, e, :], x) for k, x in zip(("Ah", "Ah", "Al", "Bh", "Bl"), x5)])\
                        .then_inc(gate_ready, 1)
                    if b == 1 and e > 0:
                        down(n, e - 1, pp)
                    if s == 0 and not first:
                        down(n - 1, NX - 1, (pp + 1) % 2)

            for st in range(SLOTS):
                for name, m, p in steps_of({k: " ".join(i for i in v.split() if i[0] == "P") for k, v in PE_PLAN.items()}, st, -2, 0):
                    step(name, m, p)
            for st in range(SLOTS):
                for name, m, p in steps_of(PE_PLAN, st, -1, 1):
                    step(name, m, p)
            body(0, 0, first=True)
            with pe.Fori(0, (PAIRS - 4) // 2) as i:
                for p in range(2):
                    body(2 * i + 1 + p, (1 + p) % 2)
            for n in range(PAIRS - 3, PAIRS):
                body(n, n % 2)
            down(PAIRS - 1, NX - 1, 1)


_OUTS = [((BATCH, SEQ, D), 'float32')]


def kernel(**inputs):
    import numpy as _np
    import concourse.bacc as _bacc
    from concourse import mybir as _mybir
    from concourse.bass_utils import run_bass_kernel_spmd as _run

    v = {k: _np.asarray(a) for k, a in inputs.items()}
    n = {k.replace("L0_tok_", "").replace("L0_attn_", "").replace("L0_ffn_", ""): a for k, a in v.items()}

    c = _np.array([[p[0] for p in tok] for tok in DISTINCT])
    step = _np.arange(WIN)
    r = _np.minimum(_np.array([[p[1] for p in tok] for tok in DISTINCT])[:, :, None] * STRIDE + step, IMG - 1)
    q = _np.minimum(_np.array([[p[2] for p in tok] for tok in DISTINCT])[:, :, None] * STRIDE + step, IMG - 1)
    win = n["x"][:, c[:, :, None, None], r[:, :, :, None], q[:, :, None, :]]
    pixels = win.reshape(PAIRS, 2, ND, KC, KP).transpose(0, 4, 3, 1, 2).reshape(PAIRS, KP, KC * PX)

    onehot = _np.zeros((YW, 3, PAIR), _np.float16)
    for b in range(2):
        for t in range(NPATCH):
            k, row = divmod(b * ND + WHICH[t], YW)
            onehot[row, k, b * SEQ + 1 + t] = 1

    def chan(a, parts):
        cols = [a[:DA]] * (parts - 1) + [_np.concatenate([a[DA:], a[DA:]])]
        return _np.stack(cols, 1)

    params = _np.concatenate(
        [chan(n["time_decay"], 3), chan(n["time_first"], 3), chan(n["mix_k"], 2), chan(n["mix_v"], 2), chan(n["mix_r"], 2),
         n["sbu"][:, None], n["bu"].T, n["sbg"][:, None], n["bg"].T], 1)
    arrays = {
        "pixels": pixels, "txt": n["txt"].reshape(PAIRS, 2, TXT, D), "pos": n["pos_embedding"], "cls_token": n["cls_token"][0],
        "patch_w": n["proj_w"].T.reshape(KC, KP, D).transpose(1, 0, 2),
        "wkvr": _np.stack([n["Wk"].T, n["Wv"].T, n["Wr"].T], 1), "wo": n["Wo"].T, "gate_w": n["gate_w"],
        "wu": n["Wu"], "wg": n["Wg"], "wd": n["Wd"], "swu": n["sWu"], "swg": n["sWg"], "swd": n["sWd"],
        "bd": n["bd"], "sbd": n["sbd"][None, :], "gate_b": n["gate_b"], "gate_bias": n["bias"], "params": params,
        "onehot": onehot, "ident32": _np.eye(128, dtype=_np.float32), "ident16": _np.eye(128, dtype=_np.float16),
    }
    nc = _bacc.Bacc("TRN2", target_bir_lowering=False, num_devices=1)
    feed, args = {}, {}
    for name, a in arrays.items():
        a = _np.ascontiguousarray(a)
        feed[f"in_{name}"] = a
        args[name] = nc.dram_tensor(f"in_{name}", a.shape, _mybir.dt.from_np(a.dtype), kind="ExternalInput").ap()
    args["out"] = nc.dram_tensor("out_0", _OUTS[0][0], _mybir.dt.from_np(_np.dtype(_OUTS[0][1])), kind="ExternalOutput").ap()
    build_fusion(nc, **args)
    res = _run(nc, [feed], core_ids=[0])
    return res.results[0]["out_0"]
```

```python
from contextlib import ExitStack

import concourse.bass as bass
from concourse import mybir

F32 = mybir.dt.float32
F16 = mybir.dt.float16
ALU = mybir.AluOpType
ACT = mybir.ActivationFunctionType
AX_X = mybir.AxisListType.X

BATCH, CH, IMG = 64, 3, 96
D = 192
DA, DB = 128, 64
GRID, STRIDE, WIN = 16, 13, 20
TXT = 32
NPATCH = GRID * GRID
SEQ = 1 + NPATCH + TXT
PAIR = 2 * SEQ
PAIRS = BATCH // 2
EXP, HID = 16, 128
NX = EXP + 1
GROUPS, TOPK = 8, 4
SCALE = 2.5
EPS = 1e-5
TILES = [(t * 128, min(128, PAIR - t * 128)) for t in range(-(-PAIR // 128))]
NT = len(TILES)
PADT = NT * 128
TILE_GROUPS = [(0, 1), (2, 3), (4,)]
KC, KP = 10, 120
SLOTS = 2 * NX


def token_patches(t):
    last = -(-(IMG - 1) // STRIDE)
    return tuple((p // NPATCH, min(p % NPATCH // GRID, last), min(p % GRID, last)) for p in range(3 * t, 3 * t + 3))


DISTINCT = []
for _t in range(NPATCH):
    if token_patches(_t) not in DISTINCT:
        DISTINCT.append(token_patches(_t))
ND = len(DISTINCT)
WHICH = [DISTINCT.index(token_patches(t)) for t in range(NPATCH)]
PX = 2 * ND
YW = -(-PX // 3)
YT = [(k * YW, min(YW, PX - k * YW)) for k in range(3)]
XPIECES = 5
XPC = KC * PX // XPIECES


def selected():
    out = []
    for t0, rows in TILES:
        ks = set()
        for tok in range(t0, t0 + rows):
            b, t = divmod(tok, SEQ)
            if 1 <= t <= NPATCH:
                ks.add((b * ND + WHICH[t - 1]) // YW)
        out.append(sorted(ks))
    return out


SELECTED = selected()


def split_at_batch(t0, t1):
    out = []
    for b in range(2):
        lo, hi = max(t0, b * SEQ), min(t1, (b + 1) * SEQ)
        if lo < hi:
            out.append((lo, lo + b + 1, hi - lo))
    return out


LANES = {"T": 0, "F": 1, "P": 2}
TURNS = [[("A", 0, 512, 0)], [("A", 512, PAIR, 0), ("B", 0, 384, PAIR - 512)], [("B", 384, PAIR, 0)]]
PE_PLAN = {1: "F.expand0", 2: "T.wrow0 T.wrow1", 3: "F.expand1", 4: "F.expand2", 6.5: "F.turn1_0", 7: "F.turn1_1",
           8: "F.turn1_2", 9: "T.wcol", 11: "F.k0 F.k1", 12: "F.k2", 13: "F.r0 F.r1", 14: "F.r2",
           15: "P.patch0 P.patch1 P.patch2", 16: "F.v0", 17: "F.v1", 18: "F.v2", 24.5: "F.proj0", 25: "F.proj1",
           26: "F.proj2", 29: "F.turn2_0 F.turn2_1", 30: "F.turn2_2", 31: "F.logits"}
ACT_PLAN = {1: "P.x_hi0", 2: "T.wrow_c0 T.wrow_c1", 3: "P.x_hi1 P.x_hi2", 4: "T.w_high P.x_hi3", 5: "P.x_hi4",
            7: "F.turned1_0 F.turned1_1", 8: "F.turned1_2", 9: "T.wcol_c F.highk", 11: "F.k0 F.k1 F.highr", 12: "F.k2 F.relu0",
            13: "F.r0 F.r1 F.relu1", 14: "F.r2 F.relu2",
            15: "F.exps0 F.highv F.exps1 F.exps2", 16: "F.v0", 17: "F.v1", 18: "F.v2", 21: "F.ohighA", 23: "F.ohighB",
            29: "F.turned2_0 F.turned2_1", 30: "F.turned2_2", 31: "F.softmax"}
DVE_PLAN = {0: "T.route3", 1: "F.sum1_0", 3: "F.sum1_1", 4: "F.norm1_0 F.sum1_2",
            5: "F.norm1_1 F.norm1_2", 6: "P.x_lo0 P.x_lo1 P.x_lo2", 7: "P.x_lo3", 8: "F.diff", 9: "F.mixk F.lowk",
            10: "F.mixr", 11: "F.lowr P.x_lo4", 12: "F.run0 F.run1", 13: "F.run2 F.mixv",
            15: "P.y0 F.div0 F.lowv P.y1 F.rec0 P.y2",
            16: "F.div1", 17: "F.rec1", 18: "F.quot0", 19: "F.div2", 20: "F.quot1", 21: "F.rec2", 22: "F.quot2",
            23: "F.olowA F.olowB", 25: "F.sum2_0 F.sum2_1", 26: "F.norm2_0 F.sum2_2", 27: "F.norm2_1 F.norm2_2",
            29: "F.xlow0 F.xlow1", 30: "F.xlow2", 31: "F.route1", 32: "F.route2"}
POOL_PLAN = {1: "F.rstd1_0", 3: "F.rstd1_1", 4: "F.rstd1_2", 6: "T.w_low", 17: "F.shares0", 18: "F.shares1", 19: "F.shares2",
             25: "F.rstd2_0 F.rstd2_1", 26: "F.rstd2_2"}


def choose_names(c):
    return [c + s for s in ("thr", "gt", "eq", "cnt", "need", "cum", "le", "and", "sel")]


PARTS = {"diff": ["dA", "dB"], "olowA": ["o_loA"], "olowB": ["o_loB0", "o_loB1"], "ohighA": ["o_hiA"],
         "ohighB": ["o_hiB0", "o_hiB1"],
         "route1": ["lg", "lmax", "lsh", "lsum", "lrec", "score", "biased", "gsum"],
         "route2": ["gsum_set"] + [f"gtop{t}" for t in range(NT)] + choose_names("g") + ["gbig", "masked", "masked2"],
         "route3": ["masked_set"] + [f"etop{t}" for t in range(NT)] + choose_names("e") + ["wfull"],
         "xlow0": ["X_lA0"], "xlow1": ["X_lA1", "X_lB0"], "xlow2": ["X_lB1"],
         "turned1_0": ["xT_A0", "xT_A1"], "turned1_1": ["xT_A2", "xT_B0", "xT_B1"], "turned1_2": ["xT_B2"],
         "turned2_0": ["X_hA0"], "turned2_1": ["X_hA1", "X_hB0"], "turned2_2": ["X_hB1"]}
for _g in range(3):
    PARTS[f"y{_g}"] = [f"y_hi{_g}", f"y_lo{_g}"]
    PARTS[f"run{_g}"] = [f"m{_g}", f"z{_g}"]
    PARTS[f"relu{_g}"] = [f"{v}{_g}" for v in ("zp", "zn", "qp", "qn")]
    PARTS[f"exps{_g}"] = [f"{v}{_g}" for v in ("e1s", "e2s", "e1", "e2", "er")]
    PARTS[f"shares{_g}"] = [f"ev{_g}", f"t2{_g}"]
    PARTS[f"div{_g}"] = [f"{v}{_g}" for v in ("den", "d1", "d2", "d3")]
    PARTS[f"quot{_g}"] = [f"{v}{_g}" for v in ("num", "t1", "t3", "o")]
    _ts = TILE_GROUPS[_g]
    for _k in (1, 2):
        PARTS[f"sum{_k}_{_g}"] = ([f"h{_k}_{_g}"] + [f"stats{_k}_{t}" for t in _ts] + [f"stats_set{_k}_{_g}"]
                                  + [f"aggr{_k}_{t}" for t in _ts] + [f"veps{_k}_{_g}"])
        PARTS[f"norm{_k}_{_g}"] = [f"{v}{_k}_{t}" for t in _ts for v in ("xn", "xd")]
for _q in "kvr":
    PARTS[f"mix{_q}"] = [f"{_q}_mA", f"{_q}_mB"]
    PARTS[f"high{_q}"] = [f"{_q}_hiA", f"{_q}_hiB"]
    PARTS[f"low{_q}"] = [f"{_q}_loA", f"{_q}_loB"]


def order_of(plan):
    out = {lane: [] for lane in LANES}
    for st in sorted(plan):
        for item in plan[st].split():
            lane, name = item.split(".")
            out[lane] += PARTS.get(name, [name])
    return out


PE, ACTE, DVE, POOL = (order_of(p) for p in (PE_PLAN, ACT_PLAN, DVE_PLAN, POOL_PLAN))
USES = [tuple(item.split(".")) for st in sorted(PE_PLAN) for item in PE_PLAN[st].split()]
READER = {f"patch{i}": ("dve", f"y_lo{i}") for i in range(3)}
READER.update({f"expand{i}": ("dve", f"h1_{i}") for i in range(3)})
READER.update({f"turn1_{i}": ("act", n) for i, n in enumerate(("xT_A1", "xT_B1", "xT_B2"))})
READER.update({f"{q}{g}": ("act", f"{q}{g}") for q in "kvr" for g in range(3)})
READER.update({f"proj{i}": ("dve", f"h2_{i}") for i in range(3)})
READER.update({f"turn2_{i}": ("dve", n) for i, n in enumerate(("X_lA0", "X_lB0", "X_lB1"))})
READER.update({"logits": ("dve", "lg"), "wrow0": ("act", "wrow_c0"), "wrow1": ("act", "wrow_c1"), "wcol": ("act", "wcol_c")})
SET_POOL = 24
WB = 2 * EXP
RING = 4
TXTS = [(b, lo, hi) for b in range(2) for t0, rows in TILES
        for lo, hi in [(max(t0, b * SEQ + 1 + NPATCH), min(t0 + rows, (b + 1) * SEQ))] if lo < hi]


def cut_at_bank(c0, c1):
    edge = (c0 // 512 + 1) * 512
    return [(c0, c1)] if c1 <= edge else [(c0, edge), (edge, c1)]


def at(order, name, n):
    return n * len(order) + order.index(name) + 1


def known(n):
    return n if type(n) is int else None


def build_fusion(nc, pixels, txt, pos, cls_token, patch_w, wkvr, wo, gate_w, wu, wg, wd, swu, swg, swd,
                 bd, sbd, gate_b, gate_bias, params, onehot, ident32, ident16, out):
    out_rows = out.rearrange("(n b) t c -> n (b t) c", b=2)
    with ExitStack() as ctx:
        def sb(name, shape, dt=F32):
            return ctx.enter_context(nc.sbuf_tensor(name, shape, dt))

        def sem(name):
            return ctx.enter_context(nc.semaphore(name))

        patch_hi, patch_lo = sb("patch_hi", [KP, KC, D], F16), sb("patch_lo", [KP, KC, D], F16)
        PW = 320
        kvr_w = {s: sb(f"kvr_{s}", [128, 3, PW], F16) for s in ("Ah", "Al", "Bh", "Bl")}
        wo_w = {s: sb(f"wo_{s}", [128, D], F16) for s in ("Ah", "Al", "Bh", "Bl")}
        gw_w = {s: sb(f"gw_{s}", [128, EXP], F16) for s in ("Ah", "Al", "Bh", "Bl")}
        up_w = {s: sb(f"up_{s}", [128, NX, HID], F16) for s in ("Ah", "Al", "Bh", "Bl")}
        gt_w = {s: sb(f"gt_{s}", [128, NX, HID], F16) for s in ("Ah", "Al", "Bh", "Bl")}
        dn_h, dn_l = sb("dn_h", [HID, NX, D], F16), sb("dn_l", [HID, NX, D], F16)
        bd_h, bd_l = sb("bd_h", [128, D], F16), sb("bd_l", [128, D], F16)
        par = sb("par", [128, 12 + 2 * NX])
        sel = sb("sel", [YW, 3, PAIR], F16)
        id32, id16 = sb("id32", [128, 128]), sb("id16", [128, 128], F16)
        gb_bc, bias_bc = sb("gb_bc", [128, EXP]), sb("bias_bc", [128, EXP])
        base = sb("base", [128, NT, D])
        decay = sb("decay", [128, 3])
        negw = sb("negw", [128, 3])
        wplusu, minusc = sb("wplusu", [128, 3]), sb("minusc", [128, 3])
        half = sb("half", [128, NT])
        reset_g, reset_e = sb("reset_g", [128, NT, GROUPS]), sb("reset_e", [128, NT, EXP])

        scan_buf, early_buf = sb("scan_buf", [128, 4 * 3 * SEQ]), sb("early_buf", [128, KC * PX + 4 * PAIR])
        xraw = scan_buf[0:KP, 0:KC * PX]
        bd32 = sb("bd32", [128, D])
        x_hi, x_lo = (early_buf[0:KP, i * KC * PX // 2:(i + 1) * KC * PX // 2].bitcast(F16).rearrange("p (c n) -> p c n", c=KC)
                      for i in range(2))
        y_hi, y_lo = sb("y_hi", [YW, 3, D], F16), sb("y_lo", [YW, 3, D], F16)
        h_in, h_mid = sb("h_in", [128, NT, D]), [sb(f"h_mid{p}", [128, NT, D]) for p in range(2)]
        stats, mv = sb("stats", [128, NT, 6]), sb("mv", [128, NT, 2])
        veps, rstd = sb("veps", [128, NT]), sb("rstd", [128, NT])
        xn = sb("xn", [128, NT, 256])
        xT = {s: sb(f"xT_{s}", [128, 2 * (SEQ + 1)]) for s in "AB"}
        dT, mix32 = ({s: early_buf[:, KC * PX + (2 * j + i) * PAIR:KC * PX + (2 * j + i + 1) * PAIR] for i, s in enumerate("AB")}
                     for j in range(2))
        mixh = [sb(f"mixh{i}", [128, PAIR], F16) for i in range(2)]
        mixl = [sb(f"mixl{i}", [128, PAIR], F16) for i in range(2)]
        mixB = [sb(f"mixB{i}", [128, PAIR], F16) for i in range(2)]
        kvr = {q: sb(f"{q}32", [128, 3, SEQ]) for q in "kvr"}
        mrun, num, den = (sb(f"{s}run", [128, 3, SEQ + 1]) for s in ("m", "n", "d"))
        z = kvr["k"]
        zp, zn, qp, qn = (scan_buf[:, i * 3 * SEQ:(i + 1) * 3 * SEQ].rearrange("p (g t) -> p g t", g=3) for i in range(4))
        e1s, e2s, e1, e2 = zp, zn, qp, qn
        ev = sb("ev", [128, 3, SEQ])
        oh_A, ol_A = mixh[0], mixl[0]
        oh_B, ol_B = sb("oh_B", [128, PAIR], F16), sb("ol_B", [128, PAIR], F16)
        XAh, XAl, XB = ([sb(f"{s}{p}", [128, PADT], F16) for p in range(2)] for s in ("XAh", "XAl", "XB"))
        def r16(name, w=EXP):
            return sb(name, [128, NT, w])

        lg, ex, score, biased, masked = (r16(s) for s in ("lg", "ex", "score", "biased", "masked"))
        egt, eeq, ecum = (r16(s) for s in ("egt", "eeq", "ecum"))
        gsum, ggt, geq, gcum, gbig, gtop, etop = (r16(s, GROUPS) for s in ("gsum", "ggt", "geq", "gcum", "gbig", "gtop", "etop"))
        rs = {s: sb(s, [128, NT]) for s in ("lmax", "lsum", "lrec", "gthr", "gcnt", "gneed", "ethr", "ecnt", "eneed")}
        wfl = r16("wfl")
        settled = sb("settled", [1, 2])
        wcat = sb("wcat", [128, NT, 128], F16)
        wT = [sb(f"wT{p}", [128, PADT], F16) for p in range(2)]
        wrow16 = sb("wrow16", [EXP, PADT])
        rows_dram = nc.dram_tensor("router_rows", [EXP, PAIR], F32)

        wb = [sb(f"wb{i}", [128, PAIR]) for i in range(RING)]
        silu = [sb(f"silu{i}", [128, SEQ]) for i in range(2)]
        a32 = [sb(f"a32_{i}", [128, SEQ]) for i in range(4)]
        a_hi = [sb(f"a_hi{i}", [128, PAIR], F16) for i in range(2)]
        a_lo = [sb(f"a_lo{i}", [128, PAIR], F16) for i in range(2)]

        ups = ctx.enter_context(nc.psum_tensor("ups", [128, 2, 512], F32))
        gts = ctx.enter_context(nc.psum_tensor("gts", [128, 2, 512], F32))
        ysum = ctx.enter_context(nc.psum_tensor("ysum", [128, 2 * 512], F32))
        lanes_ps = ctx.enter_context(nc.psum_tensor("lanes_ps", [128, 2, 512], F32))

        def bank(name):
            return lanes_ps[:, [u[1] for u in USES].index(name) % 2, :]


        consts_in = sem("consts_in")
        stage_in = [sem("stage_in0"), sem("stage_in1")]
        set_dve, set_act, set_pool = sem("set_dve"), sem("set_act"), sem("set_pool")
        base_in = sem("base_in")
        pixels_in, txt_in = sem("pixels_in"), sem("txt_in")
        rows_out, wb_in = sem("rows_out"), [sem(f"wb_in{i}") for i in range(RING)]
        pe_f, act_f, dve_f, pool_f = (sem(s) for s in ("pe_front", "act_front", "dve_front", "pool_front"))
        pe_t, act_t, dve_t, pool_t = (sem(s) for s in ("pe_tail", "act_tail", "dve_tail", "pool_tail"))
        pe_p, act_p, dve_p = (sem(s) for s in ("pe_patch", "act_patch", "dve_patch"))
        up_ready, gate_ready = sem("up_ready"), sem("gate_ready")
        silu_done, gated, weighted, hi_done, lo_done = (sem(s) for s in ("silu_done", "gated", "weighted", "hi_done", "lo_done"))
        down_done, fin_done, out_done = (sem(s) for s in ("down_done", "fin_done", "out_done"))

        def rows3(ap):
            return ap.rearrange("e k h -> k e h")

        SW = NX * D
        stage = [early_buf[:, 0:SW], scan_buf[:, 0:SW]]
        jobs = []

        def job(hi, lo, parts, p, shape):
            jobs.append((hi, lo, parts, p, shape))

        for s in range(2):
            ks = slice(0, DA) if s == 0 else slice(DA, D)
            for name, dst, routed, shared in (("up", up_w, wu, swu), ("gt", gt_w, wg, swg)):
                hi, lo = (dst["Ah"], dst["Al"]) if s == 0 else (dst["Bh"], dst["Bl"])
                parts = []
                for r in range(1 + s):
                    ps = slice(0, DA) if s == 0 else slice(r * DB, (r + 1) * DB)
                    parts.append((ps, slice(1, NX), rows3(routed)[ks]))
                    parts.append((ps, slice(0, 1), shared[ks].unsqueeze(1)))
                job(hi[:, :, :], lo[:, :, :], parts, 128, (NX, HID))
        job(dn_h[:, :, :], dn_l[:, :, :], [(slice(0, HID), slice(1, NX), rows3(wd)),
                                           (slice(0, HID), slice(0, 1), swd.unsqueeze(1))], 128, (NX, D))
        job(patch_hi[:, :, :], patch_lo[:, :, :], [(slice(0, KP), slice(0, KC), patch_w)], KP, (KC, D))
        for s in range(2):
            ks = slice(0, DA) if s == 0 else slice(DA, D)
            c = "AB"[s]
            places = [slice(0, DA)] if s == 0 else [slice(0, DB), slice(DB, 2 * DB)]
            for o0, o1, w0 in ((0, DA, 0), (DA, D, DA + DB)):
                job(kvr_w[c + "h"][:, :, w0:w0 + o1 - o0], kvr_w[c + "l"][:, :, w0:w0 + o1 - o0],
                    [(ps, slice(0, 3), wkvr[ks, :, o0:o1]) for ps in places], 128, (3, o1 - o0))
            job(wo_w[c + "h"][:, :].unsqueeze(1), wo_w[c + "l"][:, :].unsqueeze(1),
                [(ps, slice(0, 1), wo[ks].unsqueeze(1)) for ps in places], 128, (1, D))
            job(gw_w[c + "h"][:, :].unsqueeze(1), gw_w[c + "l"][:, :].unsqueeze(1),
                [(ps, slice(0, 1), gate_w[ks].unsqueeze(1)) for ps in places], 128, (1, EXP))
        JOBS = len(jobs)
        staged = [0, 0]
        need = []
        for j, (_, _, parts, _, _) in enumerate(jobs):
            staged[j % 2] += 16 * len(parts)
            need.append(staged[j % 2])

        def view(j):
            rows, cols = jobs[j][4]
            return stage[j % 2][0:jobs[j][3], 0:rows * cols].rearrange("p (a b) -> p a b", a=rows)

        T, F, P = "TFP"
        SET_DVE = (["z_settled", "z_base", "z_bd", "z_cls", "z_kh", "z_kl", "z_BH", "z_BL"] + [f"lo{j}" for j in range(JOBS)]
                   + ["bdhi", "bdlo", "cls0", "cls2", "negw", "wplusu", "minusc"])
        BASE_DMAS = 5 + sum(max(t0, b * SEQ) < min(t0 + rows, b * SEQ + 1 + NPATCH) for b in range(2) for t0, rows in TILES)
        PD, PU, PM, PBU, PBG = 0, 3, 6, 12, 12 + NX
        clsT = xn[:, :, 0:D]

        def q_at(name):
            return SET_DVE.index(name) + 1

        def steps_of(plan, st, n, pp):
            out_ = []
            for item in plan.get(st, "").split():
                lane, name = item.split(".")
                m = n + LANES[lane]
                if known(n) is None or 0 <= m < PAIRS:
                    out_.append((name, m, (pp + LANES[lane]) % 2))
            return out_

        block = ctx.enter_context(nc.Block())

        @block.sync
        def _(sp):
            nconst = 0
            for dst, src in ((par[:, :], params), (sel[:, :, :], onehot), (id32[:, :], ident32), (id16[:, :], ident16),
                             (gb_bc[:, :], gate_b.partition_broadcast(128)), (bias_bc[:, :], gate_bias.partition_broadcast(128))):
                sp.dma_start(dst, src).then_inc(consts_in, 16)
                nconst += 1
            sp.wait_ge(set_dve, q_at("z_cls"))
            nb = 0
            for b in range(2):
                for t, (t0, rows) in enumerate(TILES):
                    lo, hi = max(t0, b * SEQ), min(t0 + rows, b * SEQ + 1 + NPATCH)
                    if lo < hi:
                        sp.dma_start(base[lo - t0:hi - t0, t, :], pos[lo - b * SEQ:hi - b * SEQ]).then_inc(base_in, 16)
                        nb += 1
            for b in range(2):
                sp.dma_start(clsT[b * SEQ % 128:b * SEQ % 128 + 1, b * SEQ // 128, :], cls_token).then_inc(base_in, 16)
            for p0 in (0, 32):
                sp.dma_start(bd32[p0:p0 + EXP, :], bd).then_inc(base_in, 16)
            sp.dma_start(bd32[96:97, :], sbd).then_inc(base_in, 16)
            assert nb + 5 == BASE_DMAS
            for j, (_, _, parts, _, _) in enumerate(jobs):
                if j >= 2:
                    sp.wait_ge(set_dve, q_at(f"lo{j - 2}"))
                for ps, rs_, src in parts:
                    sp.dma_start(view(j)[ps, rs_, :], src).then_inc(stage_in[j % 2], 16)

            def load_pixels(n):
                m = n if known(n) is not None else sp.snap(n)
                if known(n) is None or n > 1:
                    sp.wait_ge(dve_f, at(DVE[F], "o2", n - 2))
                elif n == 1:
                    sp.wait_ge(dve_p, at(DVE[P], f"x_lo{XPIECES - 1}", 0))
                sp.dma_start(xraw[:, :], pixels[m]).then_inc(pixels_in, 16)

            def load_txt(n):
                m = n if known(n) is not None else sp.snap(n)
                if known(n) is None or n > 0:
                    sp.wait_ge(dve_f, at(DVE[F], "h1_2", n - 1))
                for b, lo, hi in TXTS:
                    t, r = divmod(lo, 128)
                    t_lo = lo - b * SEQ - 1 - NPATCH
                    sp.dma_start(base[r:r + hi - lo, t, :], txt[m, b, t_lo:t_lo + hi - lo, :]).then_inc(txt_in, 16)

            def spread(n, x):
                if x == 0:
                    sp.wait_ge(act_t, at(ACTE[T], "wrow_c1", n))
                    sp.dma_start(rows_dram[:, :], wrow16[:, 0:PAIR]).then_inc(rows_out, 16)
                    sp.wait_ge(rows_out, 16 * n + 16)
                elif x >= RING:
                    sp.wait_ge(weighted, WB * n + 2 * (x - RING + 1))
                sp.dma_start(wb[x % RING][:, :], rows_dram[x, :].partition_broadcast(128)).then_inc(wb_in[x % RING], 16)

            def store(n, pp):
                m = n if known(n) is not None else sp.snap(n)
                sp.wait_ge(fin_done, 3 * n + 3)
                for t, (t0, rows) in enumerate(TILES):
                    sp.dma_start(out_rows[m, t0:t0 + rows, :], h_mid[pp][0:rows, t, :]).then_inc(out_done, 16)

            def body(n, pp):
                for x in range(RING):
                    spread(n, x)
                if known(n) is None or n > 0:
                    store(n - 1, (pp + 1) % 2)
                if known(n) is None or n + 2 < PAIRS:
                    load_txt(n + 2)
                for x in range(RING, EXP):
                    spread(n, x)
                if known(n) is None or n + 3 < PAIRS:
                    load_pixels(n + 3)

            sp.wait_ge(set_dve, q_at("cls2"))
            load_pixels(0)
            load_txt(0)
            load_pixels(1)
            load_txt(1)
            load_pixels(2)
            body(0, 0)
            with sp.Fori(0, (PAIRS - 4) // 2) as i:
                for p in range(2):
                    body(2 * i + 1 + p, (1 + p) % 2)
            for n in range(PAIRS - 3, PAIRS):
                body(n, n % 2)
            store(PAIRS - 1, 1)
            sp.wait_ge(out_done, 16 * NT * PAIRS)

        @block.gpsimd
        def _(pool):
            fills = [(half[:, :], -0.5), (wcat[:, :, :], 0.0), (wcat[:, :, 96:97], 1.0), (mrun[:, :, 0:1], -1e38),
                     (num[:, :, 0:1], 0.0), (den[:, :, 0:1], 0.0)]
            fills += [(m[:, :, 1:w], 1.0) for m, w in ((reset_g, GROUPS), (reset_e, EXP))]
            fills += [(m[:, :, 0:1], 0.0) for m in (reset_g, reset_e)]
            fills += [(xT[s][:, b * (SEQ + 1):b * (SEQ + 1) + 1], 0.0) for s in "AB" for b in range(2)]
            fills += [(m[p][:, PAIR:PADT], 0.0) for m in (XAh, XAl, XB) for p in range(2)]
            fills += [(m[ps, cs], 0.0) for m in (oh_B, ol_B) for ps, cs in ((slice(0, DB), slice(SEQ, PAIR)),
                                                                        (slice(DB, 128), slice(0, SEQ)))]
            assert len(fills) == SET_POOL
            for k, (ap, value) in enumerate(fills):
                if k:
                    pool.wait_ge(set_pool, k)
                pool.memset(ap, value).then_inc(set_pool, 1)
            pool.wait_ge(set_pool, SET_POOL)

            def step(name, n, p):
                if name[:4] == "rstd":
                    k, i = name[4:].split("_")
                    ts = TILE_GROUPS[int(i)]
                    rows, c = TILES[ts[-1]][1], slice(ts[0], ts[-1] + 1)
                    pool.wait_ge(dve_f, at(DVE[F], f"veps{k}_{i}", n))
                    pool.tensor_tensor(rstd[0:rows, c], veps[0:rows, c], half[0:rows, c], ALU.pow).then_inc(pool_f, 1)
                if name == "w_low":
                    pool.wait_ge(act_t, at(ACTE[T], "w_high", n))
                    pool.tensor_tensor(wcat[:, :, 32:32 + EXP], wfl[:, :, :], wcat[:, :, 0:EXP], ALU.subtract).then_inc(pool_t, 1)
                if name[:6] == "shares":
                    g = int(name[6])
                    pool.wait_ge(act_f, at(ACTE[F], f"v{g}", n))
                    pool.tensor_tensor(ev[:, g, :], e2s[:, g, :], kvr["v"][:, g, :], ALU.mult).then_inc(pool_f, 1)
                    pool.tensor_tensor(z[:, g, :], e2[:, g, :], kvr["v"][:, g, :], ALU.mult).then_inc(pool_f, 1)

            def low_part(n, s, pp):
                S = 34 * n + s
                e, b = divmod(s, 2)
                pool.wait_ge(hi_done, S + 1)
                pool.tensor_tensor(a_lo[(pp + e) % 2][:, b * SEQ:(b + 1) * SEQ], a32[(34 * pp + s) % 4][:, :],
                                   a_hi[(pp + e) % 2][:, b * SEQ:(b + 1) * SEQ], ALU.subtract).then_inc(lo_done, 1)

            def body(n, pp):
                for s in range(SLOTS):
                    e, b = divmod(s, 2)
                    for name, m, p in steps_of(POOL_PLAN, s, n, pp):
                        step(name, m, p)
                    if s > 0:
                        low_part(n, s - 1, pp)
                    if e > 0:
                        x = e - 1
                        pool.wait_ge(wb_in[x % RING], 16 * (EXP // RING * n + x // RING + 1))
                        pool.wait_ge(gated, 34 * n + s + 1)
                        pool.tensor_tensor(a32[(34 * pp + s) % 4][:, :], a32[(34 * pp + s) % 4][:, :],
                                           wb[x % RING][:, b * SEQ:(b + 1) * SEQ], ALU.mult).then_inc(weighted, 1)
                low_part(n, SLOTS - 1, pp)

            for st in range(SLOTS):
                for name, m, p in steps_of({k: " ".join(i for i in v.split() if i[0] == "P") for k, v in POOL_PLAN.items()}, st, -2, 0):
                    step(name, m, p)
            for st in range(SLOTS):
                for name, m, p in steps_of(POOL_PLAN, st, -1, 1):
                    step(name, m, p)
            body(0, 0)
            with pool.Fori(0, (PAIRS - 4) // 2) as i:
                for p in range(2):
                    body(2 * i + 1 + p, (1 + p) % 2)
            for n in range(PAIRS - 3, PAIRS):
                body(n, n % 2)

        @block.scalar
        def _(act):
            for j, (hi, lo, parts, rows, shape) in enumerate(jobs):
                act.wait_ge(stage_in[j % 2], need[j])
                if j == 0:
                    act.wait_ge(set_dve, q_at("z_BL"))
                act.activation(hi, view(j), ACT.Copy).then_inc(set_act, 1)
            act.wait_ge(consts_in, 16 * 6)
            act.activation(decay[:, :], par[:, PD:PD + 3], ACT.Exp).then_inc(set_act, 1)
            act.wait_ge(set_pool, SET_POOL)

            def step(name, n, p):
                later = known(n) is None or n > 0
                if name[:4] == "x_hi":
                    i = int(name[4])
                    if i == 0:
                        act.wait_ge(pixels_in, 16 * n + 16)
                        if later:
                            act.wait_ge(pe_p, at(PE[P], "patch2", n - 1))
                    c = slice(i * XPC, (i + 1) * XPC)
                    act.activation(x_hi[:, :, :].rearrange("p a b -> p (a b)")[:, c], xraw[:, c], ACT.Copy).then_inc(act_p, 1)
                if name[:7] == "turned1":
                    i = int(name[8])
                    act.wait_ge(pe_f, at(PE[F], f"turn1_{i}", n))
                    if later:
                        act.wait_ge(dve_f, at(DVE[F], "v_mB", n - 1))
                    for s, lo, hi, col in TURNS[i]:
                        for tok, c, ln in split_at_batch(lo, hi):
                            act.activation(xT[s][:, c:c + ln], bank(f"turn1_{i}")[:, col + tok - lo:col + tok - lo + ln],
                                           ACT.Copy).then_inc(act_f, 1)
                if name[:4] == "high":
                    q = name[4]
                    qi = "krv".index(q)
                    for s, dst in (("A", mixh[qi % 2]), ("B", mixB[qi % 2])):
                        act.wait_ge(dve_f, at(DVE[F], f"{q}_m{s}", n))
                        if s == "A" and (qi == 2 or later):
                            act.wait_ge(pe_f, at(PE[F], {0: "v2", 1: "r2", 2: "k2"}[qi], n if qi == 2 else n - 1))
                        act.activation(dst[:, :], mix32[s][:, :], ACT.Copy).then_inc(act_f, 1)
                if name[0] in "kvr" and len(name) == 2:
                    q, g = name[0], int(name[1])
                    act.wait_ge(pe_f, at(PE[F], name, n))
                    if later and g == 0:
                        act.wait_ge(dve_f, at(DVE[F], "o2", n - 1))
                    act.activation(kvr[q][:, g, :], bank(name)[:, 0:SEQ], ACT.Copy).then_inc(act_f, 1)
                if name[:4] == "relu":
                    g = int(name[4])
                    act.wait_ge(dve_f, at(DVE[F], f"z{g}", n))
                    if later and g == 0:
                        act.wait_ge(dve_p, at(DVE[P], f"x_lo{XPIECES - 1}", n + 1 if known(n) is None else min(n + 1, PAIRS - 1)))
                    elif g == 0:
                        act.wait_ge(dve_p, at(DVE[P], f"x_lo{XPIECES - 1}", 1))
                    act.activation(zp[:, g, :], z[:, g, :], ACT.Relu).then_inc(act_f, 1)
                    act.activation(zn[:, g, :], z[:, g, :], ACT.Relu, scale=-1.0).then_inc(act_f, 1)
                    act.activation(qp[:, g, :], z[:, g, :], ACT.Relu, bias=wplusu[:, g:g + 1]).then_inc(act_f, 1)
                    act.activation(qn[:, g, :], z[:, g, :], ACT.Relu, bias=minusc[:, g:g + 1], scale=-1.0).then_inc(act_f, 1)
                if name[:4] == "exps":
                    g = int(name[4])
                    act.wait_ge(act_f, at(ACTE[F], f"qn{g}", n))
                    for e_ in (e1s, e2s, e1, e2):
                        act.activation(e_[:, g, :], e_[:, g, :], ACT.Exp, scale=-1.0).then_inc(act_f, 1)
                    act.activation(kvr["r"][:, g, :], kvr["r"][:, g, :], ACT.Exp, scale=-1.0).then_inc(act_f, 1)
                if name == "ohighA":
                    act.wait_ge(dve_f, at(DVE[F], "o1", n))
                    if later:
                        act.wait_ge(pe_f, at(PE[F], "proj2", n - 1))
                    act.activation(oh_A[:, :].rearrange("p (b t) -> p b t", b=2), ev[:, 0:2, :], ACT.Copy).then_inc(act_f, 1)
                if name == "ohighB":
                    act.wait_ge(dve_f, at(DVE[F], "o2", n))
                    for b in range(2):
                        ps, cs = slice(b * DB, (b + 1) * DB), slice(b * SEQ, (b + 1) * SEQ)
                        act.activation(oh_B[ps, cs], ev[ps, 2, :], ACT.Copy).then_inc(act_f, 1)
                if name[:7] == "turned2":
                    i = int(name[8])
                    act.wait_ge(pe_f, at(PE[F], f"turn2_{i}", n))
                    for s, lo, hi, col in TURNS[i]:
                        dst = XAh[p] if s == "A" else XB[p]
                        act.activation(dst[:, lo:hi], bank(f"turn2_{i}")[:, col:col + hi - lo], ACT.Copy).then_inc(act_f, 1)
                if name == "softmax":
                    act.wait_ge(dve_f, at(DVE[F], "lsh", n))
                    act.activation(ex[:, :, :], lg[:, :, :], ACT.Exp).then_inc(act_f, 1)
                if name[:6] == "wrow_c":
                    i = int(name[6])
                    c0, c1 = ((0, 512), (512, PADT))[i]
                    act.wait_ge(pe_t, at(PE[T], f"wrow{i}", n))
                    if later and i == 0:
                        for ring_in in wb_in:
                            act.wait_ge(ring_in, 16 * (EXP // RING) * n)
                    act.activation(wrow16[:, c0:c1], bank(f"wrow{i}")[0:EXP, 0:c1 - c0], ACT.Copy).then_inc(act_t, 1)
                if name == "w_high":
                    act.wait_ge(dve_t, at(DVE[T], "wfull", n))
                    if later:
                        act.wait_ge(pe_t, at(PE[T], "wcol", n - 1))
                    act.activation(wcat[:, :, 0:EXP], wfl[:, :, :], ACT.Copy).then_inc(act_t, 1)
                if name == "wcol_c":
                    act.wait_ge(pe_t, at(PE[T], "wcol", n))
                    act.activation(wT[p][:, :], bank("wcol").bitcast(F16)[:, 0:PADT], ACT.Copy).then_inc(act_t, 1)

            def high_part(n, s, pp):
                S = 34 * n + s
                e, b = divmod(s, 2)
                if e > 0:
                    act.wait_ge(weighted, WB * n + s - 1)
                else:
                    act.wait_ge(gated, S + 1)
                if b == 0:
                    if e >= 2:
                        act.wait_ge(down_done, NX * n + e - 1)
                    elif type(n) is not int or n > 0:
                        act.wait_ge(down_done, NX * n + e - 1)
                act.activation(a_hi[(pp + e) % 2][:, b * SEQ:(b + 1) * SEQ], a32[(34 * pp + s) % 4][:, :], ACT.Copy)\
                   .then_inc(hi_done, 1)

            def body(n, pp, first=False):
                for s in range(SLOTS):
                    S = 34 * n + s
                    e = s // 2
                    for name, m, p in steps_of(ACT_PLAN, s, n, pp):
                        step(name, m, p)
                    act.wait_ge(up_ready, S + 1)
                    if s >= 2 or known(n) is None or n > 0:
                        act.wait_ge(gated, S - 1)
                    act.activation(silu[s % 2][:, :], ups[:, s % 2, 0:SEQ], ACT.Silu, bias=par[:, PBU + e:PBU + e + 1])\
                       .then_inc(silu_done, 1)
                    if s > 0:
                        high_part(n, s - 1, pp)
                    elif not first:
                        high_part(n - 1, SLOTS - 1, (pp + 1) % 2)

            for st in range(SLOTS):
                for name, m, p in steps_of({k: " ".join(i for i in v.split() if i[0] == "P") for k, v in ACT_PLAN.items()}, st, -2, 0):
                    step(name, m, p)
            for st in range(SLOTS):
                for name, m, p in steps_of(ACT_PLAN, st, -1, 1):
                    step(name, m, p)
            body(0, 0, first=True)
            with act.Fori(0, (PAIRS - 4) // 2) as i:
                for p in range(2):
                    body(2 * i + 1 + p, (1 + p) % 2)
            for n in range(PAIRS - 3, PAIRS):
                body(n, n % 2)
            high_part(PAIRS - 1, SLOTS - 1, 1)

        @block.vector
        def _(dve):
            dve.memset(settled[:, :], 0.0).then_inc(set_dve, 1)
            dve.memset(base[:, :, :], 0.0).then_inc(set_dve, 1)
            dve.memset(bd32[:, :], 0.0).then_inc(set_dve, 1)
            dve.memset(clsT[:, :, :], 0.0).then_inc(set_dve, 1)
            for c in ("Ah", "Al", "Bh", "Bl"):
                dve.memset(kvr_w[c][:, :, :], 0.0).then_inc(set_dve, 1)
            for j, (hi, lo, parts, rows, shape) in enumerate(jobs):
                dve.wait_ge(set_act, j + 1)
                if j == 0:
                    dve.wait_ge(set_dve, q_at("z_BL"))
                dve.tensor_tensor(lo, view(j), hi, ALU.subtract).then_inc(set_dve, 1)
            dve.wait_ge(base_in, 16 * BASE_DMAS)
            dve.tensor_copy(bd_h[:, :], bd32[:, :]).then_inc(set_dve, 1)
            dve.wait_ge(set_dve, q_at("bdhi"))
            dve.tensor_tensor(bd_l[:, :], bd32[:, :], bd_h[:, :], ALU.subtract).then_inc(set_dve, 1)
            for t in (0, SEQ // 128):
                dve.tensor_tensor(base[:, t, :], base[:, t, :], clsT[:, t, :], ALU.add).then_inc(set_dve, 1)
            dve.wait_ge(set_act, JOBS + 1)
            dve.tensor_scalar(negw[:, :], decay[:, :], -1.0, None, ALU.mult).then_inc(set_dve, 1)
            dve.wait_ge(set_dve, q_at("negw"))
            dve.tensor_tensor(wplusu[:, :], negw[:, :], par[:, PU:PU + 3], ALU.add).then_inc(set_dve, 1)
            dve.wait_ge(set_dve, q_at("wplusu"))
            dve.tensor_scalar(minusc[:, :], wplusu[:, :], -1.0, None, ALU.mult).then_inc(set_dve, 1)
            dve.wait_ge(set_dve, len(SET_DVE))
            dve.wait_ge(set_pool, SET_POOL)

            def after(name, n):
                dve.wait_ge(dve_f, at(DVE[F], name, n))

            def after_t(name, n):
                dve.wait_ge(dve_t, at(DVE[T], name, n))

            def select4(x, thr, top, gt, eq, cnt, need_, cum, reset, w, names, n, done, after):
                bc = [128, NT, w]
                dve.tensor_copy(rs[thr][:, :], top[:, :, TOPK - 1]).then_inc(done, 1)
                after(names + "thr", n)
                tb = rs[thr][:, :].unsqueeze(2).to_broadcast(bc)
                dve.tensor_tensor(gt[:, :, :], x[:, :, :], tb, ALU.is_gt).then_inc(done, 1)
                dve.tensor_tensor(eq[:, :, :], x[:, :, :], tb, ALU.is_equal).then_inc(done, 1)
                after(names + "gt", n)
                dve.tensor_reduce(rs[cnt][:, :], gt[:, :, :], AX_X, ALU.add).then_inc(done, 1)
                after(names + "cnt", n)
                dve.tensor_scalar(rs[need_][:, :], rs[cnt][:, :], -1.0, float(TOPK), ALU.mult, ALU.add).then_inc(done, 1)
                dve.tensor_tensor_scan(cum[:, :, :].rearrange("p a b -> p (a b)"), reset[:, :, :].rearrange("p a b -> p (a b)"),
                                       eq[:, :, :].rearrange("p a b -> p (a b)"), 0.0, ALU.mult, ALU.add).then_inc(done, 1)
                after(names + "cum", n)
                dve.tensor_tensor(cum[:, :, :], cum[:, :, :], rs[need_][:, :].unsqueeze(2).to_broadcast(bc), ALU.is_le)\
                   .then_inc(done, 1)
                after(names + "le", n)
                dve.tensor_tensor(eq[:, :, :], cum[:, :, :], eq[:, :, :], ALU.mult).then_inc(done, 1)
                after(names + "and", n)
                dve.tensor_tensor(gt[:, :, :], gt[:, :, :], eq[:, :, :], ALU.add).then_inc(done, 1)
                after(names + "sel", n)

            def step(name, n, p):
                later = known(n) is None or n > 0
                two = lambda m: m[:, :].rearrange("p (b t) -> p b t", b=2)
                flat_x = lambda m: m[:, :, :].rearrange("p a b -> p (a b)")
                if name[:4] == "x_lo":
                    i = int(name[4])
                    c = slice(i * XPC, (i + 1) * XPC)
                    dve.wait_ge(act_p, at(ACTE[P], f"x_hi{i}", n))
                    dve.tensor_tensor(flat_x(x_lo)[:, c], xraw[:, c], flat_x(x_hi)[:, c], ALU.subtract).then_inc(dve_p, 1)
                if name[0] == "y":
                    i = int(name[1])
                    rows = YT[i][1]
                    dve.wait_ge(pe_p, at(PE[P], f"patch{i}", n))
                    dve.tensor_copy(y_hi[0:rows, i, :], bank(f"patch{i}")[0:rows, 0:D]).then_inc(dve_p, 1)
                    dve.wait_ge(dve_p, at(DVE[P], f"y_hi{i}", n))
                    dve.tensor_tensor(y_lo[0:rows, i, :], bank(f"patch{i}")[0:rows, 0:D], y_hi[0:rows, i, :], ALU.subtract)\
                       .then_inc(dve_p, 1)
                if name[:3] == "sum":
                    k, i = int(name[3]), int(name[5])
                    ts = TILE_GROUPS[i]
                    rows, c = TILES[ts[-1]][1], slice(ts[0], ts[-1] + 1)
                    use = ("expand", "proj")[k - 1] + str(i)
                    src = bank(use)[0:rows, 0:len(ts) * D].rearrange("p (t d) -> p t d", t=len(ts))
                    dve.wait_ge(pe_f, at(PE[F], use, n))
                    if k == 1:
                        dve.wait_ge(txt_in, 16 * len(TXTS) * n + 16 * len(TXTS))
                        if i == 0 and later:
                            dve.wait_ge(dve_f, at(DVE[F], "h2_2", n - 1))
                    elif i == 0 and (known(n) is None or n >= 2):
                        dve.wait_ge(out_done, 16 * NT * (n - 1))
                    addend, hp = (base, h_in) if k == 1 else (h_in, h_mid[p])
                    dve.tensor_tensor(hp[0:rows, c, :], src, addend[0:rows, c, :], ALU.add).then_inc(dve_f, 1)
                    after(f"h{k}_{i}", n)
                    for t in ts:
                        dve.bn_stats(stats[0:rows, t, :], hp[0:rows, t, :]).then_inc(dve_f, 1)
                    after(f"stats{k}_{ts[-1]}", n)
                    dve.tensor_copy(settled[0:1, 0:1], settled[0:1, 1:2]).then_inc(dve_f, 1)
                    for t in ts:
                        dve.bn_aggr(mv[0:rows, t, :], stats[0:rows, t, :]).then_inc(dve_f, 1)
                    after(f"aggr{k}_{ts[-1]}", n)
                    dve.tensor_scalar(veps[0:rows, c], mv[0:rows, c, 1], EPS, None, ALU.add).then_inc(dve_f, 1)
                if name[:4] == "norm":
                    k, i = int(name[4]), int(name[6])
                    hp = h_in if k == 1 else h_mid[p]
                    dve.wait_ge(pool_f, at(POOL[F], f"rstd{k}_{i}", n))
                    for t in TILE_GROUPS[i]:
                        rows = TILES[t][1]
                        for dst, src in ((slice(0, D), slice(0, D)), (slice(D, 256), slice(DA, D))):
                            dve.tensor_scalar(xn[0:rows, t, dst], hp[0:rows, t, src], mv[0:rows, t, 0:1], rstd[0:rows, t:t + 1],
                                              ALU.subtract, ALU.mult).then_inc(dve_f, 1)
                shifted = {s: xT[s][:, :].rearrange("p (b t) -> p b t", b=2) for s in "AB"}
                if name == "diff":
                    for s in "AB":
                        dve.wait_ge(act_f, at(ACTE[F], f"xT_{s}2", n))
                        dve.tensor_tensor(two(dT[s]), shifted[s][:, :, 1:SEQ + 1], shifted[s][:, :, 0:SEQ], ALU.subtract)\
                           .then_inc(dve_f, 1)
                if name[:3] == "mix":
                    q = name[3]
                    after("dB" if q == "k" else {"r": "k_loB", "v": "r_loB"}[q], n)
                    for si, s in enumerate("AB"):
                        col = PM + 2 * "kvr".index(q) + si
                        dve.scalar_tensor_tensor(out=two(mix32[s]), in0=two(dT[s]), scalar=par[:, col:col + 1],
                                                 in1=shifted[s][:, :, 0:SEQ], op0=ALU.mult, op1=ALU.add).then_inc(dve_f, 1)
                if name[:3] == "low":
                    q = name[3]
                    qi = "krv".index(q)
                    dve.wait_ge(act_f, at(ACTE[F], f"{q}_hiA", n))
                    dve.tensor_tensor(mixl[qi % 2][:, :], mix32["A"][:, :], mixh[qi % 2][:, :], ALU.subtract).then_inc(dve_f, 1)
                    dve.wait_ge(act_f, at(ACTE[F], f"{q}_hiB", n))
                    dve.tensor_tensor(mixB[qi % 2][DB:128, :], mix32["B"][DB:128, :], mixB[qi % 2][DB:128, :], ALU.subtract)\
                       .then_inc(dve_f, 1)
                if name[:3] == "run":
                    g = int(name[3])
                    dve.wait_ge(act_f, at(ACTE[F], f"k{g}", n))
                    dve.tensor_tensor_scan(mrun[:, g, 1:SEQ + 1], negw[:, g:g + 1].to_broadcast([128, SEQ]), kvr["k"][:, g, :], -1e38, ALU.add, ALU.max)\
                       .then_inc(dve_f, 1)
                    after(f"m{g}", n)
                    dve.scalar_tensor_tensor(out=z[:, g, :], in0=kvr["k"][:, g, :], scalar=negw[:, g:g + 1],
                                             in1=mrun[:, g, 0:SEQ], op0=ALU.subtract, op1=ALU.subtract).then_inc(dve_f, 1)
                if name[:3] == "div":
                    g = int(name[3])
                    dd = mrun[:, g, 1:SEQ + 1]
                    dve.wait_ge(act_f, at(ACTE[F], f"er{g}", n))
                    dve.tensor_tensor_scan(den[:, g, 1:SEQ + 1], e1s[:, g, :], e2s[:, g, :], 0.0, ALU.mult, ALU.add)\
                       .then_inc(dve_f, 1)
                    after(f"den{g}", n)
                    dve.tensor_tensor(dd, e1[:, g, :], den[:, g, 0:SEQ], ALU.mult).then_inc(dve_f, 1)
                    after(f"d1{g}", n)
                    dve.tensor_tensor(dd, dd, e2[:, g, :], ALU.add).then_inc(dve_f, 1)
                    after(f"d2{g}", n)
                    dve.scalar_tensor_tensor(out=dd, in0=kvr["r"][:, g, :], scalar=1.0, in1=dd,
                                             op0=ALU.add, op1=ALU.mult).then_inc(dve_f, 1)
                if name[:3] == "rec" and len(name) == 4:
                    g = int(name[3])
                    after(f"d3{g}", n)
                    dve.reciprocal(mrun[:, g, 1:SEQ + 1], mrun[:, g, 1:SEQ + 1]).then_inc(dve_f, 1)
                if name[:4] == "quot":
                    g = int(name[4])
                    dve.wait_ge(pool_f, at(POOL[F], f"t2{g}", n))
                    dve.tensor_tensor_scan(num[:, g, 1:SEQ + 1], e1s[:, g, :], ev[:, g, :], 0.0, ALU.mult, ALU.add)\
                       .then_inc(dve_f, 1)
                    after(f"num{g}", n)
                    dve.tensor_tensor(ev[:, g, :], e1[:, g, :], num[:, g, 0:SEQ], ALU.mult).then_inc(dve_f, 1)
                    after(f"t1{g}", n)
                    dve.tensor_tensor(ev[:, g, :], ev[:, g, :], z[:, g, :], ALU.add).then_inc(dve_f, 1)
                    after(f"t3{g}", n)
                    dve.tensor_tensor(ev[:, g, :], ev[:, g, :], mrun[:, g, 1:SEQ + 1], ALU.mult).then_inc(dve_f, 1)
                if name == "olowA":
                    dve.wait_ge(act_f, at(ACTE[F], "o_hiA", n))
                    dve.tensor_tensor(two(ol_A), ev[:, 0:2, :], two(oh_A), ALU.subtract).then_inc(dve_f, 1)
                if name == "olowB":
                    for b in range(2):
                        ps, cs = slice(b * DB, (b + 1) * DB), slice(b * SEQ, (b + 1) * SEQ)
                        dve.wait_ge(act_f, at(ACTE[F], f"o_hiB{b}", n))
                        dve.tensor_tensor(ol_B[ps, cs], ev[ps, 2, :], oh_B[ps, cs], ALU.subtract).then_inc(dve_f, 1)
                if name[:4] == "xlow":
                    i = int(name[4])
                    dve.wait_ge(act_f, at(ACTE[F], ("X_hA0", "X_hB0", "X_hB1")[i], n))
                    ps_ = bank(f"turn2_{i}")
                    for s, lo, hi, col in TURNS[i]:
                        if s == "A":
                            dve.tensor_tensor(XAl[p][:, lo:hi], ps_[:, col:col + hi - lo], XAh[p][:, lo:hi], ALU.subtract)\
                               .then_inc(dve_f, 1)
                        else:
                            dve.tensor_tensor(XB[p][DB:128, lo:hi], ps_[DB:128, col:col + hi - lo], XB[p][DB:128, lo:hi],
                                              ALU.subtract).then_inc(dve_f, 1)
                bc = [128, NT, EXP]
                all_t = lambda m: m[:, :].unsqueeze(1).to_broadcast(bc)
                per_t = lambda m: rs[m][:, :].unsqueeze(2).to_broadcast(bc)
                flat = lambda m: m[:, :, :].rearrange("p t g -> p (t g)").unsqueeze(2).to_broadcast([128, NT * GROUPS, 2])
                f2 = lambda m: m[:, :, :].rearrange("p t (g k) -> p (t g) k", k=2)
                if name == "route1":
                    dve.wait_ge(pe_f, at(PE[F], "logits", n))
                    dve.tensor_tensor(lg[:, :, :], bank("logits")[:, 0:NT * EXP].rearrange("p (t e) -> p t e", t=NT), all_t(gb_bc), ALU.add)\
                       .then_inc(dve_f, 1)
                    after("lg", n)
                    dve.tensor_reduce(rs["lmax"][:, :], lg[:, :, :], AX_X, ALU.max).then_inc(dve_f, 1)
                    after("lmax", n)
                    dve.tensor_tensor(lg[:, :, :], lg[:, :, :], per_t("lmax"), ALU.subtract).then_inc(dve_f, 1)
                    dve.wait_ge(act_f, at(ACTE[F], "softmax", n))
                    dve.tensor_reduce(rs["lsum"][:, :], ex[:, :, :], AX_X, ALU.add).then_inc(dve_f, 1)
                    after("lsum", n)
                    dve.reciprocal(rs["lrec"][:, :], rs["lsum"][:, :]).then_inc(dve_f, 1)
                    after("lrec", n)
                    dve.tensor_tensor(score[:, :, :], ex[:, :, :], per_t("lrec"), ALU.mult).then_inc(dve_f, 1)
                    after("score", n)
                    dve.tensor_tensor(biased[:, :, :], score[:, :, :], all_t(bias_bc), ALU.add).then_inc(dve_f, 1)
                    after("biased", n)
                    pairs = biased[:, :, :].rearrange("p t (g k) -> p t g k", k=2)
                    dve.tensor_tensor(gsum[:, :, :], pairs[:, :, :, 0], pairs[:, :, :, 1], ALU.add).then_inc(dve_f, 1)
                if name == "route2":
                    after("gsum", n)
                    dve.tensor_copy(settled[0:1, 0:1], settled[0:1, 1:2]).then_inc(dve_f, 1)
                    for t in range(NT):
                        dve.max(gtop[:, t, :], gsum[:, t, :]).then_inc(dve_f, 1)
                    after(f"gtop{NT - 1}", n)
                    select4(gsum, "gthr", gtop, ggt, geq, "gcnt", "gneed", gcum, reset_g, GROUPS, "g", n, dve_f, after)
                    dve.tensor_scalar(gbig[:, :, :], ggt[:, :, :], 1e30, -1e30, ALU.mult, ALU.add).then_inc(dve_f, 1)
                    dve.tensor_tensor(f2(masked), f2(biased), flat(ggt), ALU.mult).then_inc(dve_f, 1)
                    after("masked", n)
                    dve.tensor_tensor(f2(masked), f2(masked), flat(gbig), ALU.add).then_inc(dve_f, 1)
                if name == "route3":
                    after("masked2", n)
                    dve.tensor_copy(settled[0:1, 0:1], settled[0:1, 1:2]).then_inc(dve_t, 1)
                    for t in range(NT):
                        dve.max(etop[:, t, :], masked[:, t, :]).then_inc(dve_t, 1)
                    after_t(f"etop{NT - 1}", n)
                    select4(masked, "ethr", etop, egt, eeq, "ecnt", "eneed", ecum, reset_e, EXP, "e", n, dve_t, after_t)
                    if later:
                        dve.wait_ge(pool_t, at(POOL[T], "w_low", n - 1))
                    dve.scalar_tensor_tensor(out=wfl[:, :, :], in0=score[:, :, :], scalar=SCALE, in1=egt[:, :, :],
                                             op0=ALU.mult, op1=ALU.mult).then_inc(dve_t, 1)


            def finish(n, pp):
                dve.wait_ge(down_done, NX * n + NX)
                for i, ts in enumerate(TILE_GROUPS):
                    rows, c = TILES[ts[-1]][1], slice(ts[0], ts[-1] + 1)
                    src = ysum[0:rows, ts[0] * D:(ts[-1] + 1) * D].rearrange("p (t d) -> p t d", t=len(ts))
                    dve.tensor_tensor(h_mid[pp][0:rows, c, :], src, h_mid[pp][0:rows, c, :], ALU.add).then_inc(fin_done, 1)

            def body(n, pp, first=False):
                for s in range(SLOTS):
                    S = 34 * n + s
                    e = s // 2
                    for name, m, p in steps_of(DVE_PLAN, s, n, pp):
                        step(name, m, p)
                    dve.wait_ge(silu_done, S + 1)
                    dve.wait_ge(gate_ready, S + 1)
                    if s >= 4 or not first:
                        dve.wait_ge(lo_done, S - 3)
                    dve.scalar_tensor_tensor(out=a32[(34 * pp + s) % 4][:, :], in0=gts[:, s % 2, 0:SEQ],
                                             scalar=par[:, PBG + e:PBG + e + 1], in1=silu[s % 2][:, :],
                                             op0=ALU.add, op1=ALU.mult).then_inc(gated, 1)
                    if s == 2 and not first:
                        finish(n - 1, (pp + 1) % 2)

            for st in range(SLOTS):
                for name, m, p in steps_of({k: " ".join(i for i in v.split() if i[0] == "P") for k, v in DVE_PLAN.items()}, st, -2, 0):
                    step(name, m, p)
            for st in range(SLOTS):
                for name, m, p in steps_of(DVE_PLAN, st, -1, 1):
                    step(name, m, p)
            body(0, 0, first=True)
            with dve.Fori(0, (PAIRS - 4) // 2) as i:
                for p in range(2):
                    body(2 * i + 1 + p, (1 + p) % 2)
            for n in range(PAIRS - 3, PAIRS):
                body(n, n % 2)
            finish(PAIRS - 1, 1)

        @block.tensor
        def _(pe):
            pe.wait_ge(set_dve, len(SET_DVE))
            pe.wait_ge(set_pool, SET_POOL)

            def free(name, n):
                k = [u[1] for u in USES].index(name)
                body_n = n - LANES[USES[k][0]]
                k -= 2
                while True:
                    lane, use = USES[k]
                    m = (body_n if k >= 0 else body_n - 1) + LANES[lane]
                    if known(n) is None or 0 <= m < PAIRS:
                        break
                    if k < -len(USES) + 2:
                        return
                    k -= 2
                who, last = READER[use]
                if who == "act":
                    pe.wait_ge({T: act_t, F: act_f}[lane], at(ACTE[lane], last, m))
                else:
                    pe.wait_ge({F: dve_f, P: dve_p}[lane], at(DVE[lane], last, m))

            def chain(dst, terms, skip=False):
                for i, (lhsT, rhs) in enumerate(terms):
                    mm = pe.matmul(dst, lhsT, rhs, start=(i == 0), stop=(i == len(terms) - 1))
                return mm

            def step(name, n, p):
                out_ps = bank(name)
                free(name, n)
                if name[:5] == "patch":
                    i = int(name[5])
                    cs = slice(YT[i][0], YT[i][0] + YT[i][1])
                    pe.wait_ge(dve_p, at(DVE[P], f"x_lo{XPIECES - 1}", n))
                    chain(out_ps[0:YT[i][1], 0:D], [(x[:, c, cs], w[:, c, :]) for c in range(KC) for x, w in
                                                    ((x_hi, patch_hi), (x_lo, patch_hi), (x_hi, patch_lo))]).then_inc(pe_p, 1)
                if name[:6] == "expand":
                    i = int(name[6])
                    pe.wait_ge(dve_p, at(DVE[P], "y_lo2", n))
                    for j, t in enumerate(TILE_GROUPS[i]):
                        t0, rows = TILES[t]
                        terms = [(sel[0:YT[k][1], k, t0:t0 + rows], y[0:YT[k][1], k, :]) for k in SELECTED[t] for y in (y_hi, y_lo)]
                        for m, (a, b_) in enumerate(terms):
                            mm = pe.matmul(out_ps[0:rows, j * D:(j + 1) * D], a, b_, start=(j == 0 and m == 0),
                                           stop=(m == len(terms) - 1), skip_group_check=True)
                    mm.then_inc(pe_f, 1)
                if name[:4] == "turn":
                    k, i = int(name[4]), int(name[6])
                    pe.wait_ge(dve_f, at(DVE[F], f"xd{k}_{(3, 4, 4)[i]}", n))
                    for s, lo, hi, col in TURNS[i]:
                        for t, (t0, rows) in enumerate(TILES):
                            if lo <= t0 < hi:
                                cs = slice(0, DA) if s == "A" else slice(DA, 256)
                                mm = pe.transpose(out_ps[:, col + t0 - lo:col + t0 - lo + rows], xn[0:rows, t, cs],
                                                  id32[0:rows, 0:rows])
                    mm.then_inc(pe_f, 1)
                if name[0] in "kvr" and len(name) == 2:
                    q, g = name[0], int(name[1])
                    qb = "krv".index(q) % 2
                    pe.wait_ge(dve_f, at(DVE[F], f"{q}_loB", n))
                    W = {s: kvr_w[s][:, "kvr".index(q), :] for s in kvr_w}

                    def terms(b, c0):
                        ws, cs = slice(c0, c0 + 128), slice(b * SEQ, (b + 1) * SEQ)
                        mh, ml, mb = mixh[qb][:, cs], mixl[qb][:, cs], mixB[qb][:, cs]
                        return [(W["Ah"][:, ws], mh), (W["Ah"][:, ws], ml), (W["Al"][:, ws], mh),
                                (W["Bh"][:, ws], mb), (W["Bl"][:, ws], mb)]
                    both = terms(g, 0) if g < 2 else terms(0, DA + DB) + terms(1, DA)
                    chain(out_ps[:, 0:SEQ], both).then_inc(pe_f, 1)
                if name[:4] == "proj":
                    i = int(name[4])
                    pe.wait_ge(dve_f, at(DVE[F], "o_loB1", n))
                    for j, t in enumerate(TILE_GROUPS[i]):
                        t0, rows = TILES[t]
                        cs = slice(t0, t0 + rows)
                        terms_ = [(oh_A[:, cs], wo_w["Ah"]), (ol_A[:, cs], wo_w["Ah"]), (oh_A[:, cs], wo_w["Al"]),
                                  (oh_B[:, cs], wo_w["Bh"]), (ol_B[:, cs], wo_w["Bh"]), (oh_B[:, cs], wo_w["Bl"])]
                        for m, (a, b_) in enumerate(terms_):
                            mm = pe.matmul(out_ps[0:rows, j * D:(j + 1) * D], a, b_[:, :], start=(j == 0 and m == 0),
                                           stop=(m == 5), skip_group_check=True)
                    mm.then_inc(pe_f, 1)
                if name == "logits":
                    pe.wait_ge(dve_f, at(DVE[F], "X_lB1", n))
                    for t in range(NT):
                        cs = slice(t * 128, (t + 1) * 128)
                        terms_ = [(XAh[p][:, cs], gw_w["Ah"]), (XAl[p][:, cs], gw_w["Ah"]), (XAh[p][:, cs], gw_w["Al"]),
                                  (XB[p][:, cs], gw_w["Bh"]), (XB[p][:, cs], gw_w["Bl"])]
                        for m, (a, b_) in enumerate(terms_):
                            mm = pe.matmul(out_ps[:, t * EXP:(t + 1) * EXP], a, b_[:, :], start=(t == 0 and m == 0),
                                           stop=(m == 4), skip_group_check=True)
                    mm.then_inc(pe_f, 1)
                if name[:4] == "wrow":
                    i = int(name[4])
                    ts = (range(4), range(4, NT))[i]
                    pe.wait_ge(dve_t, at(DVE[T], "wfull", n))
                    for t in ts:
                        mm = pe.transpose(out_ps[0:EXP, (t - ts[0]) * 128:(t - ts[0] + 1) * 128], wfl[:, t, :], id32[:, :])
                    mm.then_inc(pe_t, 1)
                if name == "wcol":
                    pe.wait_ge(pool_t, at(POOL[T], "w_low", n))
                    for t in range(NT):
                        mm = pe.transpose(out_ps.bitcast(F16)[:, t * 128:(t + 1) * 128], wcat[:, t, :], id16[:, :])
                    mm.then_inc(pe_t, 1)

            def down(n, e, pp, part):
                pe.wait_ge(lo_done, 34 * n + 2 * e + 1 + part)
                if e == 0 and part == 0 and (known(n) is None or n > 0):
                    pe.wait_ge(fin_done, 3 * n)
                if e == NX - 1 and part == 0:
                    pe.wait_ge(act_t, at(ACTE[T], "wcol_c", n))
                opened = {0} if part else set()
                for t in ((0, 1), (2, 3, 4))[part]:
                    t0, rows = TILES[t]
                    ah, al = a_hi[(pp + e) % 2][:, t0:t0 + rows], a_lo[(pp + e) % 2][:, t0:t0 + rows]
                    terms = [(ah, dn_h[:, e, :]), (ah, dn_l[:, e, :]), (al, dn_h[:, e, :])]
                    if e == NX - 1:
                        terms += [(wT[pp][:, t0:t0 + rows], bd_h[:, :]), (wT[pp][:, t0:t0 + rows], bd_l[:, :])]
                    for lhsT, w in terms:
                        for c0, c1 in cut_at_bank(t * D, (t + 1) * D):
                            mm = pe.matmul(ysum[0:rows, c0:c1], lhsT, w[:, c0 - t * D:c1 - t * D],
                                           start=(e == 0 and c0 // 512 not in opened), stop=(e == NX - 1), skip_group_check=True)
                            opened.add(c0 // 512)
                if part == 1:
                    mm.then_inc(down_done, 1)

            DOWN_PLAN = {0: [(1, NX - 2, 1)], 1: [(1, NX - 1, 0)], 2: [(1, NX - 1, 1)], 3: [], 4: [(0, 0, 0), (0, 0, 1)]}
            DOWN_PLAN.update({s: [(0, (s - 3) // 2, 0) if s % 2 else (0, s // 2 - 2, 1)] for s in range(5, SLOTS)})

            def body(n, pp, first=False):
                for s in range(SLOTS):
                    e, b = divmod(s, 2)
                    S = 34 * n + s
                    cs = slice(b * SEQ, (b + 1) * SEQ)
                    for name, m, p in steps_of(PE_PLAN, s, n, pp):
                        step(name, m, p)
                    if s == 0:
                        pe.wait_ge(dve_f, at(DVE[F], "X_lB1", n))
                    x5 = (XAh[pp][:, cs], XAl[pp][:, cs], XAh[pp][:, cs], XB[pp][:, cs], XB[pp][:, cs])
                    if s >= 2 or not first:
                        pe.wait_ge(silu_done, S - 1)
                    chain(ups[:, s % 2, 0:SEQ], [(up_w[k][:, e, :], x) for k, x in zip(("Ah", "Ah", "Al", "Bh", "Bl"), x5)])\
                        .then_inc(up_ready, 1)
                    if s >= 2 or not first:
                        pe.wait_ge(gated, S - 1)
                    chain(gts[:, s % 2, 0:SEQ], [(gt_w[k][:, e, :], x) for k, x in zip(("Ah", "Ah", "Al", "Bh", "Bl"), x5)])\
                        .then_inc(gate_ready, 1)
                    for name, m, p in steps_of(PE_PLAN, s + 0.5, n, pp):
                        step(name, m, p)
                    for before, x, part in DOWN_PLAN[s]:
                        if not (before and first):
                            down(n - before, x, (pp + before) % 2, part)

            for st in sorted(PE_PLAN):
                for name, m, p in steps_of({k: " ".join(i for i in v.split() if i[0] == "P") for k, v in PE_PLAN.items()}, st, -2, 0):
                    step(name, m, p)
            for st in sorted(PE_PLAN):
                for name, m, p in steps_of(PE_PLAN, st, -1, 1):
                    step(name, m, p)
            body(0, 0, first=True)
            with pe.Fori(0, (PAIRS - 4) // 2) as i:
                for p in range(2):
                    body(2 * i + 1 + p, (1 + p) % 2)
            for n in range(PAIRS - 3, PAIRS):
                body(n, n % 2)
            for s in range(3):
                for _, x, part in DOWN_PLAN[s]:
                    down(PAIRS - 1, x, 1, part)


_OUTS = [((BATCH, SEQ, D), 'float32')]


def kernel(**inputs):
    import numpy as _np
    import concourse.bacc as _bacc
    from concourse import mybir as _mybir
    from concourse.bass_utils import run_bass_kernel_spmd as _run

    v = {k: _np.asarray(a) for k, a in inputs.items()}
    n = {k.replace("L0_tok_", "").replace("L0_attn_", "").replace("L0_ffn_", ""): a for k, a in v.items()}

    c = _np.array([[p[0] for p in tok] for tok in DISTINCT])
    step = _np.arange(WIN)
    r = _np.minimum(_np.array([[p[1] for p in tok] for tok in DISTINCT])[:, :, None] * STRIDE + step, IMG - 1)
    q = _np.minimum(_np.array([[p[2] for p in tok] for tok in DISTINCT])[:, :, None] * STRIDE + step, IMG - 1)
    win = n["x"][:, c[:, :, None, None], r[:, :, :, None], q[:, :, None, :]]
    pixels = win.reshape(PAIRS, 2, ND, KC, KP).transpose(0, 4, 3, 1, 2).reshape(PAIRS, KP, KC * PX)

    onehot = _np.zeros((YW, 3, PAIR), _np.float16)
    for b in range(2):
        for t in range(NPATCH):
            k, row = divmod(b * ND + WHICH[t], YW)
            onehot[row, k, b * SEQ + 1 + t] = 1

    def chan(a, parts):
        cols = [a[:DA]] * (parts - 1) + [_np.concatenate([a[DA:], a[DA:]])]
        return _np.stack(cols, 1)

    params = _np.concatenate(
        [chan(n["time_decay"], 3), chan(n["time_first"], 3), chan(n["mix_k"], 2), chan(n["mix_v"], 2), chan(n["mix_r"], 2),
         n["sbu"][:, None], n["bu"].T, n["sbg"][:, None], n["bg"].T], 1)
    arrays = {
        "pixels": pixels, "txt": n["txt"].reshape(PAIRS, 2, TXT, D), "pos": n["pos_embedding"], "cls_token": n["cls_token"][0],
        "patch_w": n["proj_w"].T.reshape(KC, KP, D).transpose(1, 0, 2),
        "wkvr": _np.stack([n["Wk"].T, n["Wv"].T, n["Wr"].T], 1), "wo": n["Wo"].T, "gate_w": n["gate_w"],
        "wu": n["Wu"], "wg": n["Wg"], "wd": n["Wd"], "swu": n["sWu"], "swg": n["sWg"], "swd": n["sWd"],
        "bd": n["bd"], "sbd": n["sbd"][None, :], "gate_b": n["gate_b"], "gate_bias": n["bias"], "params": params,
        "onehot": onehot, "ident32": _np.eye(128, dtype=_np.float32), "ident16": _np.eye(128, dtype=_np.float16),
    }
    nc = _bacc.Bacc("TRN2", target_bir_lowering=False, num_devices=1)
    feed, args = {}, {}
    for name, a in arrays.items():
        a = _np.ascontiguousarray(a)
        feed[f"in_{name}"] = a
        args[name] = nc.dram_tensor(f"in_{name}", a.shape, _mybir.dt.from_np(a.dtype), kind="ExternalInput").ap()
    args["out"] = nc.dram_tensor("out_0", _OUTS[0][0], _mybir.dt.from_np(_np.dtype(_OUTS[0][1])), kind="ExternalOutput").ap()
    build_fusion(nc, **args)
    res = _run(nc, [feed], core_ids=[0])
    return res.results[0]["out_0"]
```
